# Optimizing a Trainium2 kernel written in Bass

```python
import numpy as np
import jax
import jax.numpy as jnp

def _softmax(x, axis=-1):
    return jax.nn.softmax(x, axis=axis)

def _gelu(x):
    return jax.nn.gelu(x, approximate=True)

def _silu(x):
    return jax.nn.silu(x)

def _sigmoid(x):
    return jax.nn.sigmoid(x)

def _layernorm(x, axis=-1, eps=1e-05):
    m = jnp.mean(x, axis=axis, keepdims=True)
    v = jnp.var(x, axis=axis, keepdims=True)
    return (x - m) / jnp.sqrt(v + eps)

def _scatter_add(tgt, idx, src, axis=0):
    return tgt.at[idx].add(src)

def _segment_sum(src, seg, n):
    return jax.ops.segment_sum(src, seg, n)
kernel_name = 'mk_gps_d2_gnn_r8_9f1b54'

def setup_inputs(seed: int=0):
    np.random.seed(seed)
    _w = jnp.asarray

    def _rec_inputs():
        import jax
        import jax.numpy as jnp
        _gk = jax.random.key(seed)
        x = -0.0003713 + 1 * jax.random.normal(jax.random.fold_in(_gk, 1), (6250, 256), jnp.float32)
        _s = jax.random.randint(jax.random.fold_in(_gk, 2), (100000,), 0, 6250, jnp.int32)
        _d = jax.random.randint(jax.random.fold_in(_gk, 3), (100000,), 0, 6250, jnp.int32)
        _loop = jnp.arange(6250, dtype=jnp.int32)
        src = jnp.concatenate([_s, _d, _loop])
        dst = jnp.concatenate([_d, _s, _loop])
        _o = jnp.argsort(dst, stable=True)
        src = src[_o]
        dst = dst[_o]
        edge_type_16 = jax.random.randint(jax.random.fold_in(_gk, 12), (206250,), 0, 16, jnp.int32)
        return (x, src, dst, edge_type_16)
    x, src, dst, edge_type_16 = _rec_inputs()

    def _L0_gnn_setup():
        import jax, jax.numpy as jnp
        import numpy as np
        N = 6250
        E = 100000
        IN_C = 256
        HEADS = 8
        OUT_C = 32
        NEG_SLOPE = 0.2
        key = jax.random.key(seed)
        k1, k2, k3, k4, k5 = jax.random.split(key, 5)
        x = jax.random.normal(k1, (N, IN_C), dtype=jnp.float32)
        edge_index = jax.random.randint(k2, (2, E), 0, N, dtype=jnp.int64)
        W = jax.random.normal(k3, (IN_C, HEADS * OUT_C), dtype=jnp.float32) * (1.0 / np.sqrt(IN_C))
        attn_l = jax.random.normal(k4, (1, HEADS, OUT_C), dtype=jnp.float32) * 0.1
        attn_r = jax.random.normal(k5, (1, HEADS, OUT_C), dtype=jnp.float32) * 0.1
        bias = jnp.zeros((HEADS * OUT_C,), dtype=jnp.float32)
        return {'x': x, 'edge_index': edge_index, 'W': W, 'attn_l': attn_l, 'attn_r': attn_r, 'bias': bias}
    _L0_gnn_all = _L0_gnn_setup()
    _L0_gnn_in = {k: v for k, v in _L0_gnn_all.items() if k in ('W', 'attn_l', 'attn_r', 'bias')}
    del _L0_gnn_all

    def _L0_mix_setup():
        import jax, jax.numpy as jnp
        import numpy as np
        B, N, C, H = (8, 2048, 256, 8)
        D = C // H
        GH = C // 4
        key = jax.random.key(seed)
        ks = jax.random.split(key, 6)
        s = 0.02
        return {'x': jax.random.normal(ks[0], (B, N, C), dtype=jnp.float32), 'Wqkv': jax.random.normal(ks[1], (C, 3 * C), dtype=jnp.float32) * s, 'Wproj': jax.random.normal(ks[2], (C, C), dtype=jnp.float32) * s, 'bproj': jnp.zeros((C,), dtype=jnp.float32), 'ln_g': jnp.ones((C,), dtype=jnp.float32), 'ln_b': jnp.zeros((C,), dtype=jnp.float32), 'Wg1': jax.random.normal(ks[3], (C, GH), dtype=jnp.float32) * s, 'bg1': jnp.zeros((GH,), dtype=jnp.float32), 'Wg2': jax.random.normal(ks[4], (GH, C), dtype=jnp.float32) * s, 'bg2': jnp.zeros((C,), dtype=jnp.float32)}
    _L0_mix_all = _L0_mix_setup()
    _L0_mix_in = {k: v for k, v in _L0_mix_all.items() if k in ('Wqkv', 'Wproj', 'bproj', 'ln_g', 'ln_b', 'Wg1', 'bg1', 'Wg2', 'bg2')}
    del _L0_mix_all

    def _L0_ffn_setup():
        import jax, jax.numpy as jnp
        import numpy as np
        E = 8
        K = 2
        D = 256
        H = 512
        DOUT = 256
        EPS = 1e-05
        key = jax.random.key(seed)
        ks = jax.random.split(key, 9)
        s = 0.02
        return {'x': jax.random.normal(ks[0], (4, 1024, D), jnp.float32), 'gamma': 1.0 + 0.05 * jax.random.normal(ks[1], (D,), jnp.float32), 'beta': 0.05 * jax.random.normal(ks[2], (D,), jnp.float32), 'Wr': 0.01 * jax.random.normal(ks[3], (D, E), jnp.float32), 'br': jnp.zeros((E,), jnp.float32), 'W1': s * jax.random.normal(ks[4], (E, D, H), jnp.float32), 'b1': s * jax.random.normal(ks[5], (E, H), jnp.float32), 'W2': s * jax.random.normal(ks[6], (E, H, DOUT), jnp.float32), 'b2': s * jax.random.normal(ks[7], (E, DOUT), jnp.float32)}
    _L0_ffn_all = _L0_ffn_setup()
    _L0_ffn_in = {k: v for k, v in _L0_ffn_all.items() if k in ('gamma', 'beta', 'Wr', 'br', 'W1', 'b1', 'W2', 'b2')}
    del _L0_ffn_all

    def _L1_gnn_setup():
        import jax, jax.numpy as jnp
        import numpy as np
        N = 6250
        E = 100000
        R = 16
        IN = 256
        OUT = 256
        NB = 8
        key = jax.random.key(seed)
        ks = jax.random.split(key, 7)
        x = jax.random.normal(ks[0], (N, IN), dtype=jnp.float32)
        edge_index = jax.random.randint(ks[1], (2, E), 0, N)
        edge_type = jax.random.randint(ks[2], (E,), 0, R)
        basis = jax.random.normal(ks[3], (NB, IN, OUT), dtype=jnp.float32) / np.float32(np.sqrt(IN))
        comp = jax.random.normal(ks[4], (R, NB), dtype=jnp.float32) / np.float32(np.sqrt(NB))
        root = jax.random.normal(ks[5], (IN, OUT), dtype=jnp.float32) / np.float32(np.sqrt(IN))
        bias = jnp.zeros((OUT,), dtype=jnp.float32)
        return {'x': x, 'basis': basis, 'comp': comp, 'root': root, 'bias': bias, 'edge_index': edge_index, 'edge_type': edge_type}
    _L1_gnn_all = _L1_gnn_setup()
    _L1_gnn_in = {k: v for k, v in _L1_gnn_all.items() if k in ('basis', 'comp', 'root', 'bias')}
    del _L1_gnn_all

    def _L1_mix_setup():
        import jax, jax.numpy as jnp
        import numpy as np
        NUM_HEADS = 8
        key = jax.random.key(seed)
        ks = jax.random.split(key, 5)
        B, N, C = (8, 2048, 256)
        x = jax.random.normal(ks[0], (B, N, C), dtype=jnp.float32)
        Wq = jax.random.normal(ks[1], (C, C), dtype=jnp.float32) * 0.02
        Wkv = jax.random.normal(ks[2], (2 * C, C), dtype=jnp.float32) * 0.02
        Wproj = jax.random.normal(ks[3], (C, C), dtype=jnp.float32) * 0.02
        bproj = jnp.zeros((C,), dtype=jnp.float32)
        return {'x': x, 'Wq': Wq, 'Wkv': Wkv, 'Wproj': Wproj, 'bproj': bproj}
    _L1_mix_all = _L1_mix_setup()
    _L1_mix_in = {k: v for k, v in _L1_mix_all.items() if k in ('Wq', 'Wkv', 'Wproj', 'bproj')}
    del _L1_mix_all

    def _L1_ffn_setup():
        import jax, jax.numpy as jnp
        import numpy as np
        NUM_EXPERTS = 8
        TOP_K = 2
        B, S, D = (8, 1024, 256)

        def _moe(tokens, router_w, w1, b1, w2, b2):
            N = tokens.shape[0]
            E = router_w.shape[0]
            logits = tokens.astype(jnp.float32) @ router_w.astype(jnp.float32).T
            probs = jax.nn.softmax(logits, axis=-1)
            rw, re = jax.lax.top_k(probs, TOP_K)
            if TOP_K > 1:
                rw = rw / jnp.maximum(rw.sum(-1, keepdims=True), 1e-12)
            rw = rw.astype(tokens.dtype)
            combine = jnp.zeros((N, E), tokens.dtype).at[jnp.arange(N)[:, None], re].set(rw)
            out = tokens
            for e in range(E):
                h = jax.nn.gelu(tokens @ w1[e] + b1[e], approximate=False)
                y = h @ w2[e] + b2[e]
                out = out + combine[:, e:e + 1] * y
            return out
        key = jax.random.key(seed)
        ks = jax.random.split(key, 4)
        scale = 1.0 / np.sqrt(D).astype(np.float32)
        return {'input_embeddings': jax.random.normal(ks[0], (B, S, D), jnp.float32), 'router_w': jax.random.normal(ks[1], (NUM_EXPERTS, D), jnp.float32) * scale, 'w1': jax.random.normal(ks[2], (NUM_EXPERTS, D, D), jnp.float32) * scale, 'b1': jnp.zeros((NUM_EXPERTS, D), jnp.float32), 'w2': jax.random.normal(ks[3], (NUM_EXPERTS, D, D), jnp.float32) * scale, 'b2': jnp.zeros((NUM_EXPERTS, D), jnp.float32)}
    _L1_ffn_all = _L1_ffn_setup()
    _L1_ffn_in = {k: v for k, v in _L1_ffn_all.items() if k in ('router_w', 'w1', 'b1', 'w2', 'b2')}
    del _L1_ffn_all
    return {'x': x, 'src': src, 'dst': dst, 'edge_type_16': edge_type_16, 'L0_gnn_W': _L0_gnn_in['W'], 'L0_gnn_attn_l': _L0_gnn_in['attn_l'], 'L0_gnn_attn_r': _L0_gnn_in['attn_r'], 'L0_gnn_bias': _L0_gnn_in['bias'], 'L0_mix_Wqkv': _L0_mix_in['Wqkv'], 'L0_mix_Wproj': _L0_mix_in['Wproj'], 'L0_mix_bproj': _L0_mix_in['bproj'], 'L0_mix_ln_g': _L0_mix_in['ln_g'], 'L0_mix_ln_b': _L0_mix_in['ln_b'], 'L0_mix_Wg1': _L0_mix_in['Wg1'], 'L0_mix_bg1': _L0_mix_in['bg1'], 'L0_mix_Wg2': _L0_mix_in['Wg2'], 'L0_mix_bg2': _L0_mix_in['bg2'], 'L0_ffn_gamma': _L0_ffn_in['gamma'], 'L0_ffn_beta': _L0_ffn_in['beta'], 'L0_ffn_Wr': _L0_ffn_in['Wr'], 'L0_ffn_br': _L0_ffn_in['br'], 'L0_ffn_W1': _L0_ffn_in['W1'], 'L0_ffn_b1': _L0_ffn_in['b1'], 'L0_ffn_W2': _L0_ffn_in['W2'], 'L0_ffn_b2': _L0_ffn_in['b2'], 'L1_gnn_basis': _L1_gnn_in['basis'], 'L1_gnn_comp': _L1_gnn_in['comp'], 'L1_gnn_root': _L1_gnn_in['root'], 'L1_gnn_bias': _L1_gnn_in['bias'], 'L1_mix_Wq': _L1_mix_in['Wq'], 'L1_mix_Wkv': _L1_mix_in['Wkv'], 'L1_mix_Wproj': _L1_mix_in['Wproj'], 'L1_mix_bproj': _L1_mix_in['bproj'], 'L1_ffn_router_w': _L1_ffn_in['router_w'], 'L1_ffn_w1': _L1_ffn_in['w1'], 'L1_ffn_b1': _L1_ffn_in['b1'], 'L1_ffn_w2': _L1_ffn_in['w2'], 'L1_ffn_b2': _L1_ffn_in['b2']}

def reference(x, src, dst, edge_type_16, L0_gnn_W, L0_gnn_attn_l, L0_gnn_attn_r, L0_gnn_bias, L0_mix_Wqkv, L0_mix_Wproj, L0_mix_bproj, L0_mix_ln_g, L0_mix_ln_b, L0_mix_Wg1, L0_mix_bg1, L0_mix_Wg2, L0_mix_bg2, L0_ffn_gamma, L0_ffn_beta, L0_ffn_Wr, L0_ffn_br, L0_ffn_W1, L0_ffn_b1, L0_ffn_W2, L0_ffn_b2, L1_gnn_basis, L1_gnn_comp, L1_gnn_root, L1_gnn_bias, L1_mix_Wq, L1_mix_Wkv, L1_mix_Wproj, L1_mix_bproj, L1_ffn_router_w, L1_ffn_w1, L1_ffn_b1, L1_ffn_w2, L1_ffn_b2):
    import jax
    import jax.numpy as jnp

    def _L0_gnn_ref(x, edge_index, W, attn_l, attn_r, bias):
        import jax, jax.numpy as jnp
        import numpy as np
        N = 6250
        E = 100000
        IN_C = 256
        HEADS = 8
        OUT_C = 32
        NEG_SLOPE = 0.2
        n = x.shape[0]
        h = (x @ W).reshape(n, HEADS, OUT_C)
        a1 = jnp.sum(h * attn_l, axis=-1)
        a2 = jnp.sum(h * attn_r, axis=-1)
        src, dst = (edge_index[0], edge_index[1])
        e = a1[src] + a2[dst]
        e = jax.nn.leaky_relu(e, negative_slope=NEG_SLOPE)
        seg_max = jax.ops.segment_max(e, dst, num_segments=n)
        seg_max = jnp.where(jnp.isfinite(seg_max), seg_max, 0.0)
        ex = jnp.exp(e - seg_max[dst])
        denom = jax.ops.segment_sum(ex, dst, num_segments=n)
        alpha = ex / denom[dst]
        message = h[src] * alpha[:, :, None]
        out = jax.ops.segment_sum(message, dst, num_segments=n)
        out = out.reshape(n, HEADS * OUT_C)
        return out + bias

    def _L0_mix_ref(x, Wqkv, Wproj, bproj, ln_g, ln_b, Wg1, bg1, Wg2, bg2):
        import jax, jax.numpy as jnp
        import numpy as np
        B, N, C, H = (8, 2048, 256, 8)
        D = C // H
        GH = C // 4
        b, n, c = x.shape
        h, d = (H, D)
        qkv = (x @ Wqkv).reshape(b, n, 3, h, d)
        q, k, v = (qkv[:, :, 0], qkv[:, :, 1], qkv[:, :, 2])
        k = jax.nn.softmax(k, axis=1)
        context = jnp.einsum('bnhd,bnhv->bhdv', k, v)
        out = jnp.einsum('bnhd,bhdv->bnhv', q, context).reshape(b, n, c)
        mu = jnp.mean(x, axis=-1, keepdims=True)
        var = jnp.var(x, axis=-1, keepdims=True)
        xn = (x - mu) * jax.lax.rsqrt(var + 1e-05) * ln_g + ln_b
        hgate = jax.nn.gelu(xn @ Wg1 + bg1, approximate=False)
        gate = jax.nn.sigmoid(hgate @ Wg2 + bg2)
        return out * gate @ Wproj + bproj

    def _L0_ffn_ref(x, gamma, beta, Wr, br, W1, b1, W2, b2):
        import jax, jax.numpy as jnp
        import numpy as np
        E = 8
        K = 2
        D = 256
        H = 512
        DOUT = 256
        EPS = 1e-05
        mu = jnp.mean(x, axis=-1, keepdims=True)
        var = jnp.mean(jnp.square(x - mu), axis=-1, keepdims=True)
        xn = (x - mu) * jax.lax.rsqrt(var + EPS) * gamma + beta
        logits = jnp.einsum('bsd,de->bse', xn, Wr) + br
        top_vals, top_idx = jax.lax.top_k(logits, K)
        w = jax.nn.softmax(top_vals, axis=-1)
        w_full = jnp.einsum('bsk,bske->bse', w, jax.nn.one_hot(top_idx, E, dtype=w.dtype))
        y = jnp.zeros(x.shape[:-1] + (DOUT,), x.dtype)
        for e in range(E):
            h = jax.nn.gelu(jnp.einsum('bsd,dh->bsh', xn, W1[e]) + b1[e], approximate=False)
            y_e = jnp.einsum('bsh,hd->bsd', h, W2[e]) + b2[e]
            y = y + y_e * w_full[..., e, None]
        return y

    def _L1_gnn_ref(x, basis, comp, root, bias, edge_index, edge_type):
        import jax, jax.numpy as jnp
        import numpy as np
        N = 6250
        E = 100000
        R = 16
        IN = 256
        OUT = 256
        NB = 8
        n = x.shape[0]
        r = comp.shape[0]
        src, dst = (edge_index[0], edge_index[1])
        seg = dst * r + edge_type
        cnt = jax.ops.segment_sum(jnp.ones(seg.shape, x.dtype), seg, num_segments=n * r)
        agg = jax.ops.segment_sum(x[src], seg, num_segments=n * r)
        agg = (agg / jnp.maximum(cnt, 1.0)[:, None]).reshape(n, r, x.shape[1])
        weight = jnp.einsum('rb,bio->rio', comp, basis)
        out = jnp.einsum('nri,rio->no', agg, weight) + x @ root + bias
        return out

    def _L1_mix_ref(x, Wq, Wkv, Wproj, bproj):
        import jax, jax.numpy as jnp
        import numpy as np
        NUM_HEADS = 8
        B, N, C = x.shape
        h = NUM_HEADS
        d = C // h
        q = jnp.einsum('bnc,oc->bno', x, Wq).reshape(B, N, h, d).transpose(0, 2, 1, 3)
        kv = jnp.einsum('bnc,oc->bno', x, Wkv).reshape(B, N, 2, h, d)
        k = kv[:, :, 0].transpose(0, 2, 1, 3)
        v = kv[:, :, 1].transpose(0, 2, 1, 3)
        q = jax.nn.elu(q) + 1.0
        k = jax.nn.elu(k) + 1.0
        k_sum = k.sum(axis=2)
        D_inv = 1.0 / jnp.maximum(jnp.einsum('bhnd,bhd->bhn', q, k_sum), 1e-06)
        context = jnp.einsum('bhnd,bhne->bhde', k, v)
        attn = jnp.einsum('bhnd,bhde->bhne', q, context) * D_inv[..., None]
        out = attn.transpose(0, 2, 1, 3).reshape(B, N, C)
        out = jnp.einsum('bnc,oc->bno', out, Wproj) + bproj
        return out

    def _L1_ffn_ref(input_embeddings, router_w, w1, b1, w2, b2):
        import jax, jax.numpy as jnp
        import numpy as np
        NUM_EXPERTS = 8
        TOP_K = 2
        B, S, D = (8, 1024, 256)

        def _moe(tokens, router_w, w1, b1, w2, b2):
            N = tokens.shape[0]
            E = router_w.shape[0]
            logits = tokens.astype(jnp.float32) @ router_w.astype(jnp.float32).T
            probs = jax.nn.softmax(logits, axis=-1)
            rw, re = jax.lax.top_k(probs, TOP_K)
            if TOP_K > 1:
                rw = rw / jnp.maximum(rw.sum(-1, keepdims=True), 1e-12)
            rw = rw.astype(tokens.dtype)
            combine = jnp.zeros((N, E), tokens.dtype).at[jnp.arange(N)[:, None], re].set(rw)
            out = tokens
            for e in range(E):
                h = jax.nn.gelu(tokens @ w1[e] + b1[e], approximate=False)
                y = h @ w2[e] + b2[e]
                out = out + combine[:, e:e + 1] * y
            return out
        b, s, d = input_embeddings.shape
        tokens = input_embeddings.reshape(b * s, d)
        return _moe(tokens, router_w, w1, b1, w2, b2).reshape(b, s, d)
    edge_index = jnp.stack([src, dst])
    xn = _layernorm(x, axis=-1)
    x = x + _L0_gnn_ref(xn, edge_index, L0_gnn_W, L0_gnn_attn_l, L0_gnn_attn_r, L0_gnn_bias) + _L0_mix_ref(xn[None], L0_mix_Wqkv, L0_mix_Wproj, L0_mix_bproj, L0_mix_ln_g, L0_mix_ln_b, L0_mix_Wg1, L0_mix_bg1, L0_mix_Wg2, L0_mix_bg2)[0]
    x = x + _L0_ffn_ref(_layernorm(x, axis=-1)[None], L0_ffn_gamma, L0_ffn_beta, L0_ffn_Wr, L0_ffn_br, L0_ffn_W1, L0_ffn_b1, L0_ffn_W2, L0_ffn_b2)[0]
    xn = _layernorm(x, axis=-1)
    x = x + _L1_gnn_ref(xn, L1_gnn_basis, L1_gnn_comp, L1_gnn_root, L1_gnn_bias, edge_index, edge_type_16) + _L1_mix_ref(xn[None], L1_mix_Wq, L1_mix_Wkv, L1_mix_Wproj, L1_mix_bproj)[0]
    x = x + _L1_ffn_ref(_layernorm(x, axis=-1)[None], L1_ffn_router_w, L1_ffn_w1, L1_ffn_b1, L1_ffn_w2, L1_ffn_b2)[0]
    return x

_drawn_inputs = setup_inputs


def setup_inputs(seed=0):
    import zlib

    import numpy as np

    out = dict(_drawn_inputs(seed))
    spreads = {'L0_gnn_bias': (0.0, 0.8),
     'L0_mix_bproj': (0.0, 0.8),
     'L0_mix_ln_g': (1.0, 0.6),
     'L0_mix_ln_b': (0.0, 0.8),
     'L0_mix_bg1': (0.0, 0.8),
     'L0_mix_bg2': (0.0, 0.8),
     'L0_ffn_br': (0.0, 0.695),
     'L1_gnn_bias': (0.0, 0.8),
     'L1_mix_bproj': (0.0, 0.8),
     'L1_ffn_b1': (0.0, 2.0),
     'L1_ffn_b2': (0.0, 1.593)}
    factors = {'L0_mix_Wqkv': 8.0,
     'L0_mix_Wproj': 8.0,
     'L0_mix_Wg1': 8.0,
     'L0_mix_Wg2': 8.0,
     'L0_ffn_gamma': 38.928,
     'L0_ffn_beta': 32.712,
     'L0_ffn_b1': 64.0,
     'L0_ffn_b2': 30.096,
     'L1_mix_Wq': 45.949,
     'L1_mix_Wkv': 23.558,
     'L1_mix_Wproj': 24.2,
     'L0_gnn_W': 3.752,
     'L0_gnn_attn_l': 7.218,
     'L0_gnn_attn_r': 8.0}
    for name, (base, spread) in spreads.items():
        noise = np.random.default_rng([zlib.crc32(name.encode()), seed]).standard_normal(out[name].shape)
        drawn = base * np.exp(spread * noise) if base else spread * noise
        out[name] = jnp.asarray(drawn.astype(out[name].dtype))
    for name, factor in factors.items():
        out[name] = (out[name] * factor).astype(out[name].dtype)
    return out
```

```python
from contextlib import ExitStack

import concourse.bass as bass
from concourse import mybir

P = 128
G = 8
R = 4
GE = G * P
C = 256
KC = C // P
HEADS = 8
D = C // HEADS
HD = D + 1
REL = 16
NE = 8
HROW = HEADS * HD + HEADS
MROW = HEADS * HD + REL
SLOPE = 0.2
BIG = 1e30

ALU = mybir.AluOpType
ACT = mybir.ActivationFunctionType
AX = mybir.AxisListType
F32 = mybir.dt.float32
I32 = mybir.dt.int32
BF16 = mybir.dt.bfloat16
ds = bass.ds


def two_at_a_time(eng, n, body, peel=False):
    whole = (n - 1) // 2
    start = 0
    if peel and whole:
        body(0, 0, 0, False)
        body(1, 1, 0, False)
        start = 1
    if whole > start:
        with eng.Fori(start, whole) as k:
            body(k * 2, 0, k, False)
            body(k * 2 + 1, 1, k, False)
    for b in range(2 * whole, n):
        body(b, b % 2, b // 2, b == n - 1)


class Sizes:
    def __init__(self, n, e):
        self.N = n
        self.NB = -(-n // P)
        self.TAIL = n - (self.NB - 1) * P
        self.NG = -(-e // GE)
        self.NGT = R * -(-(self.NG + 1) // R)
        self.COLS = self.NGT * G


def normalise_stats(nc, name, src, mean, rstd, eps, NB):
    with ExitStack() as c:
        six = c.enter_context(nc.sbuf_tensor(name + "_six", [P, NB, 6], F32))
        tmp = c.enter_context(nc.sbuf_tensor(name + "_tmp", [P, 3, NB], F32))
        var_ready = c.enter_context(nc.semaphore(name + "_var_ready"))
        root_ready = c.enter_context(nc.semaphore(name + "_root_ready"))
        flat = six[:].rearrange("p b s -> p (b s)")
        with nc.Block() as block:
            @block.vector
            def _(v):
                with v.Fori(0, NB) as b:
                    v.bn_stats(flat[:, ds(b * 6, 6)], src[:, ds(b * C, C)])
                v.drain()
                v.tensor_tensor(tmp[:, 0, :], six[:, :, 1], six[:, :, 4], ALU.add)
                v.tensor_tensor(tmp[:, 1, :], six[:, :, 1], six[:, :, 4], ALU.subtract)
                v.tensor_tensor(tmp[:, 2, :], six[:, :, 2], six[:, :, 5], ALU.add)
                v.drain()
                v.tensor_scalar(mean[:, :], tmp[:, 0, :], 0.5, None, ALU.mult)
                v.tensor_tensor(tmp[:, 1, :], tmp[:, 1, :], tmp[:, 1, :], ALU.mult)
                v.tensor_scalar(tmp[:, 2, :], tmp[:, 2, :], 1.0 / C, eps, ALU.mult, ALU.add)
                v.drain()
                v.scalar_tensor_tensor(tmp[:, 0, :], tmp[:, 1, :], 0.25, tmp[:, 2, :], ALU.mult,
                                       ALU.add).then_inc(var_ready, 1)
                v.wait_ge(root_ready, 1)
                v.reciprocal(rstd[:, :], tmp[:, 1, :])

            @block.scalar
            def _(act):
                act.wait_ge(var_ready, 1)
                act.activation(tmp[:, 1, :], tmp[:, 0, :], ACT.Sqrt).then_inc(root_ready, 1)


def normalise_rows(nc, dst, src, mean, rstd, NB):
    with nc.Block() as block:
        @block.vector
        def _(v):
            with v.Fori(0, NB) as b:
                v.tensor_scalar(dst[:, ds(b * C, C)], src[:, ds(b * C, C)], mean[:, ds(b, 1)],
                                rstd[:, ds(b, 1)], ALU.subtract, ALU.mult)


def setup(nc, z, S, k):
    NB, NG = z.NB, z.NG
    with ExitStack() as c:
        sem = lambda n: c.enter_context(nc.semaphore("su_" + n))
        sb = lambda n, s, d=F32: c.enter_context(nc.sbuf_tensor("su_" + n, s, d))
        ints = sb("ints", [P, z.COLS], I32)
        others = sb("others", [P, 2, z.COLS], I32)
        othersf = sb("othersf", [P, 2, z.COLS])
        etypes = sb("etypes", [P, z.COLS], I32)
        bounds = sb("bounds", [NB + 1, NG - 1], I32)
        boundsf = sb("boundsf", [NB + 1, NG - 1])
        below = sb("below", [NB + 1, NG - 1])
        limit = sb("limit", [NB + 1, 1])
        counts = sb("counts", [NB + 1, 1])
        counti = sb("counti", [NB + 1, 1], I32)
        nch = -(-NG // P)
        firsts = sb("firsts", [P, NB - 1], I32)
        firstsf = sb("firstsf", [P, NB - 1])
        gid = sb("gid", [P, nch])
        hit = sb("hit", [P, nch, NB - 1])
        last_pair = sb("last_pair", [P, nch])
        last_pairi = sb("last_pairi", [P, nch], I32)
        iotas = sb("iotas", [P, P], I32)
        loaded, made, cvt, tab, tab2, ended = (sem(x) for x in
            ("loaded", "made", "cvt", "tab", "tab2", "ended"))
        with nc.Block() as block:
            @block.sync
            def _(sp):
                sp.dma_start(ints[:], S["dst"]).then_inc(loaded, 16)
                sp.dma_start(others[:, 0, :], S["dst_prev"]).then_inc(loaded, 16)
                sp.dma_start(others[:, 1, :], S["dst_next"]).then_inc(loaded, 16)
                sp.dma_start(etypes[:], S["etype"]).then_inc(loaded, 16)
                sp.dma_start(bounds[:], S["bounds"].partition_broadcast(NB + 1)).then_inc(loaded, 16)
                sp.dma_start(k.xb[:].rearrange("p (b f) -> p b f", f=C),
                             S["x"].rearrange("(b p) f -> p b f", p=P)).then_inc(loaded, 16)
                sp.dma_start(k.src[:], S["src"]).then_inc(loaded, 16)
                sp.wait_ge(loaded, 112)
                sp.wait_ge(cvt, 1)
                sp.dma_start(k.first_dram, counti[:]).then_inc(tab, 16)
                sp.wait_ge(tab, 16)
                row = k.first_dram.rearrange("n o -> o n")
                sp.dma_start(k.first_group[:], row).then_inc(tab, 16)
                sp.dma_start(firsts[:], row[0, 1:NB].partition_broadcast(P)).then_inc(tab, 16)
                sp.wait_ge(tab, 48)
                sp.wait_ge(ended, 1)
                for i in range(nch):
                    sp.dma_start(k.last_dram[i * P:(i + 1) * P, :],
                                 last_pairi[:, i:i + 1]).then_inc(tab2, 16)
                sp.wait_ge(tab2, 16 * nch)
                sp.dma_start(k.last_pair[:], k.last_dram.rearrange("n o -> o n")).then_inc(tab2, 16)
                sp.wait_ge(tab2, 16 * (nch + 1))

            @block.gpsimd
            def _(p):
                p.memset(k.ident[:], 0.0).then_inc(made, 1)
                p.wait_ge(made, 1)
                p.affine_select(out=k.ident[:], in_=k.ident[:], compare_op=ALU.not_equal, fill=1.0,
                                base=0, pattern=[[-1, P]], channel_multiplier=1).then_inc(made, 1)
                p.memset(k.ones[:], 1.0)
                p.iota(iotas[:], [[1, P]], base=0, channel_multiplier=0).then_inc(made, 1)
                p.iota(limit[:], [[0, 1]], base=0, channel_multiplier=P,
                       allow_small_or_imprecise_dtypes=True)
                p.iota(gid[:], [[P, nch]], base=0, channel_multiplier=1,
                       allow_small_or_imprecise_dtypes=True)
                p.iota(k.mask[:], [[0, 1]], base=0, channel_multiplier=1,
                       allow_small_or_imprecise_dtypes=True).then_inc(made, 1)

            @block.vector
            def _(v):
                v.wait_ge(made, 4)
                v.wait_ge(loaded, 112)
                v.tensor_copy(k.iota[:], iotas[:])
                v.tensor_copy(boundsf[:], bounds[:])
                v.tensor_copy(k.dstf[:], ints[:])
                v.tensor_copy(k.etf[:], etypes[:])
                v.scalar_tensor_tensor(k.src_rel[:], k.src[:], float(REL), etypes[:], ALU.mult, ALU.add)
                v.tensor_copy(othersf[:], others[:])
                v.tensor_scalar(k.mask[:], k.mask[:], float(z.TAIL), None, ALU.is_lt)
                v.drain()
                v.tensor_scalar(below[:], boundsf[:], limit[:, 0:1], None, ALU.is_lt)
                v.drain()
                v.tensor_reduce(counts[:], below[:], AX.X, ALU.add)
                v.drain()
                v.tensor_copy(counti[:], counts[:]).then_inc(cvt, 1)
                v.tensor_tensor(k.start[:], k.dstf[:], othersf[:, 0, :], ALU.not_equal)
                v.tensor_tensor(k.last[:], k.dstf[:], othersf[:, 1, :], ALU.not_equal)
                v.drain()
                v.tensor_scalar(k.start[:], k.start[:], -BIG, None, ALU.mult)
                v.wait_ge(tab, 48)
                v.tensor_copy(firstsf[:], firsts[:])
                v.drain()
                for i in range(nch):
                    v.tensor_scalar(hit[:, i, :], firstsf[:], gid[:, i:i + 1], None, ALU.is_le)
                v.drain()
                v.tensor_reduce(last_pair[:], hit[:], AX.X, ALU.add)
                v.drain()
                v.scalar_tensor_tensor(last_pair[:], last_pair[:], 1.0, gid[:], ALU.add, ALU.add)
                v.drain()
                v.tensor_copy(last_pairi[:], last_pair[:]).then_inc(ended, 1)


def load_weights(nc, name, pairs):
    with ExitStack() as c:
        got = c.enter_context(nc.semaphore(name))
        with nc.Block() as block:
            @block.sync
            def _(sp):
                for dst, src in pairs:
                    sp.dma_start(dst, src).then_inc(got, 16)
                sp.wait_ge(got, 16 * len(pairs))


def rows_of(w):
    return w.rearrange("(k p) n -> p k n", p=P)


def attention_table(nc, z, k, S, kt):
    NB = z.NB
    A2 = 2 * HEADS
    with ExitStack() as c:
        sem = lambda n: c.enter_context(nc.semaphore("at_" + n))
        sb = lambda n, s, d=F32: c.enter_context(nc.sbuf_tensor("at_" + n, s, d))
        w = sb("w", [P, KC, C])
        wt = sb("wt", [P, KC, C])
        attn = sb("attn", [P, 2, KC])
        lr = sb("lr", [P, KC, A2])
        waug = sb("waug", [P, KC, C + A2])
        wk = sb("wk", [P, KC, C])
        st = sb("st", [P, 2, C])
        xt = sb("xt", [P, 2, C])
        row = sb("row", [P, 2, HROW])
        psT = c.enter_context(nc.psum_tensor("at_psT", [P, 2, 512], F32))
        psH = c.enter_context(nc.psum_tensor("at_psH", [P, 2, 512], F32))
        psK = c.enter_context(nc.psum_tensor("at_psK", [P, 2, 512], F32))
        load_weights(nc, "at_load", [
            (w[:], rows_of(S["L0_gnn_W"])), (wt[:], rows_of(S["L0_gnn_W_t"])),
            (attn[:, 0, :], S["L0_gnn_attn_l"]),
            (attn[:, 1, :], S["L0_gnn_attn_r"]),
            (wk[:], rows_of(S["L0_mix_Wqkv"])[:, :, C:2 * C])])
        spread, folded = sem("spread"), sem("folded")
        with nc.Block() as block:
            @block.vector
            def _(v):
                v.memset(lr[:], 0.0)
                v.memset(row[:], 1.0)
                v.drain()
                for kc in range(KC):
                    for q in range(P // D):
                        h = kc * (P // D) + q
                        for s in range(2):
                            v.tensor_copy(lr[q * D:(q + 1) * D, kc, s * HEADS + h:s * HEADS + h + 1],
                                          attn[q * D:(q + 1) * D, s, kc:kc + 1])
                v.drain()
                v.tensor_copy(waug[:, :, 0:C], w[:]).then_inc(spread, 1)
                v.wait_ge(folded, 1)
                v.tensor_copy(waug[:, :, C:C + A2], psH[:, :, 0:A2])

            @block.tensor
            def _(pe):
                pe.wait_ge(spread, 1)
                for m in range(KC):
                    for kc in range(KC):
                        mm = pe.matmul(psH[:, m, 0:A2], wt[:, kc, m * P:(m + 1) * P], lr[:, kc, :],
                                       start=kc == 0, stop=kc == KC - 1)
                mm.then_inc(folded, 1)
        staged, turned, back, made, taken, keys = (sem(x) for x in
            ("staged", "turned", "back", "made", "taken", "keys"))
        stored = [sem("stored0"), sem("stored1")]
        with nc.Block() as block:
            @block.scalar
            def _(act):
                act.sem_inc(staged, 2)
                act.sem_inc(keys, 2)

                def body(b, u, i, last):
                    act.wait_ge(turned, b + 1)
                    act.nop()
                    act.copy(st[:, u, :], k.xa[:, ds(b * C, C)]).then_inc(staged, 1)
                    act.wait_ge(made, b + 3)
                    act.nop()
                    for kc in range(KC):
                        o = act.copy(kt[:, ds(b * P + kc * NB * P, P)], psK[:, u, kc * P:(kc + 1) * P])
                    o.then_inc(keys, 1)
                two_at_a_time(act, NB, body)

            @block.tensor
            def _(pe):
                pe.sem_inc(turned, 2)
                pe.sem_inc(made, 2)

                def body(b, u, i, last):
                    pe.wait_ge(staged, b + 3)
                    pe.wait_ge(back, b + 1)
                    for kc in range(KC):
                        t = pe.transpose(psT[:, u, kc * P:(kc + 1) * P], st[:, u, kc * P:(kc + 1) * P],
                                         k.ident[:])
                    t.then_inc(turned, 1)
                    pe.wait_ge(back, b + 3)
                    pe.wait_ge(taken, b + 1)
                    pe.wait_ge(keys, b + 1)
                    for kc in range(KC):
                        pe.matmul(psH[:, u, 0:C + A2], xt[:, u, kc * P:(kc + 1) * P], waug[:, kc, :],
                                  start=kc == 0, stop=kc == KC - 1)
                    for m in range(KC):
                        for kc in range(KC):
                            t = pe.matmul(psK[:, u, m * P:(m + 1) * P], wk[:, kc, m * P:(m + 1) * P],
                                          xt[:, u, kc * P:(kc + 1) * P], start=kc == 0, stop=kc == KC - 1)
                    t.then_inc(made, 1)
                two_at_a_time(pe, NB, body)

            @block.vector
            def _(v):
                v.sem_inc(back, 2)
                v.sem_inc(taken, 2)

                def body(b, u, i, last):
                    v.wait_ge(turned, b + 3)
                    v.wait_ge(made, b + 1)
                    v.tensor_copy(xt[:, u, :], psT[:, u, 0:C]).then_inc(back, 1)
                    if not (isinstance(i, int) and i == 0):
                        v.wait_ge(stored[u], i * 16)
                    v.wait_ge(made, b + 3)
                    v.tensor_copy(row[:, u, 0:HEADS * HD].rearrange("p (h d) -> p h d", d=HD)[:, :, 0:D],
                                  psH[:, u, 0:C].rearrange("p (h d) -> p h d", d=D))
                    v.tensor_copy(k.a2[:, ds(b * HEADS, HEADS)], psH[:, u, C + HEADS:C + A2])
                    v.tensor_copy(row[:, u, HEADS * HD:HROW], psH[:, u, C:C + HEADS]).then_inc(taken, 1)
                two_at_a_time(v, NB, body, peel=True)

            @block.sync
            def _(sp):
                def body(b, u, i, last):
                    sp.wait_ge(taken, b + 3)
                    sp.dma_start(k.h_dram[ds(b * P, P), :], row[:, u, :]).then_inc(stored[u], 16)
                two_at_a_time(sp, NB, body)
                sp.wait_ge(stored[0], 16 * ((NB + 1) // 2))
                sp.wait_ge(stored[1], 16 * (NB // 2))


def keys_to_context(nc, z, k, S, kt, wqc):
    NB, N = z.NB, z.N
    NP = NB * P
    with ExitStack() as c:
        sem = lambda n: c.enter_context(nc.semaphore("kc_" + n))
        sb = lambda n, s, d=F32: c.enter_context(nc.sbuf_tensor("kc_" + n, s, d))
        wqt = sb("wqt", [P, KC, C])
        wv = sb("wv", [P, KC, C])
        top = sb("top", [P, KC])
        total = sb("total", [P, KC])
        st = sb("st", [P, 2, C])
        ek = sb("ek", [P, 2, C])
        zero = sb("zero", [P, C])
        cs = sb("cs", [P, KC, C])
        ct = sb("ct", [P, KC, C])
        cbd = sb("cbd", [P, KC, C])
        psT = c.enter_context(nc.psum_tensor("kc_psT", [P, 2, 512], F32))
        psC = c.enter_context(nc.psum_tensor("kc_psC", [P, 2, 512], F32))
        load_weights(nc, "kc_load", [(wqt[:], rows_of(S["L0_mix_Wq_t"])),
                                     (wv[:], rows_of(S["L0_mix_Wqkv"])[:, :, 2 * C:3 * C])])
        topped, powered = sem("topped"), sem("powered")
        with nc.Block() as block:
            @block.vector
            def _(v):
                v.memset(zero[:], 0.0)
                v.memset(cbd[:], 0.0)
                for kc in range(KC):
                    v.tensor_reduce(top[:, kc:kc + 1], kt[:, kc * NP:kc * NP + N], AX.X, ALU.max)
                v.drain()
                v.tensor_scalar(top[:], top[:], -1.0, None, ALU.mult).then_inc(topped, 1)
                if NP > N:
                    for kc in range(KC):
                        v.memset(kt[:, kc * NP + N:(kc + 1) * NP], 0.0)
                v.wait_ge(powered, 1)
                v.reciprocal(total[:], total[:])

            @block.scalar
            def _(act):
                act.wait_ge(topped, 1)
                for kc in range(KC):
                    o = act.activation(kt[:, kc * NP:kc * NP + N], kt[:, kc * NP:kc * NP + N], ACT.Exp,
                                       bias=top[:, kc:kc + 1], accum_out=total[:, kc:kc + 1])
                o.then_inc(powered, 1)
        staged, turned, back, summed = (sem(x) for x in ("staged", "turned", "back", "summed"))
        with nc.Block() as block:
            @block.scalar
            def _(act):
                act.sem_inc(staged, 2)

                def body(b, u, i, last):
                    act.wait_ge(turned, b + 1)
                    act.nop()
                    for kc in range(KC):
                        o = act.copy(st[:, u, kc * P:(kc + 1) * P], kt[:, ds(b * P + kc * NP, P)])
                    o.then_inc(staged, 1)
                two_at_a_time(act, NB, body)

            @block.tensor
            def _(pe):
                pe.sem_inc(turned, 2)
                pe.sem_inc(summed, 2)
                for kc in range(KC):
                    pe.matmul(psC[:, kc, 0:C], zero[:, 0:P], zero[:], start=True, stop=False)

                def body(b, u, i, last):
                    pe.wait_ge(staged, b + 3)
                    pe.wait_ge(back, b + 1)
                    for kc in range(KC):
                        t = pe.transpose(psT[:, u, kc * P:(kc + 1) * P], st[:, u, kc * P:(kc + 1) * P],
                                         k.ident[:])
                    t.then_inc(turned, 1)
                    pe.wait_ge(back, b + 3)
                    for kc in range(KC):
                        t = pe.matmul(psC[:, kc, 0:C], ek[:, u, kc * P:(kc + 1) * P],
                                      k.xa[:, ds(b * C, C)], start=False, stop=last)
                    t.then_inc(summed, 1)
                two_at_a_time(pe, NB, body)

            @block.vector
            def _(v):
                v.sem_inc(back, 2)

                def body(b, u, i, last):
                    v.wait_ge(turned, b + 3)
                    v.wait_ge(summed, b + 1)
                    v.tensor_copy(ek[:, u, :], psT[:, u, 0:C]).then_inc(back, 1)
                two_at_a_time(v, NB, body)
        step, done = sem("step"), sem("done")
        with nc.Block() as block:
            @block.vector
            def _(v):
                for kc in range(KC):
                    o = v.tensor_scalar(cs[:, kc, :], psC[:, kc, 0:C], total[:, kc:kc + 1], None, ALU.mult)
                o.then_inc(step, 1)
                v.wait_ge(done, 1)
                v.tensor_copy(ct[:], psT[:, :, 0:C]).then_inc(step, 1)
                v.wait_ge(done, 2)
                for kc in range(KC):
                    for q in range(P // D):
                        a = kc * P + q * D
                        o = v.tensor_copy(cbd[q * D:(q + 1) * D, kc, a:a + D],
                                          psC[q * D:(q + 1) * D, kc, a:a + D])
                o.then_inc(step, 1)
                v.wait_ge(done, 3)
                v.tensor_copy(wqc[:], psT[:, :, 0:C])

            @block.tensor
            def _(pe):
                pe.wait_ge(step, 1)
                for m in range(KC):
                    for kc in range(KC):
                        t = pe.transpose(psT[:, m, kc * P:(kc + 1) * P], cs[:, kc, m * P:(m + 1) * P],
                                         k.ident[:])
                t.then_inc(done, 1)
                pe.wait_ge(step, 2)
                for m in range(KC):
                    for kc in range(KC):
                        t = pe.matmul(psC[:, m, 0:C], ct[:, kc, m * P:(m + 1) * P], wv[:, kc, :],
                                      start=kc == 0, stop=kc == KC - 1)
                t.then_inc(done, 1)
                pe.wait_ge(step, 3)
                for m in range(KC):
                    for kc in range(KC):
                        t = pe.matmul(psT[:, m, 0:C], wqt[:, kc, m * P:(m + 1) * P], cbd[:, kc, :],
                                      start=kc == 0, stop=kc == KC - 1)
                t.then_inc(done, 1)


def mix_out(nc, z, k, S, wqc, mean, rstd):
    NB = z.NB
    GH = S["L0_mix_Wg1"].shape[1]
    with ExitStack() as c:
        sem = lambda n: c.enter_context(nc.semaphore("mo_" + n))
        sb = lambda n, s, d=F32: c.enter_context(nc.sbuf_tensor("mo_" + n, s, d))
        g1 = sb("g1", [P, KC, GH])
        g2 = sb("g2", [GH, C])
        wp = sb("wp", [P, KC, C])
        cols = sb("cols", [P, 3, KC])
        bg1 = sb("bg1", [GH, 1])
        bias = sb("bias", [1, 2, C])
        st = sb("st", [P, 2, 2 * C])
        xt = sb("xt", [P, 2, 2 * C])
        hid = sb("hid", [GH, 2, P])
        gate = sb("gate", [P, 2, C])
        prod = sb("prod", [P, 2, C])
        psT = c.enter_context(nc.psum_tensor("mo_psT", [P, 2, 512], F32))
        psG = c.enter_context(nc.psum_tensor("mo_psG", [GH, 2, 512], F32))
        psU = c.enter_context(nc.psum_tensor("mo_psU", [P, 2, 512], F32))
        psM = c.enter_context(nc.psum_tensor("mo_psM", [P, 2, 512], F32))
        load_weights(nc, "mo_load", [
            (g1[:], rows_of(S["L0_mix_Wg1"])), (g2[:], S["L0_mix_Wg2"]), (wp[:], rows_of(S["L0_mix_Wproj"])),
            (cols[:, 0, :], S["L0_mix_ln_g"]), (cols[:, 1, :], S["L0_mix_ln_b"]),
            (cols[:, 2, :], S["L0_mix_bg2"]),
            (bg1[:], S["L0_mix_bg1"].rearrange("(p o) -> p o", o=1)),
            (bias[:, 0, :], S["L0_mix_bproj"].rearrange("(o n) -> o n", o=1)),
            (bias[:, 1, :], S["L0_gnn_bias"].rearrange("(o n) -> o n", o=1))])
        staged, normed, turned, back, hidden, gelu, gated, sig, timed, projected, added = (
            sem(x) for x in ("staged", "normed", "turned", "back", "hidden", "gelu", "gated", "sig",
                             "timed", "projected", "added"))
        with nc.Block() as block:
            @block.scalar
            def _(act):
                for s in (staged, back, gelu, sig):
                    act.sem_inc(s, 2)

                def body(b, u, i, last):
                    act.wait_ge(turned, b + 1)
                    act.nop()
                    act.copy(st[:, u, 0:C], k.xa[:, ds(b * C, C)]).then_inc(staged, 1)
                    act.wait_ge(turned, b + 3)
                    act.wait_ge(gated, b + 1)
                    act.nop()
                    act.copy(xt[:, u, 0:C], psT[:, u, 0:C])
                    for kc in range(KC):
                        o = act.activation(xt[:, u, C + kc * P:C + (kc + 1) * P],
                                           psT[:, u, C + kc * P:C + (kc + 1) * P], ACT.Identity,
                                           bias=cols[:, 1, kc:kc + 1], scale=cols[:, 0, kc:kc + 1])
                    o.then_inc(back, 1)
                    act.wait_ge(hidden, b + 3)
                    act.nop()
                    act.activation(hid[:, u, :], psG[:, u, 0:P], ACT.Gelu, bias=bg1[:, 0:1]).then_inc(gelu, 1)
                    act.wait_ge(gated, b + 3)
                    act.wait_ge(timed, b + 1)
                    act.nop()
                    for kc in range(KC):
                        o = act.activation(gate[:, u, kc * P:(kc + 1) * P],
                                           psU[:, u, C + kc * P:C + (kc + 1) * P], ACT.Sigmoid,
                                           bias=cols[:, 2, kc:kc + 1])
                    o.then_inc(sig, 1)
                two_at_a_time(act, NB, body)

            @block.vector
            def _(v):
                for s in (normed, timed, added):
                    v.sem_inc(s, 2)

                def body(b, u, i, last):
                    v.wait_ge(turned, b + 1)
                    v.tensor_scalar(st[:, u, C:2 * C], k.xa[:, ds(b * C, C)], mean[:, ds(b, 1)],
                                    rstd[:, ds(b, 1)], ALU.subtract, ALU.mult).then_inc(normed, 1)
                    v.wait_ge(sig, b + 3)
                    v.wait_ge(projected, b + 1)
                    v.tensor_tensor(prod[:, u, :], psU[:, u, 0:C], gate[:, u, :], ALU.mult).then_inc(timed, 1)
                    v.wait_ge(projected, b + 3)
                    v.tensor_tensor(k.xb[:, ds(b * C, C)], k.xb[:, ds(b * C, C)], psM[:, u, 0:C],
                                    ALU.add).then_inc(added, 1)
                two_at_a_time(v, NB, body)

            @block.tensor
            def _(pe):
                for s in (turned, hidden, gated, projected):
                    pe.sem_inc(s, 2)

                def body(b, u, i, last):
                    pe.wait_ge(staged, b + 3)
                    pe.wait_ge(normed, b + 3)
                    pe.wait_ge(back, b + 1)
                    for q in range(2 * KC):
                        t = pe.transpose(psT[:, u, q * P:(q + 1) * P], st[:, u, q * P:(q + 1) * P], k.ident[:])
                    t.then_inc(turned, 1)
                    pe.wait_ge(back, b + 3)
                    pe.wait_ge(gelu, b + 1)
                    for kc in range(KC):
                        t = pe.matmul(psG[:, u, 0:P], g1[:, kc, :], xt[:, u, C + kc * P:C + (kc + 1) * P],
                                      start=kc == 0, stop=kc == KC - 1)
                    t.then_inc(hidden, 1)
                    pe.wait_ge(timed, b + 1)
                    for m in range(KC):
                        for kc in range(KC):
                            pe.matmul(psU[:, u, m * P:(m + 1) * P], wqc[:, kc, m * P:(m + 1) * P],
                                      xt[:, u, kc * P:(kc + 1) * P], start=kc == 0, stop=kc == KC - 1)
                    pe.wait_ge(gelu, b + 3)
                    for m in range(KC):
                        t = pe.matmul(psU[:, u, C + m * P:C + (m + 1) * P], g2[:, m * P:(m + 1) * P],
                                      hid[:, u, :], start=True, stop=True)
                    t.then_inc(gated, 1)
                    pe.wait_ge(timed, b + 3)
                    pe.wait_ge(added, b + 1)
                    for kc in range(KC):
                        pe.matmul(psM[:, u, 0:C], prod[:, u, kc * P:(kc + 1) * P], wp[:, kc, :],
                                  start=kc == 0, stop=False)
                    for r in range(2):
                        t = pe.matmul(psM[:, u, 0:C], k.ones[0:1, :], bias[:, r, :], start=False, stop=r == 1)
                    t.then_inc(projected, 1)
                two_at_a_time(pe, NB, body)


def gather_groups(nc, z, block, k, table, rows, ring, idx, landed, gathered, ready, go, freed):
    turns = z.NGT // R

    @block.sync
    def _(sp):
        def load(g, s):
            sp.dma_start(idx[:, s, :], rows[:, ds(g * G, G)]).then_inc(landed[s], 16)
        for s in range(R):
            load(s, s)
        with sp.Fori(1, turns) as i:
            for s in range(R):
                pair = sp.value_load(k.last_pair[0:1, ds((i - 1) * R + s, 1)], min_val=1,
                                     max_val=z.NG + z.NB + R)
                sp.wait_ge(freed, pair + 1)
                load(i * R + s, s)
        sp.wait_ge(ready, z.NGT)

    @block.gpsimd
    def _(p):
        def gather(i, s):
            p.wait_ge(landed[s], (i + 1) * 16)
            p.sem_inc(go, 1)
            for j in range(G):
                p.indirect_dma_start(ring[:, s * G + j, :], None, table,
                                     bass.IndirectOffsetOnAxis(ap=idx[:, s, j:j + 1], axis=0)
                                     ).then_inc(gathered[s], 16)

        def report(i, s):
            p.wait_ge(gathered[s], (i + 1) * 16 * G)
            p.sem_inc(ready, 1)
        gather(0, 0)
        for s in range(1, R):
            gather(0, s)
            report(0, s - 1)
        with p.Fori(1, turns) as i:
            for s in range(R):
                gather(i, s)
                if s:
                    report(i, s - 1)
                else:
                    report(i - 1, R - 1)
        report(turns - 1, R - 1)


class Pair:

    def __init__(self, t, eng):
        self.before = eng.snap(t + 1)
        self.now = eng.snap(t + 2)
        self.next = eng.snap(t + 3)


def pairs(eng, z, k, before, pair, after):
    with eng.Fori(0, z.NB) as b:
        first = eng.value_load(k.first_group[0:1, ds(b, 1)], min_val=0, max_val=z.NG - 1)
        end = eng.value_load(k.first_group[0:1, ds(b + 1, 1)], min_val=0, max_val=z.NG - 1)
        if before:
            before(b)
        with eng.Fori(first, end + 1) as g:
            t = g + b
            pair(g, b, Pair(t, eng))
        if after:
            after(b, end)


def one_hot(v, k, onehot, iota_b, g):
    return v.tensor_tensor(onehot[:], iota_b[:].unsqueeze(1).to_broadcast([P, G, P]),
                           k.dstf[:, ds(g * G, G)].unsqueeze(2).to_broadcast([P, G, P]), ALU.is_equal)


def attention(nc, z, k, S):
    NB = z.NB
    with ExitStack() as c:
        sem = lambda n: c.enter_context(nc.semaphore("ga_" + n))
        sb = lambda n, s, d=F32: c.enter_context(nc.sbuf_tensor("ga_" + n, s, d))
        ring = sb("ring", [P, R * G, HROW])
        idx = sb("idx", [P, R, G], I32)
        iota_b = sb("iota_b", [P, P])
        onehot = sb("onehot", [P, G, P])
        onehot_t = sb("onehot_t", [P, G, P])
        sta = sb("sta", [P, G, HEADS])
        stb = sb("stb", [P, G, HEADS])
        starts = sb("starts", [G * HEADS, P])
        scan = sb("scan", [G * HEADS, P])
        runs = sb("runs", [P, 2 * G, HEADS + 1])
        miss = sb("miss", [P, G])
        cand = sb("cand", [P, G, HEADS])
        red = sb("red", [P, HEADS])
        top = sb("top", [P, HEADS])
        tot = sb("tot", [P, HEADS])
        look = sb("look", [P, 2 * HEADS])
        old = sb("old", [P, HEADS])
        esum = sb("esum", [P, G, HEADS])
        elog = sb("elog", [P, G, HEADS])
        arg = sb("arg", [P, G + 1, HEADS])
        w = sb("w", [P, G + 1, HEADS])
        msg = sb("msg", [P, G, MROW])
        acc = sb("acc", [P, MROW])
        rden = sb("rden", [P, HEADS])
        out = sb("out", [P, C])
        psI = c.enter_context(nc.psum_tensor("ga_psI", [P, 512], F32))
        psQ = c.enter_context(nc.psum_tensor("ga_psQ", [P, 512], F32))
        psT = c.enter_context(nc.psum_tensor("ga_psT", [P, G, P], F32))
        psX = c.enter_context(nc.psum_tensor("ga_psX", [P, 512], F32))
        psL = c.enter_context(nc.psum_tensor("ga_psL", [P, 512], F32))
        psS = c.enter_context(nc.psum_tensor("ga_psS", [P, 512], F32))
        landed = [sem(f"landed{s}") for s in range(R)]
        gathered = [sem(f"gathered{s}") for s in range(R)]
        ready, go, step, hot, hot_t, turned = (sem(x) for x in ("ready", "go", "step", "hot", "hot_t", "turned"))
        m_staged, m_turned, m_starts, m_scan, m_back, m_runs = (
            sem("m_" + x) for x in ("staged", "turned", "starts", "scan", "back", "runs"))
        maxed, shifts, looked, args, weights, messages, summed, added = (
            sem(x) for x in ("maxed", "shifts", "looked", "args", "weights", "messages", "summed", "added"))
        GH = G * HEADS
        psX_v = psX[:, 0:G * (HEADS + 1)].rearrange("p (j h) -> p j h", j=G)
        psL_v = psL[:, 0:G * 2 * HEADS].rearrange("p (j h) -> p j h", j=G)
        psQ_v = psQ[:, 0:GH].rearrange("p (j h) -> p j h", j=G)
        hd = HEADS * HD
        with nc.Block() as block:
            gather_groups(nc, z, block, k, k.h_dram, k.src, ring, idx, landed, gathered, ready, go, messages)

            def slot(g):
                return (g % R) * G

            @block.scalar
            def _(act):
                def stage(g, n1):
                    act.wait_ge(ready, g + 1)
                    act.wait_ge(m_turned, n1)
                    act.nop()
                    act.copy(sta[:], ring[:, ds(slot(g), G), hd:HROW])
                    act.copy(stb[:], k.start[:, ds(g * G, G)].unsqueeze(2).to_broadcast([P, G, HEADS])
                             ).then_inc(m_staged, 1)

                def spread(g, n, maxed_before):
                    act.wait_ge(maxed, maxed_before)
                    act.wait_ge(m_turned, n)
                    act.nop()
                    act.copy(starts[:], psI[0:GH, P:2 * P])
                    act.copy(runs[:, ds((g % 2) * G, G), HEADS:HEADS + 1],
                             k.last[:, ds(g * G, G)].unsqueeze(2)).then_inc(m_starts, 1)
                for s in (m_staged, m_starts, hot_t, weights):
                    act.sem_inc(s, 1)
                stage(0, 1)
                spread(0, 2, 1)

                def pair(g, b, t):
                    stage(g + 1, t.now)
                    act.wait_ge(turned, t.now)
                    act.wait_ge(looked, t.before)
                    act.nop()
                    for q in range(G // 4):
                        o = act.copy(onehot_t[:, 4 * q:4 * q + 4, :], psT[:, 4 * q:4 * q + 4, :])
                    o.then_inc(hot_t, 1)
                    spread(g + 1, t.next, t.before)
                    act.wait_ge(args, t.now)
                    act.wait_ge(added, t.before)
                    act.nop()
                    act.activation(w[:], arg[:], ACT.Exp).then_inc(weights, 1)
                pairs(act, z, k, None, pair, None)

            @block.tensor
            def _(pe):
                def turn(n, n1):
                    pe.wait_ge(m_staged, n)
                    pe.wait_ge(m_scan, n1)
                    pe.sem_inc(step, 1)
                    pe.transpose(psI[0:GH, 0:P], sta[:].rearrange("p j h -> p (j h)"), k.ident[:])
                    pe.transpose(psI[0:GH, P:2 * P], stb[:].rearrange("p j h -> p (j h)"), k.ident[:]
                                 ).then_inc(m_turned, 1)

                def back(n, n1):
                    pe.wait_ge(m_scan, n)
                    pe.wait_ge(m_runs, n1)
                    pe.sem_inc(step, 1)
                    pe.transpose(psQ[:, 0:GH], scan[:], k.ident[0:GH, 0:GH]).then_inc(m_back, 1)
                for s in (m_turned, m_back, turned, maxed, looked, summed):
                    pe.sem_inc(s, 1)
                turn(2, 1)
                back(2, 1)

                def pair(g, b, t):
                    pe.wait_ge(hot, t.now)
                    pe.wait_ge(hot_t, t.before)
                    for j in range(G):
                        o = pe.transpose(psT[:, j, :], onehot[:, j, :], k.ident[:])
                    o.then_inc(turned, 1)
                    pe.wait_ge(m_runs, t.now)
                    pe.wait_ge(m_starts, t.now)
                    pe.wait_ge(shifts, t.before)
                    for j in range(G):
                        o = pe.matmul(psX_v[:, j, :], onehot[:, j, :], runs[:, ds((g % 2) * G + j, 1), :],
                                      start=True, stop=True)
                    o.then_inc(maxed, 1)
                    turn(t.next, t.now)
                    pe.wait_ge(shifts, t.now)
                    pe.wait_ge(hot_t, t.now)
                    pe.wait_ge(args, t.before)
                    for j in range(G):
                        o = pe.matmul(psL_v[:, j, :], onehot_t[:, j, :], look[:], start=True, stop=True)
                    o.then_inc(looked, 1)
                    back(t.next, t.now)
                    pe.wait_ge(messages, t.now)
                    pe.wait_ge(added, t.before)
                    for j in range(G):
                        o = pe.matmul(psS[:, 0:MROW], onehot[:, j, :], msg[:, j, :], start=j == 0,
                                      stop=j == G - 1)
                    o.then_inc(summed, 1)
                pairs(pe, z, k, None, pair, None)

            @block.vector
            def _(v):
                def scan_runs(n, n1):
                    v.wait_ge(m_starts, n)
                    v.wait_ge(m_back, n1)
                    v.tensor_tensor_scan(scan[:], starts[:], psI[0:GH, 0:P], -BIG, ALU.add, ALU.max
                                         ).then_inc(m_scan, 1)

                def ends(g, n):
                    v.wait_ge(m_back, n)
                    v.tensor_tensor(runs[:, ds((g % 2) * G, G), 0:HEADS], psQ_v,
                                    k.last[:, ds(g * G, G)].unsqueeze(2).to_broadcast([P, G, HEADS]),
                                    ALU.mult).then_inc(m_runs, 1)
                for s in (m_scan, m_runs, hot, shifts, args, messages, added):
                    v.sem_inc(s, 1)
                v.tensor_scalar(iota_b[:], k.iota[:], -float(P), None, ALU.add)
                scan_runs(2, 1)
                ends(0, 2)

                def before(b):
                    v.memset(acc[:], 0.0)
                    v.memset(top[:], -BIG)
                    v.memset(old[:], -BIG)
                    v.tensor_copy(look[:, 0:HEADS], k.a2[:, ds(b * HEADS, HEADS)])
                    v.drain()
                    v.tensor_scalar(iota_b[:], iota_b[:], float(P), None, ALU.add)
                    v.drain()

                def pair(g, b, t):
                    v.wait_ge(summed, t.before)
                    one_hot(v, k, onehot, iota_b, g).then_inc(hot, 1)
                    v.tensor_tensor(msg[:, :, hd:MROW],
                                    k.iota[:, 0:REL].unsqueeze(1).to_broadcast([P, G, REL]),
                                    k.etf[:, ds(g * G, G)].unsqueeze(2).to_broadcast([P, G, REL]), ALU.is_equal)
                    v.wait_ge(maxed, t.now)
                    v.tensor_scalar(miss[:], psX_v[:, :, HEADS], -1.0, BIG, ALU.add, ALU.mult)
                    v.drain()
                    v.tensor_tensor(cand[:], psX_v[:, :, 0:HEADS],
                                    miss[:].unsqueeze(2).to_broadcast([P, G, HEADS]), ALU.add)
                    v.drain()
                    v.tensor_reduce(red[:], cand[:].rearrange("p j h -> p h j"), AX.X, ALU.max)
                    v.drain()
                    v.tensor_tensor(top[:], top[:], red[:], ALU.max)
                    v.drain()
                    v.tensor_tensor(tot[:], top[:], look[:, 0:HEADS], ALU.add)
                    v.drain()
                    v.scalar_tensor_tensor(look[:, HEADS:], tot[:], SLOPE, tot[:], ALU.mult, ALU.max
                                           ).then_inc(shifts, 1)
                    scan_runs(t.next, t.now)
                    v.wait_ge(looked, t.now)
                    v.tensor_tensor(esum[:], ring[:, ds(slot(g), G), hd:HROW], psL_v[:, :, 0:HEADS], ALU.add)
                    v.tensor_tensor(arg[:, G, :], old[:], look[:, HEADS:], ALU.subtract)
                    v.drain()
                    v.scalar_tensor_tensor(elog[:], esum[:], SLOPE, esum[:], ALU.mult, ALU.max)
                    v.tensor_copy(old[:], look[:, HEADS:])
                    v.drain()
                    v.tensor_tensor(arg[:, 0:G, :], elog[:], psL_v[:, :, HEADS:], ALU.subtract
                                    ).then_inc(args, 1)
                    ends(g + 1, t.next)
                    v.wait_ge(weights, t.now)
                    v.scalar_tensor_tensor(
                        msg[:, :, 0:hd].rearrange("p j (h d) -> p j h d", d=HD),
                        w[:, 0:G, :].unsqueeze(3).to_broadcast([P, G, HEADS, HD]), 1.0,
                        ring[:, ds(slot(g), G), 0:hd].rearrange("p j (h d) -> p j h d", d=HD),
                        ALU.min, ALU.mult).then_inc(messages, 1)
                    v.tensor_tensor(acc[:, 0:hd].rearrange("p (h d) -> p h d", d=HD),
                                    acc[:, 0:hd].rearrange("p (h d) -> p h d", d=HD),
                                    w[:, G, :].unsqueeze(2).to_broadcast([P, HEADS, HD]), ALU.mult)
                    v.drain()
                    v.wait_ge(summed, t.now)
                    v.tensor_tensor(acc[:], acc[:], psS[:, 0:MROW], ALU.add).then_inc(added, 1)

                def after(b, end):
                    heads = acc[:, 0:hd].rearrange("p (h d) -> p h d", d=HD)
                    v.drain()
                    v.tensor_scalar(rden[:], heads[:, :, D], 1e-30, None, ALU.max)
                    v.tensor_scalar(red[:, 0:HEADS], acc[:, hd:hd + HEADS], 1.0, None, ALU.max)
                    v.tensor_scalar(tot[:, 0:HEADS], acc[:, hd + HEADS:MROW], 1.0, None, ALU.max)
                    v.drain()
                    v.reciprocal(rden[:], rden[:])
                    v.reciprocal(k.icnt[:, ds(b * REL, HEADS)], red[:])
                    v.reciprocal(k.icnt[:, ds(b * REL + HEADS, HEADS)], tot[:])
                    v.drain()
                    v.tensor_tensor(out[:].rearrange("p (h d) -> p h d", d=D), heads[:, :, 0:D],
                                    rden[:].unsqueeze(2).to_broadcast([P, HEADS, D]), ALU.mult)
                    v.drain()
                    v.tensor_tensor(k.xb[:, ds(b * C, C)], k.xb[:, ds(b * C, C)], out[:], ALU.add)
                pairs(v, z, k, before, pair, after)


def relations(nc, z, k, S):
    with ExitStack() as c:
        sem = lambda n: c.enter_context(nc.semaphore("rg_" + n))
        sb = lambda n, s, d=F32: c.enter_context(nc.sbuf_tensor("rg_" + n, s, d))
        ring = sb("ring", [P, R * G, C])
        idx = sb("idx", [P, R, G], I32)
        iota_b = sb("iota_b", [P, P])
        onehot = sb("onehot", [P, G, P])
        onehot_t = sb("onehot_t", [P, G, P])
        look = sb("look", [P, REL])
        rel = sb("rel", [P, G, REL])
        picked = sb("picked", [P, G, REL])
        w = sb("w", [P, G])
        wonehot = sb("wonehot", [P, G, P])
        acc = sb("acc", [P, C])
        psT = c.enter_context(nc.psum_tensor("rg_psT", [P, G, P], F32))
        psL = c.enter_context(nc.psum_tensor("rg_psL", [P, 512], F32))
        psS = c.enter_context(nc.psum_tensor("rg_psS", [P, 512], F32))
        landed = [sem(f"landed{s}") for s in range(R)]
        gathered = [sem(f"gathered{s}") for s in range(R)]
        ready, go, hot, hot_t, turned, looked, weighted, summed, added = (
            sem(x) for x in ("ready", "go", "hot", "hot_t", "turned", "looked", "weighted", "summed", "added"))
        psL_v = psL[:, 0:G * REL].rearrange("p (j r) -> p j r", j=G)
        with nc.Block() as block:
            gather_groups(nc, z, block, k, k.y_dram, k.src_rel, ring, idx, landed, gathered,
                          ready, go, summed)

            @block.scalar
            def _(act):
                def pair(g, b, t):
                    act.wait_ge(turned, t.now)
                    act.wait_ge(looked, t.before)
                    act.nop()
                    for q in range(G // 4):
                        o = act.copy(onehot_t[:, 4 * q:4 * q + 4, :], psT[:, 4 * q:4 * q + 4, :])
                    o.then_inc(hot_t, 1)
                act.sem_inc(hot_t, 1)
                pairs(act, z, k, None, pair, None)

            @block.tensor
            def _(pe):
                def pair(g, b, t):
                    pe.wait_ge(hot, t.now)
                    pe.wait_ge(hot_t, t.before)
                    for j in range(G):
                        o = pe.transpose(psT[:, j, :], onehot[:, j, :], k.ident[:])
                    o.then_inc(turned, 1)
                    pe.wait_ge(hot_t, t.now)
                    pe.wait_ge(weighted, t.before)
                    for j in range(G):
                        o = pe.matmul(psL_v[:, j, :], onehot_t[:, j, :], look[:], start=True, stop=True)
                    o.then_inc(looked, 1)
                    pe.wait_ge(weighted, t.now)
                    pe.wait_ge(ready, g + 1)
                    pe.wait_ge(added, t.before)
                    for j in range(G):
                        o = pe.matmul(psS[:, 0:C], wonehot[:, j, :], ring[:, ds((g % R) * G + j, 1), :],
                                      start=j == 0, stop=j == G - 1)
                    o.then_inc(summed, 1)
                for s in (turned, looked, summed):
                    pe.sem_inc(s, 1)
                pairs(pe, z, k, None, pair, None)

            @block.vector
            def _(v):
                for s in (hot, weighted, added):
                    v.sem_inc(s, 1)
                v.tensor_scalar(iota_b[:], k.iota[:], -float(P), None, ALU.add)
                v.drain()

                def before(b):
                    v.tensor_scalar(iota_b[:], iota_b[:], float(P), None, ALU.add)
                    v.tensor_copy(look[:], k.icnt[:, ds(b * REL, REL)])
                    v.drain()

                def pair(g, b, t):
                    one_hot(v, k, onehot, iota_b, g).then_inc(hot, 1)
                    v.tensor_tensor(rel[:], k.iota[:, 0:REL].unsqueeze(1).to_broadcast([P, G, REL]),
                                    k.etf[:, ds(g * G, G)].unsqueeze(2).to_broadcast([P, G, REL]), ALU.is_equal)
                    v.drain()
                    v.wait_ge(looked, t.now)
                    v.tensor_tensor(picked[:], rel[:], psL_v, ALU.mult)
                    v.drain()
                    v.tensor_reduce(w[:], picked[:], AX.X, ALU.add)
                    v.drain()
                    v.tensor_tensor(wonehot[:], onehot[:], w[:].unsqueeze(2).to_broadcast([P, G, P]),
                                    ALU.mult).then_inc(weighted, 1)
                    v.wait_ge(summed, t.now)
                    v.tensor_tensor(k.xb[:, ds(b * C, C)], k.xb[:, ds(b * C, C)], psS[:, 0:C],
                                    ALU.add).then_inc(added, 1)
                    v.drain()
                pairs(v, z, k, before, pair, None)


def relation_rows(nc, z, k, S, ctxw, ksum):
    NB = z.NB
    with ExitStack() as c:
        work = c.enter_context(ExitStack())
        sem = lambda n: c.enter_context(nc.semaphore("rr_" + n))
        sb = lambda n, s, d=F32: work.enter_context(nc.sbuf_tensor("rr_" + n, s, d))
        wr = sb("wr", [P, KC, REL * C])
        rkq = sb("rkq", [P, KC, 3 * C])
        bias = sb("bias", [1, 2, C])
        comp = sb("comp", [P, REL * NE])
        with ExitStack() as c2:
            basis = c2.enter_context(nc.sbuf_tensor("rr_basis", [P, NE, KC, C], F32))
            nb = S["L1_gnn_basis"].shape[0]
            load_weights(nc, "rr_load", [
                (basis[:, b, :, :], rows_of(S["L1_gnn_basis"][b])) for b in range(nb)] + [
                (comp[:], S["L1_gnn_comp"].rearrange("r b -> (r b)").partition_broadcast(P)),
                (rkq[:, :, 0:C], rows_of(S["L1_gnn_root"])),
                (rkq[:, :, C:2 * C], rows_of(S["L1_mix_Wk_t"])),
                (rkq[:, :, 2 * C:], rows_of(S["L1_mix_Wq_t"])),
                (bias[:, 0, :], S["L1_gnn_bias"].rearrange("(o n) -> o n", o=1)),
                (bias[:, 1, :], S["L1_mix_bproj"].rearrange("(o n) -> o n", o=1))])
            with nc.Block() as block:
                @block.vector
                def _(v):
                    for b in range(nb):
                        for r in range(REL):
                            w = wr[:, :, r * C:(r + 1) * C]
                            s = comp[:, r * nb + b:r * nb + b + 1]
                            if b == 0:
                                v.tensor_scalar(w, basis[:, b, :, :], s, None, ALU.mult)
                            else:
                                v.scalar_tensor_tensor(w, basis[:, b, :, :], s, w, ALU.mult, ALU.add)
                        v.drain()
        st = sb("st", [P, 2, C + 2])
        xt = sb("xt", [P, 2, C])
        y = sb("y", [P, 2, REL * C // 2])
        low = sb("low", [P, 2, 2 * C])
        kk = sb("kk", [P, 2, C])
        zero = sb("zero", [P, C + 2])
        psT = c.enter_context(nc.psum_tensor("rr_psT", [P, 512], F32))
        psY = c.enter_context(nc.psum_tensor("rr_psY", [P, 2, 512], F32))
        psR = c.enter_context(nc.psum_tensor("rr_psR", [P, 512], F32))
        psQ = c.enter_context(nc.psum_tensor("rr_psQ", [P, 512], F32))
        psC = c.enter_context(nc.psum_tensor("rr_psC", [P, 2, 512], F32))
        YP = REL * C // 512
        staged, turned, back, rooted, root_in, kq, floored, powered, kq_in, summed, parts, parts_in = (
            sem(x) for x in ("staged", "turned", "back", "rooted", "root_in", "kq", "floored", "powered",
                             "kq_in", "summed", "parts", "parts_in"))
        stored = [sem("stored0"), sem("stored1")]
        with nc.Block() as block:
            @block.vector
            def _(v):
                v.memset(zero[:], 0.0)
                v.memset(st[:], 1.0)
        with nc.Block() as block:
            @block.scalar
            def _(act):
                for s in (staged, powered):
                    act.sem_inc(s, 2)
                act.sem_inc(parts_in, 2)

                def body(b, u, i, last):
                    act.wait_ge(summed, b + 1)
                    act.nop()
                    act.copy(st[:, u, 0:C], k.xa[:, ds(b * C, C)]).then_inc(staged, 1)
                    act.wait_ge(floored, b + 3)
                    act.nop()
                    act.activation(low[:, u, :], low[:, u, :], ACT.Exp).then_inc(powered, 1)
                    for q in range(YP):
                        half, at = divmod(q, YP // 2)
                        if at == 0 and not (isinstance(b, int) and b == 0):
                            act.wait_ge(stored[half], b * 16)
                        act.wait_ge(parts, b * YP + q + 1)
                        act.nop()
                        act.copy(y[:, half, at * 512:(at + 1) * 512], psY[:, q % 2, :]).then_inc(parts_in, 1)
                two_at_a_time(act, NB, body, peel=True)

            @block.tensor
            def _(pe):
                for s in (turned, rooted, kq, summed):
                    pe.sem_inc(s, 2)
                for kc in range(KC):
                    pe.matmul(psC[:, kc, 0:C + 2], zero[:, 0:P], zero[:], start=True, stop=False)

                def body(b, u, i, last):
                    pe.wait_ge(staged, b + 3)
                    pe.wait_ge(back, b + 2)
                    for kc in range(KC):
                        t = pe.transpose(psT[:, kc * P:(kc + 1) * P], st[:, u, kc * P:(kc + 1) * P], k.ident[:])
                    t.then_inc(turned, 1)
                    pe.wait_ge(back, b + 3)
                    pe.wait_ge(kq_in, b + 2)
                    for kc in range(KC):
                        t = pe.matmul(psQ[:, :], xt[:, u, kc * P:(kc + 1) * P], rkq[:, kc, C:],
                                      start=kc == 0, stop=kc == KC - 1)
                    t.then_inc(kq, 1)
                    pe.wait_ge(root_in, b + 2)
                    for kc in range(KC):
                        pe.matmul(psR[:, 0:C], xt[:, u, kc * P:(kc + 1) * P], rkq[:, kc, 0:C],
                                  start=kc == 0, stop=False)
                    for r in range(2):
                        t = pe.matmul(psR[:, 0:C], k.ones[0:1, :], bias[:, r, :], start=False, stop=r == 1)
                    t.then_inc(rooted, 1)
                    for q in range(YP):
                        pe.wait_ge(parts_in, b * YP + q + 1)
                        for kc in range(KC):
                            t = pe.matmul(psY[:, q % 2, :], xt[:, u, kc * P:(kc + 1) * P],
                                          wr[:, kc, q * 512:(q + 1) * 512], start=kc == 0, stop=kc == KC - 1)
                        t.then_inc(parts, 1)
                    pe.wait_ge(kq_in, b + 3)
                    for kc in range(KC):
                        t = pe.matmul(psC[:, kc, 0:C + 2], kk[:, u, kc * P:(kc + 1) * P], st[:, u, :],
                                      start=False, stop=last)
                    t.then_inc(summed, 1)
                two_at_a_time(pe, NB, body)

            @block.vector
            def _(v):
                for s in (back, root_in, floored, kq_in):
                    v.sem_inc(s, 2)

                def body(b, u, i, last):
                    v.wait_ge(turned, b + 3)
                    v.wait_ge(summed, b + 1)
                    v.tensor_copy(xt[:, u, :], psT[:, 0:C]).then_inc(back, 1)
                    v.wait_ge(kq, b + 3)
                    v.tensor_scalar(low[:, u, :], psQ[:, :], 0.0, None, ALU.min).then_inc(floored, 1)
                    v.wait_ge(rooted, b + 3)
                    v.tensor_tensor(k.xb[:, ds(b * C, C)], k.xb[:, ds(b * C, C)], psR[:, 0:C], ALU.add
                                    ).then_inc(root_in, 1)
                    v.wait_ge(powered, b + 3)
                    v.wait_ge(staged, b + 3)
                    if last:
                        v.scalar_tensor_tensor(kk[:, u, :], psQ[:, 0:C], 0.0, low[:, u, 0:C], ALU.max, ALU.add)
                        v.drain()
                        v.tensor_scalar(kk[:, u, :], kk[:, u, :], k.mask[:, 0:1], None, ALU.mult)
                    else:
                        v.scalar_tensor_tensor(kk[:, u, :], psQ[:, 0:C], 0.0, low[:, u, 0:C], ALU.max, ALU.add)
                    v.scalar_tensor_tensor(k.xa[:, ds(b * C, C)], psQ[:, C:2 * C], 0.0, low[:, u, C:], ALU.max,
                                           ALU.add).then_inc(kq_in, 1)
                two_at_a_time(v, NB, body)

            @block.sync
            def _(sp):
                rows = k.y_dram.rearrange("(n r) c -> n (r c)", r=REL)

                def body(b, u, i, last):
                    for half in range(2):
                        width = REL * C // 2
                        sp.wait_ge(parts_in, b * YP + YP // 2 * (half + 1) + 2)
                        sp.dma_start(rows[ds(b * P, P), half * width:(half + 1) * width], y[:, half, :]
                                     ).then_inc(stored[half], 16)
                two_at_a_time(sp, NB, body)
                for half in range(2):
                    sp.wait_ge(stored[half], 16 * NB)
        work.close()
        sb = lambda n, s, d=F32: c.enter_context(nc.sbuf_tensor("rr_" + n, s, d))
        wv = sb("wv", [P, KC, C])
        wp = sb("wp", [P, KC, C])
        cs = sb("cs", [P, KC, C + 2])
        ct = sb("ct", [P, KC, C])
        cbd = sb("cbd", [P, KC, C])
        kcol = sb("kcol", [P, KC, P])
        load_weights(nc, "rr_load2", [(wv[:], rows_of(S["L1_mix_Wv_t"])), (wp[:], rows_of(S["L1_mix_Wproj_t"]))])
        step, done = sem("step"), sem("done")
        with nc.Block() as block:
            @block.vector
            def _(v):
                v.memset(cbd[:], 0.0)
                v.tensor_copy(cs[:], psC[:, :, 0:C + 2])
                v.drain()
                for kc in range(KC):
                    o = v.tensor_scalar(kcol[:, kc, :], k.ones[:], cs[:, kc, C:C + 1], None, ALU.mult)
                o.then_inc(step, 1)
                v.wait_ge(done, 1)
                v.tensor_copy(ct[:], psC[:, :, 0:C])
                v.tensor_copy(ksum[:], psT[:, 0:C]).then_inc(step, 1)
                v.wait_ge(done, 2)
                for kc in range(KC):
                    for q in range(P // D):
                        a = kc * P + q * D
                        o = v.tensor_copy(cbd[q * D:(q + 1) * D, kc, a:a + D],
                                          psY[q * D:(q + 1) * D, kc, a:a + D])
                o.then_inc(step, 1)
                v.wait_ge(done, 3)
                v.tensor_copy(ctxw[:], psC[:, :, 0:C])

            @block.tensor
            def _(pe):
                pe.wait_ge(step, 1)
                for m in range(KC):
                    for kc in range(KC):
                        pe.transpose(psC[:, m, kc * P:(kc + 1) * P], cs[:, kc, m * P:(m + 1) * P], k.ident[:])
                for kc in range(KC):
                    t = pe.matmul(psT[:, kc * P:(kc + 1) * P], kcol[:, kc, :], k.ident[:], start=True, stop=True)
                t.then_inc(done, 1)
                pe.wait_ge(step, 2)
                for m in range(KC):
                    for kc in range(KC):
                        t = pe.matmul(psY[:, m, 0:C], wv[:, kc, m * P:(m + 1) * P], ct[:, kc, :],
                                      start=kc == 0, stop=kc == KC - 1)
                t.then_inc(done, 1)
                pe.wait_ge(step, 3)
                for m in range(KC):
                    for kc in range(KC):
                        t = pe.matmul(psC[:, m, 0:C], cbd[:, kc, m * P:(m + 1) * P], wp[:, kc, :],
                                      start=kc == 0, stop=kc == KC - 1)
                t.then_inc(done, 1)


def linear_attention_out(nc, z, k, ctxw, ksum):
    NB = z.NB
    with ExitStack() as c:
        sem = lambda n: c.enter_context(nc.semaphore("lo_" + n))
        sb = lambda n, s, d=F32: c.enter_context(nc.sbuf_tensor("lo_" + n, s, d))
        prod = sb("prod", [P, C])
        den = sb("den", [P, HEADS])
        st = sb("st", [P, 2, C])
        xt = sb("xt", [P, 2, C])
        psT = c.enter_context(nc.psum_tensor("lo_psT", [P, 2, 512], F32))
        psM = c.enter_context(nc.psum_tensor("lo_psM", [P, 2, 512], F32))
        scaled, turned, back, projected, added = (sem(x) for x in
            ("scaled", "turned", "back", "projected", "added"))
        with nc.Block() as block:
            @block.vector
            def _(v):
                v.sem_inc(scaled, 2)
                v.sem_inc(added, 2)

                def scale(b, u):
                    q = k.xa[:, ds(b * C, C)]
                    v.tensor_tensor(prod[:], q, ksum[:], ALU.mult)
                    v.drain()
                    v.tensor_reduce(den[:], prod[:].rearrange("p (h d) -> p h d", d=D), AX.X, ALU.add)
                    v.drain()
                    v.tensor_scalar(den[:], den[:], 1e-6, None, ALU.max)
                    v.drain()
                    v.reciprocal(den[:], den[:])
                    v.drain()
                    v.wait_ge(turned, b + 1)
                    v.tensor_tensor(st[:, u, :].rearrange("p (h d) -> p h d", d=D),
                                    q.rearrange("p (h d) -> p h d", d=D),
                                    den[:].unsqueeze(2).to_broadcast([P, HEADS, D]), ALU.mult
                                    ).then_inc(scaled, 1)

                def body(b, u, i, last):
                    if not last:
                        scale(b + 1, 1 - u)
                    v.wait_ge(projected, b + 3)
                    v.tensor_tensor(k.xb[:, ds(b * C, C)], k.xb[:, ds(b * C, C)], psM[:, u, 0:C], ALU.add
                                    ).then_inc(added, 1)
                scale(0, 0)
                two_at_a_time(v, NB, body)

            @block.tensor
            def _(pe):
                pe.sem_inc(turned, 2)
                pe.sem_inc(projected, 2)

                def body(b, u, i, last):
                    pe.wait_ge(scaled, b + 3)
                    pe.wait_ge(back, b + 1)
                    for kc in range(KC):
                        t = pe.transpose(psT[:, u, kc * P:(kc + 1) * P], st[:, u, kc * P:(kc + 1) * P], k.ident[:])
                    t.then_inc(turned, 1)
                    pe.wait_ge(back, b + 3)
                    pe.wait_ge(added, b + 1)
                    for kc in range(KC):
                        t = pe.matmul(psM[:, u, 0:C], xt[:, u, kc * P:(kc + 1) * P], ctxw[:, kc, :],
                                      start=kc == 0, stop=kc == KC - 1)
                    t.then_inc(projected, 1)
                two_at_a_time(pe, NB, body)

            @block.scalar
            def _(act):
                act.sem_inc(back, 2)

                def body(b, u, i, last):
                    act.wait_ge(turned, b + 3)
                    act.wait_ge(projected, b + 1)
                    act.nop()
                    act.copy(xt[:, u, :], psT[:, u, 0:C]).then_inc(back, 1)
                two_at_a_time(act, NB, body)


def experts(nc, z, k, name, norms, w1d, b1d, w2d, b2d, routed, br, gamma, beta, tokens, probs):
    NB = z.NB
    HID = w1d.shape[2]
    HC = HID // P
    with ExitStack() as c:
        sem = lambda n: c.enter_context(nc.semaphore(name + n))
        sb = lambda n, s, d=F32: c.enter_context(nc.sbuf_tensor(name + n, s, d))
        w1 = sb("w1", [P, NE, KC, HID])
        w2 = sb("w2", [P, NE, HC, C])
        b1 = sb("b1", [P, NE, HC])
        b2 = sb("b2", [NE, C])
        wr = sb("wr", [P, KC, NE])
        brow = sb("brow", [1, NE])
        cols = sb("cols", [P, 2, KC])
        lower = sb("lower", [P, NE, NE])
        st = sb("st", [P, 2, C])
        xt = sb("xt", [P, 2, C])
        lg = sb("lg", [P, NE])
        mx = sb("mx", [P, 2])
        ex = sb("ex", [P, NE])
        gt = sb("gt", [P, NE, NE])
        eq = sb("eq", [P, NE, NE])
        rank = sb("rank", [P, NE])
        gates = sb("gates", [P, 2, NE])
        gates_t = sb("gates_t", [NE, 2, P])
        hid = sb("hid", [P, 2, HC * P])
        psT = c.enter_context(nc.psum_tensor(name + "psT", [P, 512], F32))
        psG = c.enter_context(nc.psum_tensor(name + "psG", [P, 512], F32))
        psW = c.enter_context(nc.psum_tensor(name + "psW", [P, 512], F32))
        psB = c.enter_context(nc.psum_tensor(name + "psB", [P, 512], F32))
        psH = c.enter_context(nc.psum_tensor(name + "psH", [P, 2, 512], F32))
        psO = c.enter_context(nc.psum_tensor(name + "psO", [P, 2, 512], F32))
        loads = [(w1[:, e, :, :], rows_of(w1d[e])) for e in range(NE)]
        loads += [(w2[:, e, :, :], rows_of(w2d[e])) for e in range(NE)]
        loads += [(b1[:, e, :], b1d[e]) for e in range(NE)]
        loads += [(b2[:], b2d), (wr[:], rows_of(routed))]
        if br is not None:
            loads.append((brow[:], br.rearrange("(o n) -> o n", o=1)))
        if gamma is not None:
            loads += [(cols[:, 0, :], gamma), (cols[:, 1, :], beta)]
        load_weights(nc, name + "load", loads)
        zeroed = sem("zeroed")
        with nc.Block() as block:
            @block.gpsimd
            def _(p):
                p.memset(lower[:], 0.0).then_inc(zeroed, 1)
                p.wait_ge(zeroed, 1)
                p.affine_select(out=lower[:], in_=lower[:], compare_op=ALU.is_ge, fill=1.0, base=0,
                                pattern=[[-1, NE], [1, NE]], channel_multiplier=0)
            if br is None:
                @block.vector
                def _(v):
                    v.memset(brow[:], 0.0)
        staged, turned, back, logits, e_arg, e_done, gated, gates_turned, gates_back, biased, bias_in = (
            sem(x) for x in ("staged", "turned", "back", "logits", "e_arg", "e_done", "gated",
                             "gates_turned", "gates_back", "biased", "bias_in"))
        hidden, act_out, outs, taken = (sem(x) for x in ("hidden", "act_out", "outs", "taken"))
        with nc.Block() as block:
            @block.scalar
            def _(act):
                for s in (back, e_done, act_out):
                    act.sem_inc(s, 2)

                def prep(b, u):
                    act.wait_ge(turned, b + 3)
                    act.nop()
                    for kc in range(KC):
                        x = (xt[:, u, kc * P:(kc + 1) * P], psT[:, kc * P:(kc + 1) * P])
                        if gamma is None:
                            o = act.copy(*x)
                        else:
                            o = act.activation(*x, ACT.Identity, bias=cols[:, 1, kc:kc + 1], scale=cols[:, 0, kc:kc + 1])
                    o.then_inc(back, 1)

                def power(b):
                    act.wait_ge(e_arg, b + 3)
                    act.nop()
                    act.activation(ex[:], ex[:], ACT.Exp).then_inc(e_done, 1)

                def body(b, u, i, last):
                    for e in range(NE):
                        n = b * NE + e
                        act.wait_ge(hidden, n + 3)
                        act.wait_ge(outs, n + 1)
                        act.nop()
                        for q in range(HC):
                            o = act.activation(hid[:, e % 2, q * P:(q + 1) * P],
                                               psH[:, e % 2, q * P:(q + 1) * P], ACT.Gelu,
                                               bias=b1[:, e, q:q + 1])
                        o.then_inc(act_out, 1)
                        if e == 1 and not last:
                            prep(b + 1, 1 - u)
                        if e == 3 and not last:
                            power(b + 1)
                prep(0, 0)
                power(0)
                two_at_a_time(act, NB, body)

            @block.tensor
            def _(pe):
                for s in (turned, logits, gates_turned, biased, hidden, outs):
                    pe.sem_inc(s, 2)

                def prep(b, u):
                    pe.wait_ge(staged, b + 3)
                    pe.wait_ge(back, b + 2)
                    for kc in range(KC):
                        t = pe.transpose(psT[:, kc * P:(kc + 1) * P], st[:, u, kc * P:(kc + 1) * P], k.ident[:])
                    t.then_inc(turned, 1)

                def route(b, u):
                    pe.wait_ge(back, b + 3)
                    pe.wait_ge(gated, b + 2)
                    for kc in range(KC):
                        pe.matmul(psG[:, 0:NE], xt[:, u, kc * P:(kc + 1) * P], wr[:, kc, :],
                                  start=kc == 0, stop=False)
                    pe.matmul(psG[:, 0:NE], k.ones[0:1, :], brow[:], start=False, stop=True).then_inc(logits, 1)

                def bias(b, u):
                    pe.wait_ge(gated, b + 3)
                    pe.wait_ge(gates_back, b + 2)
                    pe.transpose(psW[0:NE, 0:P], gates[:, u, :], k.ident[:]).then_inc(gates_turned, 1)
                    pe.wait_ge(gates_back, b + 3)
                    pe.wait_ge(bias_in, b + 2)
                    pe.matmul(psB[:, 0:C], gates_t[:, u, :], b2[:], start=True, stop=True).then_inc(biased, 1)

                def hide(b, u, e):
                    pe.wait_ge(act_out, b * NE + e + 1)
                    for q in range(HC):
                        for kc in range(KC):
                            t = pe.matmul(psH[:, e % 2, q * P:(q + 1) * P], w1[:, e, kc, q * P:(q + 1) * P],
                                          xt[:, u, kc * P:(kc + 1) * P], start=kc == 0, stop=kc == KC - 1)
                    t.then_inc(hidden, 1)

                def body(b, u, i, last):
                    hide(b, u, 0)
                    for e in range(NE):
                        if e + 1 < NE:
                            hide(b, u, e + 1)
                        if not last:
                            if e == 1:
                                prep(b + 1, 1 - u)
                            if e == 3:
                                route(b + 1, 1 - u)
                            if e == 6:
                                bias(b + 1, 1 - u)
                        n = b * NE + e
                        pe.wait_ge(act_out, n + 3)
                        pe.wait_ge(taken, n + 1)
                        for q in range(HC):
                            t = pe.matmul(psO[:, e % 2, 0:C], hid[:, e % 2, q * P:(q + 1) * P],
                                          w2[:, e, q, :], start=q == 0, stop=q == HC - 1)
                        t.then_inc(outs, 1)
                prep(0, 0)
                route(0, 0)
                bias(0, 0)
                two_at_a_time(pe, NB, body)

            @block.vector
            def _(v):
                for s in (staged, e_arg, gated, gates_back, bias_in, taken):
                    v.sem_inc(s, 2)

                def prep(b, u):
                    v.wait_ge(turned, b + 1)
                    o = v.tensor_scalar(st[:, u, :], k.xb[:, ds(b * C, C)], norms[0][:, ds(b, 1)],
                                        norms[1][:, ds(b, 1)], ALU.subtract, ALU.mult)
                    if len(norms) == 4:
                        v.drain()
                        o = v.tensor_scalar(st[:, u, :], st[:, u, :], norms[2][:, ds(b, 1)],
                                            norms[3][:, ds(b, 1)], ALU.subtract, ALU.mult)
                    o.then_inc(staged, 1)
                    if tokens:
                        v.drain()
                        v.tensor_tensor(k.xb[:, ds(b * C, C)], k.xb[:, ds(b * C, C)], st[:, u, :], ALU.add)

                def choose(b, u):
                    v.wait_ge(logits, b + 3)
                    v.tensor_copy(lg[:], psG[:, 0:NE])
                    v.tensor_reduce(mx[:, 0:1], psG[:, 0:NE], AX.X, ALU.max)
                    v.drain()
                    v.tensor_scalar(ex[:], lg[:], mx[:, 0:1], None, ALU.subtract).then_inc(e_arg, 1)
                    if probs:
                        v.wait_ge(e_done, b + 3)
                        v.tensor_reduce(mx[:, 1:2], ex[:], AX.X, ALU.add)
                        v.drain()
                        v.reciprocal(mx[:, 1:2], mx[:, 1:2])
                        v.drain()
                        v.tensor_scalar(ex[:], ex[:], mx[:, 1:2], None, ALU.mult)
                        v.drain()
                        v.tensor_copy(lg[:], ex[:])
                        v.drain()
                    other = lg[:].unsqueeze(1).to_broadcast([P, NE, NE])
                    own = lg[:].unsqueeze(2).to_broadcast([P, NE, NE])
                    v.tensor_tensor(gt[:], other, own, ALU.is_gt)
                    v.tensor_tensor(eq[:], other, own, ALU.is_equal)
                    v.drain()
                    v.tensor_tensor(eq[:], eq[:], lower[:], ALU.mult)
                    v.drain()
                    v.tensor_tensor(gt[:], gt[:], eq[:], ALU.add)
                    v.drain()
                    v.tensor_reduce(rank[:], gt[:], AX.X, ALU.add)
                    v.drain()
                    v.tensor_scalar(rank[:], rank[:], 2.0, None, ALU.is_lt)
                    v.drain()
                    v.wait_ge(e_done, b + 3)
                    v.tensor_tensor(ex[:], ex[:], rank[:], ALU.mult)
                    v.drain()
                    v.tensor_reduce(mx[:, 1:2], ex[:], AX.X, ALU.add)
                    v.drain()
                    v.tensor_scalar(mx[:, 1:2], mx[:, 1:2], 1e-12, None, ALU.max)
                    v.drain()
                    v.reciprocal(mx[:, 1:2], mx[:, 1:2])
                    v.drain()
                    v.tensor_scalar(gates[:, u, :], ex[:], mx[:, 1:2], None, ALU.mult).then_inc(gated, 1)

                def biases(b, u):
                    v.wait_ge(gates_turned, b + 3)
                    v.tensor_copy(gates_t[:, u, :], psW[0:NE, 0:P]).then_inc(gates_back, 1)
                    v.drain()
                    v.wait_ge(biased, b + 3)
                    v.tensor_tensor(k.xb[:, ds(b * C, C)], k.xb[:, ds(b * C, C)], psB[:, 0:C], ALU.add
                                    ).then_inc(bias_in, 1)

                def body(b, u, i, last):
                    for e in range(NE):
                        if not last:
                            if e == 0:
                                prep(b + 1, 1 - u)
                            if e == 3:
                                choose(b + 1, 1 - u)
                            if e == 6:
                                biases(b + 1, 1 - u)
                        v.drain()
                        v.wait_ge(outs, b * NE + e + 3)
                        x = k.xb[:, ds(b * C, C)]
                        v.scalar_tensor_tensor(x, psO[:, e % 2, 0:C], gates[:, u, e:e + 1], x, ALU.mult,
                                               ALU.add).then_inc(taken, 1)
                prep(0, 0)
                choose(0, 0)
                biases(0, 0)
                two_at_a_time(v, NB, body)


class Kept:
    pass


def graph_network(nc, S, out):
    n, _ = out.shape
    z = Sizes(n, S["n_edges"])
    NB = z.NB
    k = Kept()
    with ExitStack() as c:
        sb = lambda n, s, d=F32: c.enter_context(nc.sbuf_tensor(n, s, d))
        k.xb = sb("xb", [P, NB * C])
        k.ident = sb("ident", [P, P])
        k.iota = sb("iota", [P, P])
        k.ones = sb("ones", [P, P])
        k.mask = sb("mask", [P, 1])
        k.a2 = sb("a2", [P, NB * HEADS])
        k.icnt = sb("icnt", [P, NB * REL])
        k.dstf = sb("dstf", [P, z.COLS])
        k.etf = sb("etf", [P, z.COLS], BF16)
        k.start = sb("start", [P, z.COLS], BF16)
        k.last = sb("last", [P, z.COLS], BF16)
        k.src = sb("src_row", [P, z.COLS], I32)
        k.src_rel = sb("src_rel_row", [P, z.COLS], I32)
        nch = -(-z.NG // P)
        k.first_group = sb("first_group", [1, NB + 1], I32)
        k.last_pair = sb("last_pair", [1, nch * P], I32)
        mean = sb("mean", [P, NB])
        rstd = sb("rstd", [P, NB])
        mean2 = sb("mean2", [P, NB])
        rstd2 = sb("rstd2", [P, NB])
        k.first_dram = nc.dram_tensor("first_dram", (NB + 1, 1), I32).ap()
        k.last_dram = nc.dram_tensor("last_dram", (nch * P, 1), I32).ap()
        k.h_dram = nc.dram_tensor("h_dram", (NB * P, HROW), F32).ap()
        k.y_dram = nc.dram_tensor("y_dram", (NB * P * REL, C), F32).ap()
        setup(nc, z, S, k)

        with nc.sbuf_tensor("xa0", [P, NB * C], F32) as xa:
            k.xa = xa
            normalise_stats(nc, "n0", k.xb, mean, rstd, 1e-5, NB)
            normalise_rows(nc, k.xa, k.xb, mean, rstd, NB)
            with nc.sbuf_tensor("wqc", [P, KC, C], F32) as wqc:
                with nc.sbuf_tensor("kt", [P, KC * NB * P], F32) as kt:
                    attention_table(nc, z, k, S, kt)
                    keys_to_context(nc, z, k, S, kt, wqc)
                normalise_stats(nc, "n1", k.xa, mean, rstd, 1e-5, NB)
                mix_out(nc, z, k, S, wqc, mean, rstd)
        attention(nc, z, k, S)
        with nc.sbuf_tensor("xa1", [P, NB * C], F32) as xa:
            k.xa = xa
            normalise_stats(nc, "n2", k.xb, mean, rstd, 1e-5, NB)
            normalise_rows(nc, k.xa, k.xb, mean, rstd, NB)
            normalise_stats(nc, "n3", k.xa, mean2, rstd2, 1e-5, NB)
        experts(nc, z, k, "f0_", (mean, rstd, mean2, rstd2), S["L0_ffn_W1"], S["L0_ffn_b1"], S["L0_ffn_W2"],
                    S["L0_ffn_b2"], S["L0_ffn_Wr"], S["L0_ffn_br"], S["L0_ffn_gamma"], S["L0_ffn_beta"],
                    False, False)
        with nc.sbuf_tensor("xa2", [P, NB * C], F32) as xa:
            k.xa = xa
            normalise_stats(nc, "n4", k.xb, mean, rstd, 1e-5, NB)
            normalise_rows(nc, k.xa, k.xb, mean, rstd, NB)
            with nc.sbuf_tensor("ctxw", [P, KC, C], F32) as ctxw, nc.sbuf_tensor("ksum", [P, C], F32) as ksum:
                relation_rows(nc, z, k, S, ctxw, ksum)
                linear_attention_out(nc, z, k, ctxw, ksum)
        relations(nc, z, k, S)
        normalise_stats(nc, "n5", k.xb, mean, rstd, 1e-5, NB)
        experts(nc, z, k, "f1_", (mean, rstd), S["L1_ffn_w1"], S["L1_ffn_b1"], S["L1_ffn_w2"],
                S["L1_ffn_b2"], S["L1_ffn_router_w_t"], None, None, None, True, True)
        with nc.semaphore("stored") as stored, nc.Block() as block:
            @block.sync
            def _(sp):
                full = (NB - 1) * P
                if full:
                    sp.dma_start(out[0:full, :].rearrange("(b p) f -> p b f", p=P),
                                 k.xb[:, 0:full // P * C].rearrange("p (b f) -> p b f", f=C)).then_inc(stored, 16)
                sp.dma_start(out[full:n, :], k.xb[0:z.TAIL, full // P * C:NB * C]).then_inc(stored, 16)
                sp.wait_ge(stored, 16 * (2 if full else 1))


COLUMNS = ("L0_gnn_attn_l", "L0_gnn_attn_r", "L0_mix_ln_g", "L0_mix_ln_b", "L0_mix_bg2", "L0_ffn_gamma",
           "L0_ffn_beta")


def _layouts(x, src, dst, edge_type_16, w):
    import numpy as np
    z = Sizes(x.shape[0], src.shape[0])
    E = src.shape[0]
    far = 1 << 20

    def table(a, fill):
        full = np.full(z.NGT * GE, fill, np.int32)
        full[:E] = a
        return full.reshape(z.NGT, P, G)
    lay = lambda a: np.ascontiguousarray(a.transpose(1, 0, 2).reshape(P, z.COLS))
    d = table(dst, far)
    before = np.full_like(d, -1)
    before[:, 1:] = d[:, :-1]
    behind = np.full_like(d, -1)
    behind[:, :-1] = d[:, 1:]
    xp = np.zeros((z.NB * P, C), np.float32)
    xp[:x.shape[0]] = x
    out = {"x": xp, "src": lay(table(src, 0)), "dst": lay(d), "dst_prev": lay(before),
           "dst_next": lay(behind), "etype": lay(table(edge_type_16, 0)),
           "bounds": np.ascontiguousarray(dst[GE - 1::GE][:z.NG - 1])}
    for name, a in w.items():
        a = np.asarray(a)
        if name == "L0_gnn_W":
            out["L0_gnn_W_t"] = a.T
        if name == "L0_mix_Wqkv":
            out["L0_mix_Wq_t"] = a[:, 0:C].T
        if name in COLUMNS:
            a = a.reshape(KC, P).T
        if name == "L1_mix_Wkv":
            out["L1_mix_Wk_t"], out["L1_mix_Wv_t"] = a[0:C].T, a[C:2 * C].T
        elif name in ("L1_mix_Wq", "L1_mix_Wproj", "L1_ffn_router_w"):
            out[name + "_t"] = a.T
        elif name in ("L0_ffn_b1", "L1_ffn_b1"):
            out[name] = a.reshape(NE, -1, P).transpose(0, 2, 1)
        else:
            out[name] = a
    return {name: np.ascontiguousarray(a) for name, a in out.items()}


def kernel(x, src, dst, edge_type_16, **weights):
    import numpy as _np
    import concourse.bacc as _bacc
    from concourse import mybir as _mybir
    from concourse.bass_utils import run_bass_kernel_spmd as _run

    x, src, dst, edge_type_16 = (_np.asarray(a) for a in (x, src, dst, edge_type_16))
    arrays = _layouts(x, src, dst, edge_type_16, weights)
    nc = _bacc.Bacc("TRN2", target_bir_lowering=False, num_devices=1)
    S = {"n_edges": src.shape[0]}
    for name, a in arrays.items():
        S[name] = nc.dram_tensor(name, a.shape, _mybir.dt.from_np(a.dtype), kind="ExternalInput").ap()
    out = nc.dram_tensor("out", x.shape, F32, kind="ExternalOutput").ap()
    graph_network(nc, S, out)
    r = _run(nc, [arrays], core_ids=[0])
    return r.results[0]["out"]
```

```python
from contextlib import ExitStack

import concourse.bass as bass
from concourse import mybir

P = 128
G = 8
R = 4
GE = G * P
C = 256
KC = C // P
HEADS = 8
D = C // HEADS
HD = D + 1
REL = 16
NE = 8
U = 3
AHEAD = 2
BASE = 3
HROW = HEADS * HD + HEADS
MROW = HEADS * HD + REL
SLOPE = 0.2
BIG = 1e30

ALU = mybir.AluOpType
ACT = mybir.ActivationFunctionType
AX = mybir.AxisListType
F32 = mybir.dt.float32
I32 = mybir.dt.int32
BF16 = mybir.dt.bfloat16
ds = bass.ds


def two_at_a_time(eng, n, body, peel=False):
    whole = (n - 1) // 2
    start = 0
    if peel and whole:
        body(0, 0, 0, False)
        body(1, 1, 0, False)
        start = 1
    if whole > start:
        with eng.Fori(start, whole) as k:
            body(k * 2, 0, k, False)
            body(k * 2 + 1, 1, k, False)
    for b in range(2 * whole, n):
        body(b, b % 2, b // 2, b == n - 1)


class Sizes:
    def __init__(self, n, e):
        self.N = n
        self.NB = -(-n // P)
        self.TAIL = n - (self.NB - 1) * P
        self.NG = -(-e // GE)
        self.T = -(-(self.NG + self.NB - 1) // U) * U
        while True:
            groups = self.T + AHEAD - (self.NB - 1)
            self.NGT = R * -(-groups // R)
            if self.NGT - R - 1 + self.NB - 1 < self.T:
                break
            self.T += U
        self.NCH = -(-max(self.T + AHEAD, self.NGT) // P)
        self.COLS = self.NGT * G


def normalise_stats(nc, name, src, mean, rstd, eps, NB):
    with ExitStack() as c:
        six = c.enter_context(nc.sbuf_tensor(name + "_six", [P, NB, 6], F32))
        tmp = c.enter_context(nc.sbuf_tensor(name + "_tmp", [P, 3, NB], F32))
        var_ready = c.enter_context(nc.semaphore(name + "_var_ready"))
        root_ready = c.enter_context(nc.semaphore(name + "_root_ready"))
        flat = six[:].rearrange("p b s -> p (b s)")
        with nc.Block() as block:
            @block.vector
            def _(v):
                with v.Fori(0, NB) as b:
                    v.bn_stats(flat[:, ds(b * 6, 6)], src[:, ds(b * C, C)])
                v.drain()
                v.tensor_tensor(tmp[:, 0, :], six[:, :, 1], six[:, :, 4], ALU.add)
                v.tensor_tensor(tmp[:, 1, :], six[:, :, 1], six[:, :, 4], ALU.subtract)
                v.tensor_tensor(tmp[:, 2, :], six[:, :, 2], six[:, :, 5], ALU.add)
                v.drain()
                v.tensor_scalar(mean[:, :], tmp[:, 0, :], 0.5, None, ALU.mult)
                v.tensor_tensor(tmp[:, 1, :], tmp[:, 1, :], tmp[:, 1, :], ALU.mult)
                v.tensor_scalar(tmp[:, 2, :], tmp[:, 2, :], 1.0 / C, eps, ALU.mult, ALU.add)
                v.drain()
                v.scalar_tensor_tensor(tmp[:, 0, :], tmp[:, 1, :], 0.25, tmp[:, 2, :], ALU.mult,
                                       ALU.add).then_inc(var_ready, 1)
                v.wait_ge(root_ready, 1)
                v.reciprocal(rstd[:, :], tmp[:, 1, :])

            @block.scalar
            def _(act):
                act.wait_ge(var_ready, 1)
                act.activation(tmp[:, 1, :], tmp[:, 0, :], ACT.Sqrt).then_inc(root_ready, 1)


def normalise_rows(nc, dst, src, mean, rstd, NB):
    with nc.Block() as block:
        @block.vector
        def _(v):
            with v.Fori(0, NB) as b:
                v.tensor_scalar(dst[:, ds(b * C, C)], src[:, ds(b * C, C)], mean[:, ds(b, 1)],
                                rstd[:, ds(b, 1)], ALU.subtract, ALU.mult)


def setup(nc, z, S, k):
    NB, NG = z.NB, z.NG
    with ExitStack() as c:
        sem = lambda n: c.enter_context(nc.semaphore("su_" + n))
        sb = lambda n, s, d=F32: c.enter_context(nc.sbuf_tensor("su_" + n, s, d))
        ints = sb("ints", [P, z.COLS], I32)
        others = sb("others", [P, 2, z.COLS], I32)
        othersf = sb("othersf", [P, 2, z.COLS])
        etypes = sb("etypes", [P, z.COLS], I32)
        bounds = sb("bounds", [NB + 1, NG - 1], I32)
        boundsf = sb("boundsf", [NB + 1, NG - 1])
        below = sb("below", [NB + 1, NG - 1])
        limit = sb("limit", [NB + 1, 1])
        counts = sb("counts", [NB + 1, 1])
        counti = sb("counti", [NB + 1, 1], I32)
        nch = z.NCH
        firsts = sb("firsts", [P, NB - 1], I32)
        firstsf = sb("firstsf", [P, NB - 1])
        gid = sb("gid", [P, nch])
        pairsf = sb("pairsf", [P, NB - 1])
        blockno = sb("blockno", [P, NB - 1])
        hit = sb("hit", [P, 2, nch, NB - 1])
        tables = sb("tables", [P, 2, nch])
        tablesi = sb("tablesi", [P, 2, nch], I32)
        blocks = sb("blocks", [P, nch * P], I32)
        srci = sb("srci", [P, z.COLS], I32)
        src_rel = sb("src_rel", [P, z.COLS], I32)
        iotas = sb("iotas", [P, P], I32)
        loaded, made, cvt, tab, tab2, tab3, ended = (sem(x) for x in
            ("loaded", "made", "cvt", "tab", "tab2", "tab3", "ended"))
        with nc.Block() as block:
            @block.sync
            def _(sp):
                sp.dma_start(ints[:], S["dst"]).then_inc(loaded, 16)
                sp.dma_start(others[:, 0, :], S["dst_prev"]).then_inc(loaded, 16)
                sp.dma_start(others[:, 1, :], S["dst_next"]).then_inc(loaded, 16)
                sp.dma_start(etypes[:], S["etype"]).then_inc(loaded, 16)
                sp.dma_start(bounds[:], S["bounds"].partition_broadcast(NB + 1)).then_inc(loaded, 16)
                sp.dma_start(k.xb[:].rearrange("p (b f) -> p b f", f=C),
                             S["x"].rearrange("(b p) f -> p b f", p=P)).then_inc(loaded, 16)
                sp.dma_start(srci[:], S["src"]).then_inc(loaded, 16)
                sp.wait_ge(loaded, 112)
                sp.wait_ge(cvt, 1)
                sp.dma_start(k.first_dram, counti[:]).then_inc(tab, 16)
                sp.wait_ge(tab, 16)
                row = k.first_dram.rearrange("n o -> o n")
                sp.dma_start(firsts[:], row[0, 1:NB].partition_broadcast(P)).then_inc(tab, 16)
                sp.wait_ge(tab, 32)
                sp.wait_ge(ended, 1)
                for i in range(nch):
                    for q in range(2):
                        sp.dma_start(k.table_dram[q, i * P:(i + 1) * P, :],
                                     tablesi[:, q, i:i + 1]).then_inc(tab2, 16)
                sp.dma_start(k.src_rel, src_rel[:]).then_inc(tab2, 16)
                sp.wait_ge(tab2, 16 * (2 * nch + 1))
                rows = k.table_dram.rearrange("q n o -> q (n o)")
                sp.dma_start(k.last_pair[:], rows[0:1, :]).then_inc(tab3, 16)
                sp.dma_start(k.pair_block[:], rows[1:2, :]).then_inc(tab3, 16)
                sp.dma_start(blocks[:], rows[1, :].partition_broadcast(P)).then_inc(tab3, 16)
                sp.wait_ge(tab3, 48)

            @block.gpsimd
            def _(p):
                p.memset(k.ident[:], 0.0).then_inc(made, 1)
                p.wait_ge(made, 1)
                p.affine_select(out=k.ident[:], in_=k.ident[:], compare_op=ALU.not_equal, fill=1.0,
                                base=0, pattern=[[-1, P]], channel_multiplier=1).then_inc(made, 1)
                p.memset(k.ones[:], 1.0)
                p.iota(iotas[:], [[1, P]], base=0, channel_multiplier=0).then_inc(made, 1)
                p.iota(k.pair_group[:], [[1, nch * P]], base=0, channel_multiplier=0)
                p.iota(limit[:], [[0, 1]], base=0, channel_multiplier=P,
                       allow_small_or_imprecise_dtypes=True)
                p.iota(gid[:], [[P, nch]], base=0, channel_multiplier=1,
                       allow_small_or_imprecise_dtypes=True)
                p.iota(blockno[:], [[1, NB - 1]], base=1, channel_multiplier=0,
                       allow_small_or_imprecise_dtypes=True)
                p.iota(k.mask[:], [[0, 1]], base=0, channel_multiplier=1,
                       allow_small_or_imprecise_dtypes=True).then_inc(made, 1)

            @block.vector
            def _(v):
                v.wait_ge(made, 4)
                v.wait_ge(loaded, 112)
                v.tensor_copy(k.iota[:], iotas[:])
                v.tensor_copy(boundsf[:], bounds[:])
                v.tensor_copy(k.dstf[:], ints[:])
                v.tensor_copy(k.etf[:], etypes[:])
                v.scalar_tensor_tensor(src_rel[:], srci[:], float(REL), etypes[:], ALU.mult, ALU.add)
                v.tensor_copy(othersf[:], others[:])
                v.tensor_scalar(k.mask[:], k.mask[:], float(z.TAIL), None, ALU.is_lt)
                v.drain()
                v.tensor_scalar(below[:], boundsf[:], limit[:, 0:1], None, ALU.is_lt)
                v.drain()
                v.tensor_reduce(counts[:], below[:], AX.X, ALU.add)
                v.drain()
                v.tensor_copy(counti[:], counts[:]).then_inc(cvt, 1)
                v.tensor_tensor(k.start[:], k.dstf[:], othersf[:, 0, :], ALU.not_equal)
                v.tensor_tensor(k.last[:], k.dstf[:], othersf[:, 1, :], ALU.not_equal)
                v.drain()
                v.tensor_scalar(k.start[:], k.start[:], -BIG, None, ALU.mult)
                v.wait_ge(tab, 32)
                v.tensor_copy(firstsf[:], firsts[:])
                v.drain()
                v.tensor_tensor(pairsf[:], firstsf[:], blockno[:], ALU.add)
                v.drain()
                for i in range(nch):
                    v.tensor_scalar(hit[:, 0, i, :], firstsf[:], gid[:, i:i + 1], None, ALU.is_le)
                    v.tensor_scalar(hit[:, 1, i, :], pairsf[:], gid[:, i:i + 1], None, ALU.is_le)
                v.drain()
                v.tensor_reduce(tables[:], hit[:], AX.X, ALU.add)
                v.drain()
                v.scalar_tensor_tensor(tables[:, 0, :], tables[:, 0, :], 1.0, gid[:], ALU.add, ALU.add)
                v.drain()
                v.tensor_copy(tablesi[:], tables[:]).then_inc(ended, 1)
                v.wait_ge(tab3, 48)
                v.tensor_scalar(k.pair_node[:], blocks[:], float(P), None, ALU.mult)
                v.tensor_tensor(k.pair_group[:], k.pair_group[:], k.pair_block[:], ALU.subtract)


def load_weights(nc, name, pairs):
    with ExitStack() as c:
        got = c.enter_context(nc.semaphore(name))
        with nc.Block() as block:
            @block.sync
            def _(sp):
                for dst, src in pairs:
                    sp.dma_start(dst, src).then_inc(got, 16)
                sp.wait_ge(got, 16 * len(pairs))


def rows_of(w):
    return w.rearrange("(k p) n -> p k n", p=P)


def attention_table(nc, z, k, S, kt):
    NB = z.NB
    A2 = 2 * HEADS
    with ExitStack() as c:
        sem = lambda n: c.enter_context(nc.semaphore("at_" + n))
        sb = lambda n, s, d=F32: c.enter_context(nc.sbuf_tensor("at_" + n, s, d))
        w = sb("w", [P, KC, C])
        wt = sb("wt", [P, KC, C])
        attn = sb("attn", [P, 2, KC])
        lr = sb("lr", [P, KC, A2])
        waug = sb("waug", [P, KC, C + A2])
        wk = sb("wk", [P, KC, C])
        st = sb("st", [P, 2, C])
        xt = sb("xt", [P, 2, C])
        row = sb("row", [P, 2, HROW])
        psT = c.enter_context(nc.psum_tensor("at_psT", [P, 2, 512], F32))
        psH = c.enter_context(nc.psum_tensor("at_psH", [P, 2, 512], F32))
        psK = c.enter_context(nc.psum_tensor("at_psK", [P, 2, 512], F32))
        load_weights(nc, "at_load", [
            (w[:], rows_of(S["L0_gnn_W"])), (wt[:], rows_of(S["L0_gnn_W_t"])),
            (attn[:, 0, :], S["L0_gnn_attn_l"]),
            (attn[:, 1, :], S["L0_gnn_attn_r"]),
            (wk[:], rows_of(S["L0_mix_Wqkv"])[:, :, C:2 * C])])
        spread, folded = sem("spread"), sem("folded")
        with nc.Block() as block:
            @block.vector
            def _(v):
                v.memset(lr[:], 0.0)
                v.memset(row[:], 1.0)
                v.drain()
                for kc in range(KC):
                    for q in range(P // D):
                        h = kc * (P // D) + q
                        for s in range(2):
                            v.tensor_copy(lr[q * D:(q + 1) * D, kc, s * HEADS + h:s * HEADS + h + 1],
                                          attn[q * D:(q + 1) * D, s, kc:kc + 1])
                v.drain()
                v.tensor_copy(waug[:, :, 0:C], w[:]).then_inc(spread, 1)
                v.wait_ge(folded, 1)
                v.tensor_copy(waug[:, :, C:C + A2], psH[:, :, 0:A2])

            @block.tensor
            def _(pe):
                pe.wait_ge(spread, 1)
                for m in range(KC):
                    for kc in range(KC):
                        mm = pe.matmul(psH[:, m, 0:A2], wt[:, kc, m * P:(m + 1) * P], lr[:, kc, :],
                                       start=kc == 0, stop=kc == KC - 1)
                mm.then_inc(folded, 1)
        staged, turned, back, made, taken, keys = (sem(x) for x in
            ("staged", "turned", "back", "made", "taken", "keys"))
        stored = [sem("stored0"), sem("stored1")]
        with nc.Block() as block:
            @block.scalar
            def _(act):
                act.sem_inc(staged, 2)
                act.sem_inc(keys, 2)

                def body(b, u, i, last):
                    act.wait_ge(turned, b + 1)
                    act.nop()
                    act.copy(st[:, u, :], k.xa[:, ds(b * C, C)]).then_inc(staged, 1)
                    act.wait_ge(made, b + 3)
                    act.nop()
                    for kc in range(KC):
                        o = act.copy(kt[:, ds(b * P + kc * NB * P, P)], psK[:, u, kc * P:(kc + 1) * P])
                    o.then_inc(keys, 1)
                two_at_a_time(act, NB, body)

            @block.tensor
            def _(pe):
                pe.sem_inc(turned, 2)
                pe.sem_inc(made, 2)

                def body(b, u, i, last):
                    pe.wait_ge(staged, b + 3)
                    pe.wait_ge(back, b + 1)
                    for kc in range(KC):
                        t = pe.transpose(psT[:, u, kc * P:(kc + 1) * P], st[:, u, kc * P:(kc + 1) * P],
                                         k.ident[:])
                    t.then_inc(turned, 1)
                    pe.wait_ge(back, b + 3)
                    pe.wait_ge(taken, b + 1)
                    pe.wait_ge(keys, b + 1)
                    for kc in range(KC):
                        pe.matmul(psH[:, u, 0:C + A2], xt[:, u, kc * P:(kc + 1) * P], waug[:, kc, :],
                                  start=kc == 0, stop=kc == KC - 1)
                    for m in range(KC):
                        for kc in range(KC):
                            t = pe.matmul(psK[:, u, m * P:(m + 1) * P], wk[:, kc, m * P:(m + 1) * P],
                                          xt[:, u, kc * P:(kc + 1) * P], start=kc == 0, stop=kc == KC - 1)
                    t.then_inc(made, 1)
                two_at_a_time(pe, NB, body)

            @block.vector
            def _(v):
                v.sem_inc(back, 2)
                v.sem_inc(taken, 2)

                def body(b, u, i, last):
                    v.wait_ge(turned, b + 3)
                    v.wait_ge(made, b + 1)
                    v.tensor_copy(xt[:, u, :], psT[:, u, 0:C]).then_inc(back, 1)
                    if not (isinstance(i, int) and i == 0):
                        v.wait_ge(stored[u], i * 16)
                    v.wait_ge(made, b + 3)
                    v.tensor_copy(row[:, u, 0:HEADS * HD].rearrange("p (h d) -> p h d", d=HD)[:, :, 0:D],
                                  psH[:, u, 0:C].rearrange("p (h d) -> p h d", d=D))
                    v.tensor_copy(k.a2[:, ds(b * HEADS, HEADS)], psH[:, u, C + HEADS:C + A2])
                    v.tensor_copy(row[:, u, HEADS * HD:HROW], psH[:, u, C:C + HEADS]).then_inc(taken, 1)
                two_at_a_time(v, NB, body, peel=True)

            @block.sync
            def _(sp):
                def body(b, u, i, last):
                    sp.wait_ge(taken, b + 3)
                    sp.dma_start(k.h_dram[ds(b * P, P), :], row[:, u, :]).then_inc(stored[u], 16)
                two_at_a_time(sp, NB, body)
                sp.wait_ge(stored[0], 16 * ((NB + 1) // 2))
                sp.wait_ge(stored[1], 16 * (NB // 2))


def keys_to_context(nc, z, k, S, kt, wqc):
    NB, N = z.NB, z.N
    NP = NB * P
    with ExitStack() as c:
        sem = lambda n: c.enter_context(nc.semaphore("kc_" + n))
        sb = lambda n, s, d=F32: c.enter_context(nc.sbuf_tensor("kc_" + n, s, d))
        wqt = sb("wqt", [P, KC, C])
        wv = sb("wv", [P, KC, C])
        top = sb("top", [P, KC])
        total = sb("total", [P, KC])
        st = sb("st", [P, 2, C])
        ek = sb("ek", [P, 2, C])
        zero = sb("zero", [P, C])
        cs = sb("cs", [P, KC, C])
        ct = sb("ct", [P, KC, C])
        cbd = sb("cbd", [P, KC, C])
        psT = c.enter_context(nc.psum_tensor("kc_psT", [P, 2, 512], F32))
        psC = c.enter_context(nc.psum_tensor("kc_psC", [P, 2, 512], F32))
        load_weights(nc, "kc_load", [(wqt[:], rows_of(S["L0_mix_Wq_t"])),
                                     (wv[:], rows_of(S["L0_mix_Wqkv"])[:, :, 2 * C:3 * C])])
        topped, powered = sem("topped"), sem("powered")
        with nc.Block() as block:
            @block.vector
            def _(v):
                v.memset(zero[:], 0.0)
                v.memset(cbd[:], 0.0)
                for kc in range(KC):
                    v.tensor_reduce(top[:, kc:kc + 1], kt[:, kc * NP:kc * NP + N], AX.X, ALU.max)
                v.drain()
                v.tensor_scalar(top[:], top[:], -1.0, None, ALU.mult).then_inc(topped, 1)
                if NP > N:
                    for kc in range(KC):
                        v.memset(kt[:, kc * NP + N:(kc + 1) * NP], 0.0)
                v.wait_ge(powered, 1)
                v.reciprocal(total[:], total[:])

            @block.scalar
            def _(act):
                act.wait_ge(topped, 1)
                for kc in range(KC):
                    o = act.activation(kt[:, kc * NP:kc * NP + N], kt[:, kc * NP:kc * NP + N], ACT.Exp,
                                       bias=top[:, kc:kc + 1], accum_out=total[:, kc:kc + 1])
                o.then_inc(powered, 1)
        staged, turned, back, summed = (sem(x) for x in ("staged", "turned", "back", "summed"))
        with nc.Block() as block:
            @block.scalar
            def _(act):
                act.sem_inc(staged, 2)

                def body(b, u, i, last):
                    act.wait_ge(turned, b + 1)
                    act.nop()
                    for kc in range(KC):
                        o = act.copy(st[:, u, kc * P:(kc + 1) * P], kt[:, ds(b * P + kc * NP, P)])
                    o.then_inc(staged, 1)
                two_at_a_time(act, NB, body)

            @block.tensor
            def _(pe):
                pe.sem_inc(turned, 2)
                pe.sem_inc(summed, 2)
                for kc in range(KC):
                    pe.matmul(psC[:, kc, 0:C], zero[:, 0:P], zero[:], start=True, stop=False)

                def body(b, u, i, last):
                    pe.wait_ge(staged, b + 3)
                    pe.wait_ge(back, b + 1)
                    for kc in range(KC):
                        t = pe.transpose(psT[:, u, kc * P:(kc + 1) * P], st[:, u, kc * P:(kc + 1) * P],
                                         k.ident[:])
                    t.then_inc(turned, 1)
                    pe.wait_ge(back, b + 3)
                    for kc in range(KC):
                        t = pe.matmul(psC[:, kc, 0:C], ek[:, u, kc * P:(kc + 1) * P],
                                      k.xa[:, ds(b * C, C)], start=False, stop=last)
                    t.then_inc(summed, 1)
                two_at_a_time(pe, NB, body)

            @block.vector
            def _(v):
                v.sem_inc(back, 2)

                def body(b, u, i, last):
                    v.wait_ge(turned, b + 3)
                    v.wait_ge(summed, b + 1)
                    v.tensor_copy(ek[:, u, :], psT[:, u, 0:C]).then_inc(back, 1)
                two_at_a_time(v, NB, body)
        step, done = sem("step"), sem("done")
        with nc.Block() as block:
            @block.vector
            def _(v):
                for kc in range(KC):
                    o = v.tensor_scalar(cs[:, kc, :], psC[:, kc, 0:C], total[:, kc:kc + 1], None, ALU.mult)
                o.then_inc(step, 1)
                v.wait_ge(done, 1)
                v.tensor_copy(ct[:], psT[:, :, 0:C]).then_inc(step, 1)
                v.wait_ge(done, 2)
                for kc in range(KC):
                    for q in range(P // D):
                        a = kc * P + q * D
                        o = v.tensor_copy(cbd[q * D:(q + 1) * D, kc, a:a + D],
                                          psC[q * D:(q + 1) * D, kc, a:a + D])
                o.then_inc(step, 1)
                v.wait_ge(done, 3)
                v.tensor_copy(wqc[:], psT[:, :, 0:C])

            @block.tensor
            def _(pe):
                pe.wait_ge(step, 1)
                for m in range(KC):
                    for kc in range(KC):
                        t = pe.transpose(psT[:, m, kc * P:(kc + 1) * P], cs[:, kc, m * P:(m + 1) * P],
                                         k.ident[:])
                t.then_inc(done, 1)
                pe.wait_ge(step, 2)
                for m in range(KC):
                    for kc in range(KC):
                        t = pe.matmul(psC[:, m, 0:C], ct[:, kc, m * P:(m + 1) * P], wv[:, kc, :],
                                      start=kc == 0, stop=kc == KC - 1)
                t.then_inc(done, 1)
                pe.wait_ge(step, 3)
                for m in range(KC):
                    for kc in range(KC):
                        t = pe.matmul(psT[:, m, 0:C], wqt[:, kc, m * P:(m + 1) * P], cbd[:, kc, :],
                                      start=kc == 0, stop=kc == KC - 1)
                t.then_inc(done, 1)


def mix_out(nc, z, k, S, wqc, mean, rstd):
    NB = z.NB
    GH = S["L0_mix_Wg1"].shape[1]
    with ExitStack() as c:
        sem = lambda n: c.enter_context(nc.semaphore("mo_" + n))
        sb = lambda n, s, d=F32: c.enter_context(nc.sbuf_tensor("mo_" + n, s, d))
        g1 = sb("g1", [P, KC, GH])
        g2 = sb("g2", [GH, C])
        wp = sb("wp", [P, KC, C])
        cols = sb("cols", [P, 3, KC])
        bg1 = sb("bg1", [GH, 1])
        bias = sb("bias", [1, 2, C])
        st = sb("st", [P, 2, 2 * C])
        xt = sb("xt", [P, 2, 2 * C])
        hid = sb("hid", [GH, 2, P])
        gate = sb("gate", [P, 2, C])
        prod = sb("prod", [P, 2, C])
        psT = c.enter_context(nc.psum_tensor("mo_psT", [P, 2, 512], F32))
        psG = c.enter_context(nc.psum_tensor("mo_psG", [GH, 2, 512], F32))
        psU = c.enter_context(nc.psum_tensor("mo_psU", [P, 2, 512], F32))
        psM = c.enter_context(nc.psum_tensor("mo_psM", [P, 2, 512], F32))
        load_weights(nc, "mo_load", [
            (g1[:], rows_of(S["L0_mix_Wg1"])), (g2[:], S["L0_mix_Wg2"]), (wp[:], rows_of(S["L0_mix_Wproj"])),
            (cols[:, 0, :], S["L0_mix_ln_g"]), (cols[:, 1, :], S["L0_mix_ln_b"]),
            (cols[:, 2, :], S["L0_mix_bg2"]),
            (bg1[:], S["L0_mix_bg1"].rearrange("(p o) -> p o", o=1)),
            (bias[:, 0, :], S["L0_mix_bproj"].rearrange("(o n) -> o n", o=1)),
            (bias[:, 1, :], S["L0_gnn_bias"].rearrange("(o n) -> o n", o=1))])
        staged, normed, turned, back, hidden, gelu, gated, sig, timed, projected, added = (
            sem(x) for x in ("staged", "normed", "turned", "back", "hidden", "gelu", "gated", "sig",
                             "timed", "projected", "added"))
        with nc.Block() as block:
            @block.scalar
            def _(act):
                for s in (staged, back, gelu, sig):
                    act.sem_inc(s, 2)

                def body(b, u, i, last):
                    act.wait_ge(turned, b + 1)
                    act.nop()
                    act.copy(st[:, u, 0:C], k.xa[:, ds(b * C, C)]).then_inc(staged, 1)
                    act.wait_ge(turned, b + 3)
                    act.wait_ge(gated, b + 1)
                    act.nop()
                    act.copy(xt[:, u, 0:C], psT[:, u, 0:C])
                    for kc in range(KC):
                        o = act.activation(xt[:, u, C + kc * P:C + (kc + 1) * P],
                                           psT[:, u, C + kc * P:C + (kc + 1) * P], ACT.Identity,
                                           bias=cols[:, 1, kc:kc + 1], scale=cols[:, 0, kc:kc + 1])
                    o.then_inc(back, 1)
                    act.wait_ge(hidden, b + 3)
                    act.nop()
                    act.activation(hid[:, u, :], psG[:, u, 0:P], ACT.Gelu, bias=bg1[:, 0:1]).then_inc(gelu, 1)
                    act.wait_ge(gated, b + 3)
                    act.wait_ge(timed, b + 1)
                    act.nop()
                    for kc in range(KC):
                        o = act.activation(gate[:, u, kc * P:(kc + 1) * P],
                                           psU[:, u, C + kc * P:C + (kc + 1) * P], ACT.Sigmoid,
                                           bias=cols[:, 2, kc:kc + 1])
                    o.then_inc(sig, 1)
                two_at_a_time(act, NB, body)

            @block.vector
            def _(v):
                for s in (normed, timed, added):
                    v.sem_inc(s, 2)

                def body(b, u, i, last):
                    v.wait_ge(turned, b + 1)
                    v.tensor_scalar(st[:, u, C:2 * C], k.xa[:, ds(b * C, C)], mean[:, ds(b, 1)],
                                    rstd[:, ds(b, 1)], ALU.subtract, ALU.mult).then_inc(normed, 1)
                    v.wait_ge(sig, b + 3)
                    v.wait_ge(projected, b + 1)
                    v.tensor_tensor(prod[:, u, :], psU[:, u, 0:C], gate[:, u, :], ALU.mult).then_inc(timed, 1)
                    v.wait_ge(projected, b + 3)
                    v.tensor_tensor(k.xb[:, ds(b * C, C)], k.xb[:, ds(b * C, C)], psM[:, u, 0:C],
                                    ALU.add).then_inc(added, 1)
                two_at_a_time(v, NB, body)

            @block.tensor
            def _(pe):
                for s in (turned, hidden, gated, projected):
                    pe.sem_inc(s, 2)

                def body(b, u, i, last):
                    pe.wait_ge(staged, b + 3)
                    pe.wait_ge(normed, b + 3)
                    pe.wait_ge(back, b + 1)
                    for q in range(2 * KC):
                        t = pe.transpose(psT[:, u, q * P:(q + 1) * P], st[:, u, q * P:(q + 1) * P], k.ident[:])
                    t.then_inc(turned, 1)
                    pe.wait_ge(back, b + 3)
                    pe.wait_ge(gelu, b + 1)
                    for kc in range(KC):
                        t = pe.matmul(psG[:, u, 0:P], g1[:, kc, :], xt[:, u, C + kc * P:C + (kc + 1) * P],
                                      start=kc == 0, stop=kc == KC - 1)
                    t.then_inc(hidden, 1)
                    pe.wait_ge(timed, b + 1)
                    for m in range(KC):
                        for kc in range(KC):
                            pe.matmul(psU[:, u, m * P:(m + 1) * P], wqc[:, kc, m * P:(m + 1) * P],
                                      xt[:, u, kc * P:(kc + 1) * P], start=kc == 0, stop=kc == KC - 1)
                    pe.wait_ge(gelu, b + 3)
                    for m in range(KC):
                        t = pe.matmul(psU[:, u, C + m * P:C + (m + 1) * P], g2[:, m * P:(m + 1) * P],
                                      hid[:, u, :], start=True, stop=True)
                    t.then_inc(gated, 1)
                    pe.wait_ge(timed, b + 3)
                    pe.wait_ge(added, b + 1)
                    for kc in range(KC):
                        pe.matmul(psM[:, u, 0:C], prod[:, u, kc * P:(kc + 1) * P], wp[:, kc, :],
                                  start=kc == 0, stop=False)
                    for r in range(2):
                        t = pe.matmul(psM[:, u, 0:C], k.ones[0:1, :], bias[:, r, :], start=False, stop=r == 1)
                    t.then_inc(projected, 1)
                two_at_a_time(pe, NB, body)


def gather_groups(nc, z, block, k, table, rows, ring, idx, landed, gathered, ready, go, freed):
    turns = z.NGT // R

    @block.sync
    def _(sp):
        def load(g, s):
            sp.dma_start(idx[:, s, :], rows[:, ds(g * G, G)]).then_inc(landed[s], 16)
        for s in range(R):
            load(s, s)
        with sp.Fori(1, turns) as i:
            for s in range(R):
                pair = sp.value_load(k.last_pair[0:1, ds((i - 1) * R + s, 1)], min_val=1,
                                     max_val=z.T)
                sp.wait_ge(freed, pair + BASE)
                load(i * R + s, s)
        sp.wait_ge(ready, z.NGT)

    @block.gpsimd
    def _(p):
        def gather(i, s):
            p.wait_ge(landed[s], (i + 1) * 16)
            p.sem_inc(go, 1)
            for j in range(G):
                p.indirect_dma_start(ring[:, s * G + j, :], None, table,
                                     bass.IndirectOffsetOnAxis(ap=idx[:, s, j:j + 1], axis=0)
                                     ).then_inc(gathered[s], 16)

        def report(i, s):
            p.wait_ge(gathered[s], (i + 1) * 16 * G)
            p.sem_inc(ready, 1)
        gather(0, 0)
        for s in range(1, R):
            gather(0, s)
            report(0, s - 1)
        with p.Fori(1, turns) as i:
            for s in range(R):
                gather(i, s)
                if s:
                    report(i, s - 1)
                else:
                    report(i - 1, R - 1)
        report(turns - 1, R - 1)


def pair_turns(eng, z, step):
    for t in range(U):
        step(t, t)
    with eng.Fori(1, z.T // U) as i:
        for u in range(U):
            step(i * U + u, u)


def group_of(eng, z, k, t):
    return eng.value_load(k.pair_group[0:1, ds(t, 1)], min_val=0, max_val=z.NGT - 1)


def block_of(eng, z, k, t):
    return eng.value_load(k.pair_block[0:1, ds(t, 1)], min_val=0, max_val=z.NB - 1)


def start_at(eng, value, *sems):
    for s in sems:
        eng.sem_inc(s, value)


def pair_one_hot(v, k, onehot, t, g):
    return v.scalar_tensor_tensor(onehot, k.dstf[:, ds(g * G, G)].unsqueeze(2).to_broadcast([P, G, P]),
                                  k.pair_node[:, ds(t, 1)],
                                  k.iota[:].unsqueeze(1).to_broadcast([P, G, P]), ALU.subtract, ALU.is_equal)


def attention(nc, z, k, S):
    NB = z.NB
    with ExitStack() as c:
        sem = lambda n: c.enter_context(nc.semaphore("ga_" + n))
        sb = lambda n, s, d=F32: c.enter_context(nc.sbuf_tensor("ga_" + n, s, d))
        ring = sb("ring", [P, R * G, HROW])
        idx = sb("idx", [P, R, G], I32)
        onehot = sb("onehot", [P, U, G, P])
        onehot_t = sb("onehot_t", [P, G, P])
        sta = sb("sta", [P, G, HEADS])
        stb = sb("stb", [P, G, HEADS])
        starts = sb("starts", [G * HEADS, P])
        scan = sb("scan", [G * HEADS, P])
        runs = sb("runs", [P, 2 * G, HEADS + 1])
        miss = sb("miss", [P, G])
        cand = sb("cand", [P, G, HEADS])
        red = sb("red", [P, HEADS])
        tot = sb("tot", [P, HEADS])
        log = sb("log", [P, HEADS])
        old = sb("old", [P, HEADS])
        look = sb("look", [P, NB, 2 * HEADS])
        esum = sb("esum", [P, G, HEADS])
        elog = sb("elog", [P, G, HEADS])
        arg = sb("arg", [P, G + 1, HEADS])
        w = sb("w", [P, U, G + 1, HEADS])
        msg = sb("msg", [P, 2 * G, MROW])
        acc = sb("acc", [P, NB * MROW])
        rden = sb("rden", [P, NB, HEADS])
        psI = c.enter_context(nc.psum_tensor("ga_psI", [P, 512], F32))
        psQ = c.enter_context(nc.psum_tensor("ga_psQ", [P, 512], F32))
        psT = c.enter_context(nc.psum_tensor("ga_psT", [P, G, P], F32))
        psX = c.enter_context(nc.psum_tensor("ga_psX", [P, 512], F32))
        psL = c.enter_context(nc.psum_tensor("ga_psL", [P, 512], F32))
        psS = c.enter_context(nc.psum_tensor("ga_psS", [P, 512], F32))
        landed = [sem(f"landed{s}") for s in range(R)]
        gathered = [sem(f"gathered{s}") for s in range(R)]
        ready, go, pe_go, hot, hot_t, turned = (
            sem(x) for x in ("ready", "go", "pe_go", "hot", "hot_t", "turned"))
        m_staged, m_turned, m_starts, m_scan, m_back, m_runs = (
            sem("m_" + x) for x in ("staged", "turned", "starts", "scan", "back", "runs"))
        maxed, shifts, looked, args, weights, messages, summed, added = (
            sem(x) for x in ("maxed", "shifts", "looked", "args", "weights", "messages", "summed", "added"))
        GH = G * HEADS
        psX_v = psX[:, 0:G * (HEADS + 1)].rearrange("p (j h) -> p j h", j=G)
        psL_v = psL[:, 0:G * 2 * HEADS].rearrange("p (j h) -> p j h", j=G)
        psQ_v = psQ[:, 0:GH].rearrange("p (j h) -> p j h", j=G)
        hd = HEADS * HD
        look_f = look[:].rearrange("p b h -> p (b h)")
        with nc.Block() as block:
            @block.vector
            def _(v):
                v.memset(acc[:], 0.0)
                v.memset(look[:, :, HEADS:], -BIG)
                v.tensor_copy(look[:, :, 0:HEADS], k.a2[:].rearrange("p (b h) -> p b h", h=HEADS))
        with nc.Block() as block:
            gather_groups(nc, z, block, k, k.h_dram, S["src"], ring, idx, landed, gathered, ready, go, messages)

            def slot(g):
                return (g % R) * G

            @block.scalar
            def _(act):
                start_at(act, BASE, m_staged, m_starts, hot_t, weights)

                def stage(t):
                    g = group_of(act, z, k, t)
                    act.wait_ge(ready, g + 1)
                    act.wait_ge(m_turned, t + 3)
                    act.nop()
                    act.copy(sta[:], ring[:, ds(slot(g), G), hd:HROW])
                    act.copy(stb[:], k.start[:, ds(g * G, G)].unsqueeze(2).to_broadcast([P, G, HEADS])
                             ).then_inc(m_staged, 1)

                def spread_starts(t):
                    g = group_of(act, z, k, t)
                    act.wait_ge(maxed, t + 2)
                    act.wait_ge(m_turned, t + 4)
                    act.nop()
                    act.copy(starts[:], psI[0:GH, P:2 * P])
                    act.copy(runs[:, ds((t % 2) * G, G), HEADS:HEADS + 1],
                             k.last[:, ds(g * G, G)].unsqueeze(2)).then_inc(m_starts, 1)

                def turn_one_hot(t):
                    act.wait_ge(turned, t + 4)
                    act.wait_ge(looked, t + 3)
                    act.nop()
                    for q in range(G // 4):
                        o = act.copy(onehot_t[:, 4 * q:4 * q + 4, :], psT[:, 4 * q:4 * q + 4, :])
                    o.then_inc(hot_t, 1)

                def power(t, u):
                    act.wait_ge(args, t + 4)
                    act.wait_ge(added, t + 1)
                    act.nop()
                    act.activation(w[:, u, :, :], arg[:], ACT.Exp).then_inc(weights, 1)

                def step(t, u):
                    stage(t + 2)
                    turn_one_hot(t + 1)
                    spread_starts(t + 2)
                    power(t + 1, (u + 1) % U)
                stage(0)
                spread_starts(0)
                stage(1)
                turn_one_hot(0)
                spread_starts(1)
                power(0, 0)
                pair_turns(act, z, step)

            @block.tensor
            def _(pe):
                start_at(pe, BASE, m_turned, m_back, turned, maxed, looked, summed)

                def turn_runs(t):
                    pe.wait_ge(m_staged, t + 4)
                    pe.wait_ge(m_scan, t + 3)
                    pe.sem_inc(pe_go, 1)
                    pe.transpose(psI[0:GH, 0:P], sta[:].rearrange("p j h -> p (j h)"), k.ident[:])
                    pe.transpose(psI[0:GH, P:2 * P], stb[:].rearrange("p j h -> p (j h)"), k.ident[:]
                                 ).then_inc(m_turned, 1)

                def turn_back(t):
                    pe.wait_ge(m_scan, t + 4)
                    pe.wait_ge(m_runs, t + 3)
                    pe.sem_inc(pe_go, 1)
                    pe.transpose(psQ[:, 0:GH], scan[:], k.ident[0:GH, 0:GH]).then_inc(m_back, 1)

                def turn(t, u):
                    pe.wait_ge(hot, t + 4)
                    pe.wait_ge(hot_t, t + 3)
                    for j in range(G):
                        o = pe.transpose(psT[:, j, :], onehot[:, u, j, :], k.ident[:])
                    o.then_inc(turned, 1)

                def maxima(t, u):
                    pe.wait_ge(m_runs, t + 4)
                    pe.wait_ge(m_starts, t + 4)
                    pe.wait_ge(shifts, t + 3)
                    for j in range(G):
                        o = pe.matmul(psX_v[:, j, :], onehot[:, u, j, :], runs[:, ds((t % 2) * G + j, 1), :],
                                      start=True, stop=True)
                    o.then_inc(maxed, 1)

                def look_up(t):
                    b = block_of(pe, z, k, t)
                    pe.wait_ge(shifts, t + 4)
                    pe.wait_ge(hot_t, t + 4)
                    pe.wait_ge(args, t + 3)
                    for j in range(G):
                        o = pe.matmul(psL_v[:, j, :], onehot_t[:, j, :], look_f[:, ds(b * 2 * HEADS, 2 * HEADS)],
                                      start=True, stop=True)
                    o.then_inc(looked, 1)

                def sum_up(t, u):
                    pe.wait_ge(messages, t + 4)
                    pe.wait_ge(added, t + 3)
                    for j in range(G):
                        o = pe.matmul(psS[:, 0:MROW], onehot[:, u, j, :], msg[:, ds((t % 2) * G + j, 1), :],
                                      start=j == 0, stop=j == G - 1)
                    o.then_inc(summed, 1)

                def step(t, u):
                    turn(t + 1, (u + 1) % U)
                    maxima(t + 1, (u + 1) % U)
                    turn_runs(t + 2)
                    look_up(t + 1)
                    turn_back(t + 2)
                    sum_up(t, u)
                turn_runs(0)
                turn_back(0)
                turn(0, 0)
                maxima(0, 0)
                turn_runs(1)
                look_up(0)
                turn_back(1)
                pair_turns(pe, z, step)

            @block.vector
            def _(v):
                start_at(v, BASE, m_scan, m_runs, hot, shifts, args, messages, added)

                def scan_runs(t):
                    v.wait_ge(m_starts, t + 4)
                    v.wait_ge(m_back, t + 3)
                    v.tensor_tensor_scan(scan[:], starts[:], psI[0:GH, 0:P], -BIG, ALU.add, ALU.max
                                         ).then_inc(m_scan, 1)

                def keep_ends(t):
                    g = group_of(v, z, k, t)
                    v.wait_ge(m_back, t + 4)
                    v.tensor_tensor(runs[:, ds((t % 2) * G, G), 0:HEADS], psQ_v,
                                    k.last[:, ds(g * G, G)].unsqueeze(2).to_broadcast([P, G, HEADS]),
                                    ALU.mult).then_inc(m_runs, 1)

                def mark(t, u):
                    g = group_of(v, z, k, t)
                    v.wait_ge(summed, t + 1)
                    pair_one_hot(v, k, onehot[:, u, :, :], t, g).then_inc(hot, 1)

                def shift(t):
                    b = block_of(v, z, k, t)
                    shifts_b = look_f[:, ds(b * 2 * HEADS + HEADS, HEADS)]
                    v.tensor_copy(old[:], shifts_b)
                    v.wait_ge(maxed, t + 4)
                    v.tensor_scalar(miss[:], psX_v[:, :, HEADS], -1.0, BIG, ALU.add, ALU.mult)
                    v.drain()
                    v.tensor_tensor(cand[:], psX_v[:, :, 0:HEADS],
                                    miss[:].unsqueeze(2).to_broadcast([P, G, HEADS]), ALU.add)
                    v.drain()
                    v.tensor_reduce(red[:], cand[:].rearrange("p j h -> p h j"), AX.X, ALU.max)
                    v.drain()
                    v.tensor_tensor(tot[:], red[:], look_f[:, ds(b * 2 * HEADS, HEADS)], ALU.add)
                    v.drain()
                    v.scalar_tensor_tensor(log[:], tot[:], SLOPE, tot[:], ALU.mult, ALU.max)
                    v.drain()
                    v.tensor_tensor(shifts_b, log[:], old[:], ALU.max).then_inc(shifts, 1)
                    v.drain()
                    v.tensor_tensor(arg[:, G, :], old[:], shifts_b, ALU.subtract)

                def arguments(t):
                    g = group_of(v, z, k, t)
                    v.wait_ge(looked, t + 4)
                    v.tensor_tensor(esum[:], ring[:, ds(slot(g), G), hd:HROW], psL_v[:, :, 0:HEADS], ALU.add)
                    v.drain()
                    v.scalar_tensor_tensor(elog[:], esum[:], SLOPE, esum[:], ALU.mult, ALU.max)
                    v.drain()
                    v.tensor_tensor(arg[:, 0:G, :], elog[:], psL_v[:, :, HEADS:], ALU.subtract
                                    ).then_inc(args, 1)

                def weigh(t, u):
                    g = group_of(v, z, k, t)
                    m = (t % 2) * G
                    v.wait_ge(summed, t + 2)
                    v.tensor_tensor(msg[:, ds(m, G), hd:MROW],
                                    k.iota[:, 0:REL].unsqueeze(1).to_broadcast([P, G, REL]),
                                    k.etf[:, ds(g * G, G)].unsqueeze(2).to_broadcast([P, G, REL]), ALU.is_equal)
                    v.wait_ge(weights, t + 4)
                    v.scalar_tensor_tensor(
                        msg[:, ds(m, G), 0:hd].rearrange("p j (h d) -> p j h d", d=HD),
                        w[:, u, 0:G, :].unsqueeze(3).to_broadcast([P, G, HEADS, HD]), 1.0,
                        ring[:, ds(slot(g), G), 0:hd].rearrange("p j (h d) -> p j h d", d=HD),
                        ALU.min, ALU.mult).then_inc(messages, 1)

                def add_up(t, u):
                    b = block_of(v, z, k, t)
                    heads = acc[:, ds(b * MROW, hd)].rearrange("p (h d) -> p h d", d=HD)
                    v.tensor_tensor(heads, heads, w[:, u, G, :].unsqueeze(2).to_broadcast([P, HEADS, HD]),
                                    ALU.mult)
                    v.drain()
                    v.wait_ge(summed, t + 4)
                    v.tensor_tensor(acc[:, ds(b * MROW, MROW)], acc[:, ds(b * MROW, MROW)], psS[:, 0:MROW],
                                    ALU.add).then_inc(added, 1)
                    v.drain()

                def step(t, u):
                    mark(t + 1, (u + 1) % U)
                    weigh(t, u)
                    if not (isinstance(t, int) and t == 0):
                        add_up(t - 1, (u - 1) % U)
                    scan_runs(t + 2)
                    shift(t + 1)
                    arguments(t + 1)
                    keep_ends(t + 2)
                scan_runs(0)
                keep_ends(0)
                mark(0, 0)
                scan_runs(1)
                shift(0)
                arguments(0)
                keep_ends(1)
                pair_turns(v, z, step)
                add_up(z.T - 1, U - 1)
        with nc.Block() as block:
            @block.vector
            def _(v):
                rows = acc[:].rearrange("p (b r) -> p b r", r=MROW)
                v.tensor_scalar(rden[:], rows[:, :, D:hd:HD], 1e-30, None, ALU.max)
                v.tensor_scalar(rows[:, :, hd:MROW], rows[:, :, hd:MROW], 1.0, None, ALU.max)
                v.drain()
                v.reciprocal(rden[:], rden[:])
                v.reciprocal(k.icnt[:].rearrange("p (b r) -> p b r", r=REL), rows[:, :, hd:MROW])
                v.drain()
                for h in range(HEADS):
                    v.tensor_tensor(rows[:, :, h * HD:h * HD + D], rows[:, :, h * HD:h * HD + D],
                                    rden[:, :, h:h + 1].to_broadcast([P, NB, D]), ALU.mult)
                v.drain()
                xb = k.xb[:].rearrange("p (b c) -> p b c", c=C)
                for h in range(HEADS):
                    v.tensor_tensor(xb[:, :, h * D:(h + 1) * D], xb[:, :, h * D:(h + 1) * D],
                                    rows[:, :, h * HD:h * HD + D], ALU.add)


def relations(nc, z, k, S):
    with ExitStack() as c:
        sem = lambda n: c.enter_context(nc.semaphore("rg_" + n))
        sb = lambda n, s, d=F32: c.enter_context(nc.sbuf_tensor("rg_" + n, s, d))
        ring = sb("ring", [P, R * G, C])
        idx = sb("idx", [P, R, G], I32)
        onehot = sb("onehot", [P, U, G, P])
        onehot_t = sb("onehot_t", [P, U, G, P])
        rel = sb("rel", [P, G, REL])
        picked = sb("picked", [P, G, REL])
        w = sb("w", [P, G])
        psT = c.enter_context(nc.psum_tensor("rg_psT", [P, G, P], F32))
        psL = c.enter_context(nc.psum_tensor("rg_psL", [P, 512], F32))
        psS = c.enter_context(nc.psum_tensor("rg_psS", [P, 512], F32))
        landed = [sem(f"landed{s}") for s in range(R)]
        gathered = [sem(f"gathered{s}") for s in range(R)]
        ready, go, hot, hot_t, turned, looked, weighted, summed, added = (
            sem(x) for x in ("ready", "go", "hot", "hot_t", "turned", "looked", "weighted", "summed", "added"))
        psL_v = psL[:, 0:G * REL].rearrange("p (j r) -> p j r", j=G)
        with nc.Block() as block:
            gather_groups(nc, z, block, k, k.y_dram, k.src_rel, ring, idx, landed, gathered, ready, go, summed)

            @block.scalar
            def _(act):
                start_at(act, BASE, hot_t)

                def turn_one_hot(t, u):
                    act.wait_ge(turned, t + 4)
                    act.wait_ge(looked, t + 1)
                    act.nop()
                    for q in range(G // 4):
                        o = act.copy(onehot_t[:, u, 4 * q:4 * q + 4, :], psT[:, 4 * q:4 * q + 4, :])
                    o.then_inc(hot_t, 1)
                turn_one_hot(0, 0)
                turn_one_hot(1, 1)
                pair_turns(act, z, lambda t, u: turn_one_hot(t + 2, (u + 2) % U))

            @block.tensor
            def _(pe):
                start_at(pe, BASE, turned, looked, summed)

                def turn(t, u):
                    pe.wait_ge(hot, t + 4)
                    pe.wait_ge(hot_t, t + 3)
                    for j in range(G):
                        o = pe.transpose(psT[:, j, :], onehot[:, u, j, :], k.ident[:])
                    o.then_inc(turned, 1)

                def look_up(t, u):
                    b = block_of(pe, z, k, t)
                    pe.wait_ge(hot_t, t + 4)
                    pe.wait_ge(weighted, t + 3)
                    for j in range(G):
                        o = pe.matmul(psL_v[:, j, :], onehot_t[:, u, j, :], k.icnt[:, ds(b * REL, REL)],
                                      start=True, stop=True)
                    o.then_inc(looked, 1)

                def sum_up(t, u):
                    g = group_of(pe, z, k, t)
                    pe.wait_ge(weighted, t + 4)
                    pe.wait_ge(ready, g + 1)
                    pe.wait_ge(added, t + 3)
                    for j in range(G):
                        o = pe.matmul(psS[:, 0:C], onehot[:, u, j, :], ring[:, ds((g % R) * G + j, 1), :],
                                      start=j == 0, stop=j == G - 1)
                    o.then_inc(summed, 1)

                def step(t, u):
                    turn(t + 2, (u + 2) % U)
                    look_up(t + 1, (u + 1) % U)
                    sum_up(t, u)
                turn(0, 0)
                turn(1, 1)
                look_up(0, 0)
                pair_turns(pe, z, step)

            @block.vector
            def _(v):
                start_at(v, BASE, hot, weighted, added)

                def mark(t, u):
                    g = group_of(v, z, k, t)
                    v.wait_ge(summed, t + 1)
                    pair_one_hot(v, k, onehot[:, u, :, :], t, g).then_inc(hot, 1)

                def weigh(t, u):
                    g = group_of(v, z, k, t)
                    v.tensor_tensor(rel[:], k.iota[:, 0:REL].unsqueeze(1).to_broadcast([P, G, REL]),
                                    k.etf[:, ds(g * G, G)].unsqueeze(2).to_broadcast([P, G, REL]), ALU.is_equal)
                    v.drain()
                    v.wait_ge(looked, t + 4)
                    v.tensor_tensor(picked[:], rel[:], psL_v, ALU.mult)
                    v.drain()
                    v.tensor_reduce(w[:], picked[:], AX.X, ALU.add)
                    v.drain()
                    v.tensor_tensor(onehot[:, u, :, :], onehot[:, u, :, :],
                                    w[:].unsqueeze(2).to_broadcast([P, G, P]), ALU.mult).then_inc(weighted, 1)

                def add_up(t):
                    b = block_of(v, z, k, t)
                    v.wait_ge(summed, t + 4)
                    v.tensor_tensor(k.xb[:, ds(b * C, C)], k.xb[:, ds(b * C, C)], psS[:, 0:C],
                                    ALU.add).then_inc(added, 1)
                    v.drain()

                def step(t, u):
                    mark(t + 2, (u + 2) % U)
                    if not (isinstance(t, int) and t == 0):
                        add_up(t - 1)
                    weigh(t + 1, (u + 1) % U)
                mark(0, 0)
                mark(1, 1)
                weigh(0, 0)
                pair_turns(v, z, step)
                add_up(z.T - 1)


def relation_rows(nc, z, k, S, ctxw, ksum):
    NB = z.NB
    with ExitStack() as c:
        work = c.enter_context(ExitStack())
        sem = lambda n: c.enter_context(nc.semaphore("rr_" + n))
        sb = lambda n, s, d=F32: work.enter_context(nc.sbuf_tensor("rr_" + n, s, d))
        wr = sb("wr", [P, KC, REL * C])
        rkq = sb("rkq", [P, KC, 3 * C])
        bias = sb("bias", [1, 2, C])
        comp = sb("comp", [P, REL * NE])
        with ExitStack() as c2:
            basis = c2.enter_context(nc.sbuf_tensor("rr_basis", [P, NE, KC, C], F32))
            nb = S["L1_gnn_basis"].shape[0]
            load_weights(nc, "rr_load", [
                (basis[:, b, :, :], rows_of(S["L1_gnn_basis"][b])) for b in range(nb)] + [
                (comp[:], S["L1_gnn_comp"].rearrange("r b -> (r b)").partition_broadcast(P)),
                (rkq[:, :, 0:C], rows_of(S["L1_gnn_root"])),
                (rkq[:, :, C:2 * C], rows_of(S["L1_mix_Wk_t"])),
                (rkq[:, :, 2 * C:], rows_of(S["L1_mix_Wq_t"])),
                (bias[:, 0, :], S["L1_gnn_bias"].rearrange("(o n) -> o n", o=1)),
                (bias[:, 1, :], S["L1_mix_bproj"].rearrange("(o n) -> o n", o=1))])
            with nc.Block() as block:
                @block.vector
                def _(v):
                    for b in range(nb):
                        for r in range(REL):
                            w = wr[:, :, r * C:(r + 1) * C]
                            s = comp[:, r * nb + b:r * nb + b + 1]
                            if b == 0:
                                v.tensor_scalar(w, basis[:, b, :, :], s, None, ALU.mult)
                            else:
                                v.scalar_tensor_tensor(w, basis[:, b, :, :], s, w, ALU.mult, ALU.add)
                        v.drain()
        st = sb("st", [P, 2, C + 2])
        xt = sb("xt", [P, 2, C])
        y = sb("y", [P, 2, REL * C // 2])
        low = sb("low", [P, 2, 2 * C])
        kk = sb("kk", [P, 2, C])
        zero = sb("zero", [P, C + 2])
        psT = c.enter_context(nc.psum_tensor("rr_psT", [P, 512], F32))
        psY = c.enter_context(nc.psum_tensor("rr_psY", [P, 2, 512], F32))
        psR = c.enter_context(nc.psum_tensor("rr_psR", [P, 512], F32))
        psQ = c.enter_context(nc.psum_tensor("rr_psQ", [P, 512], F32))
        psC = c.enter_context(nc.psum_tensor("rr_psC", [P, 2, 512], F32))
        YP = REL * C // 512
        staged, turned, back, rooted, root_in, kq, floored, powered, kq_in, summed, parts, parts_in = (
            sem(x) for x in ("staged", "turned", "back", "rooted", "root_in", "kq", "floored", "powered",
                             "kq_in", "summed", "parts", "parts_in"))
        stored = [sem("stored0"), sem("stored1")]
        with nc.Block() as block:
            @block.vector
            def _(v):
                v.memset(zero[:], 0.0)
                v.memset(st[:], 1.0)
        with nc.Block() as block:
            @block.scalar
            def _(act):
                for s in (staged, powered):
                    act.sem_inc(s, 2)
                act.sem_inc(parts_in, 2)

                def body(b, u, i, last):
                    act.wait_ge(summed, b + 1)
                    act.nop()
                    act.copy(st[:, u, 0:C], k.xa[:, ds(b * C, C)]).then_inc(staged, 1)
                    act.wait_ge(floored, b + 3)
                    act.nop()
                    act.activation(low[:, u, :], low[:, u, :], ACT.Exp).then_inc(powered, 1)
                    for q in range(YP):
                        half, at = divmod(q, YP // 2)
                        if at == 0 and not (isinstance(b, int) and b == 0):
                            act.wait_ge(stored[half], b * 16)
                        act.wait_ge(parts, b * YP + q + 1)
                        act.nop()
                        act.copy(y[:, half, at * 512:(at + 1) * 512], psY[:, q % 2, :]).then_inc(parts_in, 1)
                two_at_a_time(act, NB, body, peel=True)

            @block.tensor
            def _(pe):
                for s in (turned, rooted, kq, summed):
                    pe.sem_inc(s, 2)
                for kc in range(KC):
                    pe.matmul(psC[:, kc, 0:C + 2], zero[:, 0:P], zero[:], start=True, stop=False)

                def body(b, u, i, last):
                    pe.wait_ge(staged, b + 3)
                    pe.wait_ge(back, b + 2)
                    for kc in range(KC):
                        t = pe.transpose(psT[:, kc * P:(kc + 1) * P], st[:, u, kc * P:(kc + 1) * P], k.ident[:])
                    t.then_inc(turned, 1)
                    pe.wait_ge(back, b + 3)
                    pe.wait_ge(kq_in, b + 2)
                    for kc in range(KC):
                        t = pe.matmul(psQ[:, :], xt[:, u, kc * P:(kc + 1) * P], rkq[:, kc, C:],
                                      start=kc == 0, stop=kc == KC - 1)
                    t.then_inc(kq, 1)
                    pe.wait_ge(root_in, b + 2)
                    for kc in range(KC):
                        pe.matmul(psR[:, 0:C], xt[:, u, kc * P:(kc + 1) * P], rkq[:, kc, 0:C],
                                  start=kc == 0, stop=False)
                    for r in range(2):
                        t = pe.matmul(psR[:, 0:C], k.ones[0:1, :], bias[:, r, :], start=False, stop=r == 1)
                    t.then_inc(rooted, 1)
                    for q in range(YP):
                        pe.wait_ge(parts_in, b * YP + q + 1)
                        for kc in range(KC):
                            t = pe.matmul(psY[:, q % 2, :], xt[:, u, kc * P:(kc + 1) * P],
                                          wr[:, kc, q * 512:(q + 1) * 512], start=kc == 0, stop=kc == KC - 1)
                        t.then_inc(parts, 1)
                    pe.wait_ge(kq_in, b + 3)
                    for kc in range(KC):
                        t = pe.matmul(psC[:, kc, 0:C + 2], kk[:, u, kc * P:(kc + 1) * P], st[:, u, :],
                                      start=False, stop=last)
                    t.then_inc(summed, 1)
                two_at_a_time(pe, NB, body)

            @block.vector
            def _(v):
                for s in (back, root_in, floored, kq_in):
                    v.sem_inc(s, 2)

                def body(b, u, i, last):
                    v.wait_ge(turned, b + 3)
                    v.wait_ge(summed, b + 1)
                    v.tensor_copy(xt[:, u, :], psT[:, 0:C]).then_inc(back, 1)
                    v.wait_ge(kq, b + 3)
                    v.tensor_scalar(low[:, u, :], psQ[:, :], 0.0, None, ALU.min).then_inc(floored, 1)
                    v.wait_ge(rooted, b + 3)
                    v.tensor_tensor(k.xb[:, ds(b * C, C)], k.xb[:, ds(b * C, C)], psR[:, 0:C], ALU.add
                                    ).then_inc(root_in, 1)
                    v.wait_ge(powered, b + 3)
                    v.wait_ge(staged, b + 3)
                    if last:
                        v.scalar_tensor_tensor(kk[:, u, :], psQ[:, 0:C], 0.0, low[:, u, 0:C], ALU.max, ALU.add)
                        v.drain()
                        v.tensor_scalar(kk[:, u, :], kk[:, u, :], k.mask[:, 0:1], None, ALU.mult)
                    else:
                        v.scalar_tensor_tensor(kk[:, u, :], psQ[:, 0:C], 0.0, low[:, u, 0:C], ALU.max, ALU.add)
                    v.scalar_tensor_tensor(k.xa[:, ds(b * C, C)], psQ[:, C:2 * C], 0.0, low[:, u, C:], ALU.max,
                                           ALU.add).then_inc(kq_in, 1)
                two_at_a_time(v, NB, body)

            @block.sync
            def _(sp):
                rows = k.y_dram.rearrange("(n r) c -> n (r c)", r=REL)

                def body(b, u, i, last):
                    for half in range(2):
                        width = REL * C // 2
                        sp.wait_ge(parts_in, b * YP + YP // 2 * (half + 1) + 2)
                        sp.dma_start(rows[ds(b * P, P), half * width:(half + 1) * width], y[:, half, :]
                                     ).then_inc(stored[half], 16)
                two_at_a_time(sp, NB, body)
                for half in range(2):
                    sp.wait_ge(stored[half], 16 * NB)
        work.close()
        sb = lambda n, s, d=F32: c.enter_context(nc.sbuf_tensor("rr_" + n, s, d))
        wv = sb("wv", [P, KC, C])
        wp = sb("wp", [P, KC, C])
        cs = sb("cs", [P, KC, C + 2])
        ct = sb("ct", [P, KC, C])
        cbd = sb("cbd", [P, KC, C])
        kcol = sb("kcol", [P, KC, P])
        load_weights(nc, "rr_load2", [(wv[:], rows_of(S["L1_mix_Wv_t"])), (wp[:], rows_of(S["L1_mix_Wproj_t"]))])
        step, done = sem("step"), sem("done")
        with nc.Block() as block:
            @block.vector
            def _(v):
                v.memset(cbd[:], 0.0)
                v.tensor_copy(cs[:], psC[:, :, 0:C + 2])
                v.drain()
                for kc in range(KC):
                    o = v.tensor_scalar(kcol[:, kc, :], k.ones[:], cs[:, kc, C:C + 1], None, ALU.mult)
                o.then_inc(step, 1)
                v.wait_ge(done, 1)
                v.tensor_copy(ct[:], psC[:, :, 0:C])
                v.tensor_copy(ksum[:], psT[:, 0:C]).then_inc(step, 1)
                v.wait_ge(done, 2)
                for kc in range(KC):
                    for q in range(P // D):
                        a = kc * P + q * D
                        o = v.tensor_copy(cbd[q * D:(q + 1) * D, kc, a:a + D],
                                          psY[q * D:(q + 1) * D, kc, a:a + D])
                o.then_inc(step, 1)
                v.wait_ge(done, 3)
                v.tensor_copy(ctxw[:], psC[:, :, 0:C])

            @block.tensor
            def _(pe):
                pe.wait_ge(step, 1)
                for m in range(KC):
                    for kc in range(KC):
                        pe.transpose(psC[:, m, kc * P:(kc + 1) * P], cs[:, kc, m * P:(m + 1) * P], k.ident[:])
                for kc in range(KC):
                    t = pe.matmul(psT[:, kc * P:(kc + 1) * P], kcol[:, kc, :], k.ident[:], start=True, stop=True)
                t.then_inc(done, 1)
                pe.wait_ge(step, 2)
                for m in range(KC):
                    for kc in range(KC):
                        t = pe.matmul(psY[:, m, 0:C], wv[:, kc, m * P:(m + 1) * P], ct[:, kc, :],
                                      start=kc == 0, stop=kc == KC - 1)
                t.then_inc(done, 1)
                pe.wait_ge(step, 3)
                for m in range(KC):
                    for kc in range(KC):
                        t = pe.matmul(psC[:, m, 0:C], cbd[:, kc, m * P:(m + 1) * P], wp[:, kc, :],
                                      start=kc == 0, stop=kc == KC - 1)
                t.then_inc(done, 1)


def linear_attention_out(nc, z, k, ctxw, ksum):
    NB = z.NB
    with ExitStack() as c:
        sem = lambda n: c.enter_context(nc.semaphore("lo_" + n))
        sb = lambda n, s, d=F32: c.enter_context(nc.sbuf_tensor("lo_" + n, s, d))
        prod = sb("prod", [P, C])
        den = sb("den", [P, HEADS])
        st = sb("st", [P, 2, C])
        xt = sb("xt", [P, 2, C])
        psT = c.enter_context(nc.psum_tensor("lo_psT", [P, 2, 512], F32))
        psM = c.enter_context(nc.psum_tensor("lo_psM", [P, 2, 512], F32))
        scaled, turned, back, projected, added = (sem(x) for x in
            ("scaled", "turned", "back", "projected", "added"))
        with nc.Block() as block:
            @block.vector
            def _(v):
                v.sem_inc(scaled, 2)
                v.sem_inc(added, 2)

                def scale(b, u):
                    q = k.xa[:, ds(b * C, C)]
                    v.tensor_tensor(prod[:], q, ksum[:], ALU.mult)
                    v.drain()
                    v.tensor_reduce(den[:], prod[:].rearrange("p (h d) -> p h d", d=D), AX.X, ALU.add)
                    v.drain()
                    v.tensor_scalar(den[:], den[:], 1e-6, None, ALU.max)
                    v.drain()
                    v.reciprocal(den[:], den[:])
                    v.drain()
                    v.wait_ge(turned, b + 1)
                    v.tensor_tensor(st[:, u, :].rearrange("p (h d) -> p h d", d=D),
                                    q.rearrange("p (h d) -> p h d", d=D),
                                    den[:].unsqueeze(2).to_broadcast([P, HEADS, D]), ALU.mult
                                    ).then_inc(scaled, 1)

                def body(b, u, i, last):
                    if not last:
                        scale(b + 1, 1 - u)
                    v.wait_ge(projected, b + 3)
                    v.tensor_tensor(k.xb[:, ds(b * C, C)], k.xb[:, ds(b * C, C)], psM[:, u, 0:C], ALU.add
                                    ).then_inc(added, 1)
                scale(0, 0)
                two_at_a_time(v, NB, body)

            @block.tensor
            def _(pe):
                pe.sem_inc(turned, 2)
                pe.sem_inc(projected, 2)

                def body(b, u, i, last):
                    pe.wait_ge(scaled, b + 3)
                    pe.wait_ge(back, b + 1)
                    for kc in range(KC):
                        t = pe.transpose(psT[:, u, kc * P:(kc + 1) * P], st[:, u, kc * P:(kc + 1) * P], k.ident[:])
                    t.then_inc(turned, 1)
                    pe.wait_ge(back, b + 3)
                    pe.wait_ge(added, b + 1)
                    for kc in range(KC):
                        t = pe.matmul(psM[:, u, 0:C], xt[:, u, kc * P:(kc + 1) * P], ctxw[:, kc, :],
                                      start=kc == 0, stop=kc == KC - 1)
                    t.then_inc(projected, 1)
                two_at_a_time(pe, NB, body)

            @block.scalar
            def _(act):
                act.sem_inc(back, 2)

                def body(b, u, i, last):
                    act.wait_ge(turned, b + 3)
                    act.wait_ge(projected, b + 1)
                    act.nop()
                    act.copy(xt[:, u, :], psT[:, u, 0:C]).then_inc(back, 1)
                two_at_a_time(act, NB, body)


def experts(nc, z, k, name, norms, w1d, b1d, w2d, b2d, routed, br, gamma, beta, tokens, probs):
    NB = z.NB
    HID = w1d.shape[2]
    HC = HID // P
    with ExitStack() as c:
        sem = lambda n: c.enter_context(nc.semaphore(name + n))
        sb = lambda n, s, d=F32: c.enter_context(nc.sbuf_tensor(name + n, s, d))
        w1 = sb("w1", [P, NE, KC, HID])
        w2 = sb("w2", [P, NE, HC, C])
        b1 = sb("b1", [P, NE, HC])
        b2 = sb("b2", [NE, C])
        wr = sb("wr", [P, KC, NE])
        brow = sb("brow", [1, NE])
        cols = sb("cols", [P, 2, KC])
        lower = sb("lower", [P, NE, NE])
        st = sb("st", [P, 2, C])
        xt = sb("xt", [P, 2, C])
        lg = sb("lg", [P, NE])
        mx = sb("mx", [P, 2])
        ex = sb("ex", [P, NE])
        gt = sb("gt", [P, NE, NE])
        eq = sb("eq", [P, NE, NE])
        rank = sb("rank", [P, NE])
        gates = sb("gates", [P, 2, NE])
        gates_t = sb("gates_t", [NE, 2, P])
        hid = sb("hid", [P, 2, HC * P])
        psT = c.enter_context(nc.psum_tensor(name + "psT", [P, 512], F32))
        psG = c.enter_context(nc.psum_tensor(name + "psG", [P, 512], F32))
        psW = c.enter_context(nc.psum_tensor(name + "psW", [P, 512], F32))
        psB = c.enter_context(nc.psum_tensor(name + "psB", [P, 512], F32))
        psH = c.enter_context(nc.psum_tensor(name + "psH", [P, 2, 512], F32))
        psO = c.enter_context(nc.psum_tensor(name + "psO", [P, 2, 512], F32))
        loads = [(w1[:, e, :, :], rows_of(w1d[e])) for e in range(NE)]
        loads += [(w2[:, e, :, :], rows_of(w2d[e])) for e in range(NE)]
        loads += [(b1[:, e, :], b1d[e]) for e in range(NE)]
        loads += [(b2[:], b2d), (wr[:], rows_of(routed))]
        if br is not None:
            loads.append((brow[:], br.rearrange("(o n) -> o n", o=1)))
        if gamma is not None:
            loads += [(cols[:, 0, :], gamma), (cols[:, 1, :], beta)]
        load_weights(nc, name + "load", loads)
        zeroed = sem("zeroed")
        with nc.Block() as block:
            @block.gpsimd
            def _(p):
                p.memset(lower[:], 0.0).then_inc(zeroed, 1)
                p.wait_ge(zeroed, 1)
                p.affine_select(out=lower[:], in_=lower[:], compare_op=ALU.is_ge, fill=1.0, base=0,
                                pattern=[[-1, NE], [1, NE]], channel_multiplier=0)
            if br is None:
                @block.vector
                def _(v):
                    v.memset(brow[:], 0.0)
        staged, turned, back, logits, e_arg, e_done, gated, gates_turned, gates_back, biased, bias_in = (
            sem(x) for x in ("staged", "turned", "back", "logits", "e_arg", "e_done", "gated",
                             "gates_turned", "gates_back", "biased", "bias_in"))
        hidden, act_out, outs, taken = (sem(x) for x in ("hidden", "act_out", "outs", "taken"))
        with nc.Block() as block:
            @block.scalar
            def _(act):
                for s in (back, e_done, act_out):
                    act.sem_inc(s, 2)

                def prep(b, u):
                    act.wait_ge(turned, b + 3)
                    act.nop()
                    for kc in range(KC):
                        x = (xt[:, u, kc * P:(kc + 1) * P], psT[:, kc * P:(kc + 1) * P])
                        if gamma is None:
                            o = act.copy(*x)
                        else:
                            o = act.activation(*x, ACT.Identity, bias=cols[:, 1, kc:kc + 1], scale=cols[:, 0, kc:kc + 1])
                    o.then_inc(back, 1)

                def power(b):
                    act.wait_ge(e_arg, b + 3)
                    act.nop()
                    act.activation(ex[:], ex[:], ACT.Exp).then_inc(e_done, 1)

                def body(b, u, i, last):
                    for e in range(NE):
                        n = b * NE + e
                        act.wait_ge(hidden, n + 3)
                        act.wait_ge(outs, n + 1)
                        act.nop()
                        for q in range(HC):
                            o = act.activation(hid[:, e % 2, q * P:(q + 1) * P],
                                               psH[:, e % 2, q * P:(q + 1) * P], ACT.Gelu,
                                               bias=b1[:, e, q:q + 1])
                        o.then_inc(act_out, 1)
                        if e == 1 and not last:
                            prep(b + 1, 1 - u)
                        if e == 3 and not last:
                            power(b + 1)
                prep(0, 0)
                power(0)
                two_at_a_time(act, NB, body)

            @block.tensor
            def _(pe):
                for s in (turned, logits, gates_turned, biased, hidden, outs):
                    pe.sem_inc(s, 2)

                def prep(b, u):
                    pe.wait_ge(staged, b + 3)
                    pe.wait_ge(back, b + 2)
                    for kc in range(KC):
                        t = pe.transpose(psT[:, kc * P:(kc + 1) * P], st[:, u, kc * P:(kc + 1) * P], k.ident[:])
                    t.then_inc(turned, 1)

                def route(b, u):
                    pe.wait_ge(back, b + 3)
                    pe.wait_ge(gated, b + 2)
                    for kc in range(KC):
                        pe.matmul(psG[:, 0:NE], xt[:, u, kc * P:(kc + 1) * P], wr[:, kc, :],
                                  start=kc == 0, stop=False)
                    pe.matmul(psG[:, 0:NE], k.ones[0:1, :], brow[:], start=False, stop=True).then_inc(logits, 1)

                def bias(b, u):
                    pe.wait_ge(gated, b + 3)
                    pe.wait_ge(gates_back, b + 2)
                    pe.transpose(psW[0:NE, 0:P], gates[:, u, :], k.ident[:]).then_inc(gates_turned, 1)
                    pe.wait_ge(gates_back, b + 3)
                    pe.wait_ge(bias_in, b + 2)
                    pe.matmul(psB[:, 0:C], gates_t[:, u, :], b2[:], start=True, stop=True).then_inc(biased, 1)

                def hide(b, u, e):
                    pe.wait_ge(act_out, b * NE + e + 1)
                    for q in range(HC):
                        for kc in range(KC):
                            t = pe.matmul(psH[:, e % 2, q * P:(q + 1) * P], w1[:, e, kc, q * P:(q + 1) * P],
                                          xt[:, u, kc * P:(kc + 1) * P], start=kc == 0, stop=kc == KC - 1)
                    t.then_inc(hidden, 1)

                def body(b, u, i, last):
                    hide(b, u, 0)
                    for e in range(NE):
                        if e + 1 < NE:
                            hide(b, u, e + 1)
                        if not last:
                            if e == 1:
                                prep(b + 1, 1 - u)
                            if e == 3:
                                route(b + 1, 1 - u)
                            if e == 6:
                                bias(b + 1, 1 - u)
                        n = b * NE + e
                        pe.wait_ge(act_out, n + 3)
                        pe.wait_ge(taken, n + 1)
                        for q in range(HC):
                            t = pe.matmul(psO[:, e % 2, 0:C], hid[:, e % 2, q * P:(q + 1) * P],
                                          w2[:, e, q, :], start=q == 0, stop=q == HC - 1)
                        t.then_inc(outs, 1)
                prep(0, 0)
                route(0, 0)
                bias(0, 0)
                two_at_a_time(pe, NB, body)

            @block.vector
            def _(v):
                for s in (staged, e_arg, gated, gates_back, bias_in, taken):
                    v.sem_inc(s, 2)

                def prep(b, u):
                    v.wait_ge(turned, b + 1)
                    o = v.tensor_scalar(st[:, u, :], k.xb[:, ds(b * C, C)], norms[0][:, ds(b, 1)],
                                        norms[1][:, ds(b, 1)], ALU.subtract, ALU.mult)
                    if len(norms) == 4:
                        v.drain()
                        o = v.tensor_scalar(st[:, u, :], st[:, u, :], norms[2][:, ds(b, 1)],
                                            norms[3][:, ds(b, 1)], ALU.subtract, ALU.mult)
                    o.then_inc(staged, 1)
                    if tokens:
                        v.drain()
                        v.tensor_tensor(k.xb[:, ds(b * C, C)], k.xb[:, ds(b * C, C)], st[:, u, :], ALU.add)

                def choose(b, u):
                    v.wait_ge(logits, b + 3)
                    v.tensor_copy(lg[:], psG[:, 0:NE])
                    v.tensor_reduce(mx[:, 0:1], psG[:, 0:NE], AX.X, ALU.max)
                    v.drain()
                    v.tensor_scalar(ex[:], lg[:], mx[:, 0:1], None, ALU.subtract).then_inc(e_arg, 1)
                    if probs:
                        v.wait_ge(e_done, b + 3)
                        v.tensor_reduce(mx[:, 1:2], ex[:], AX.X, ALU.add)
                        v.drain()
                        v.reciprocal(mx[:, 1:2], mx[:, 1:2])
                        v.drain()
                        v.tensor_scalar(ex[:], ex[:], mx[:, 1:2], None, ALU.mult)
                        v.drain()
                        v.tensor_copy(lg[:], ex[:])
                        v.drain()
                    other = lg[:].unsqueeze(1).to_broadcast([P, NE, NE])
                    own = lg[:].unsqueeze(2).to_broadcast([P, NE, NE])
                    v.tensor_tensor(gt[:], other, own, ALU.is_gt)
                    v.tensor_tensor(eq[:], other, own, ALU.is_equal)
                    v.drain()
                    v.tensor_tensor(eq[:], eq[:], lower[:], ALU.mult)
                    v.drain()
                    v.tensor_tensor(gt[:], gt[:], eq[:], ALU.add)
                    v.drain()
                    v.tensor_reduce(rank[:], gt[:], AX.X, ALU.add)
                    v.drain()
                    v.tensor_scalar(rank[:], rank[:], 2.0, None, ALU.is_lt)
                    v.drain()
                    v.wait_ge(e_done, b + 3)
                    v.tensor_tensor(ex[:], ex[:], rank[:], ALU.mult)
                    v.drain()
                    v.tensor_reduce(mx[:, 1:2], ex[:], AX.X, ALU.add)
                    v.drain()
                    v.tensor_scalar(mx[:, 1:2], mx[:, 1:2], 1e-12, None, ALU.max)
                    v.drain()
                    v.reciprocal(mx[:, 1:2], mx[:, 1:2])
                    v.drain()
                    v.tensor_scalar(gates[:, u, :], ex[:], mx[:, 1:2], None, ALU.mult).then_inc(gated, 1)

                def biases(b, u):
                    v.wait_ge(gates_turned, b + 3)
                    v.tensor_copy(gates_t[:, u, :], psW[0:NE, 0:P]).then_inc(gates_back, 1)
                    v.drain()
                    v.wait_ge(biased, b + 3)
                    v.tensor_tensor(k.xb[:, ds(b * C, C)], k.xb[:, ds(b * C, C)], psB[:, 0:C], ALU.add
                                    ).then_inc(bias_in, 1)

                def body(b, u, i, last):
                    for e in range(NE):
                        if not last:
                            if e == 0:
                                prep(b + 1, 1 - u)
                            if e == 3:
                                choose(b + 1, 1 - u)
                            if e == 6:
                                biases(b + 1, 1 - u)
                        v.drain()
                        v.wait_ge(outs, b * NE + e + 3)
                        x = k.xb[:, ds(b * C, C)]
                        v.scalar_tensor_tensor(x, psO[:, e % 2, 0:C], gates[:, u, e:e + 1], x, ALU.mult,
                                               ALU.add).then_inc(taken, 1)
                prep(0, 0)
                choose(0, 0)
                biases(0, 0)
                two_at_a_time(v, NB, body)


class Kept:
    pass


def graph_network(nc, S, out):
    n, _ = out.shape
    z = Sizes(n, S["n_edges"])
    NB = z.NB
    k = Kept()
    with ExitStack() as c:
        sb = lambda n, s, d=F32: c.enter_context(nc.sbuf_tensor(n, s, d))
        k.xb = sb("xb", [P, NB * C])
        k.ident = sb("ident", [P, P])
        k.iota = sb("iota", [P, P])
        k.ones = sb("ones", [P, P])
        k.mask = sb("mask", [P, 1])
        k.a2 = sb("a2", [P, NB * HEADS])
        k.icnt = sb("icnt", [P, NB * REL])
        k.dstf = sb("dstf", [P, z.COLS])
        k.etf = sb("etf", [P, z.COLS], BF16)
        k.start = sb("start", [P, z.COLS], BF16)
        k.last = sb("last", [P, z.COLS], BF16)
        k.last_pair = sb("last_pair", [1, z.NCH * P], I32)
        k.pair_block = sb("pair_block", [1, z.NCH * P], I32)
        k.pair_group = sb("pair_group", [1, z.NCH * P], I32)
        k.pair_node = sb("pair_node", [P, z.NCH * P])
        k.src_rel = nc.dram_tensor("src_rel", (P, z.COLS), I32).ap()
        k.table_dram = nc.dram_tensor("table_dram", (2, z.NCH * P, 1), I32).ap()
        mean = sb("mean", [P, NB])
        rstd = sb("rstd", [P, NB])
        mean2 = sb("mean2", [P, NB])
        rstd2 = sb("rstd2", [P, NB])
        k.first_dram = nc.dram_tensor("first_dram", (NB + 1, 1), I32).ap()
        k.h_dram = nc.dram_tensor("h_dram", (NB * P, HROW), F32).ap()
        k.y_dram = nc.dram_tensor("y_dram", (NB * P * REL, C), F32).ap()
        setup(nc, z, S, k)

        with nc.sbuf_tensor("xa0", [P, NB * C], F32) as xa:
            k.xa = xa
            normalise_stats(nc, "n0", k.xb, mean, rstd, 1e-5, NB)
            normalise_rows(nc, k.xa, k.xb, mean, rstd, NB)
            with nc.sbuf_tensor("wqc", [P, KC, C], F32) as wqc:
                with nc.sbuf_tensor("kt", [P, KC * NB * P], F32) as kt:
                    attention_table(nc, z, k, S, kt)
                    keys_to_context(nc, z, k, S, kt, wqc)
                normalise_stats(nc, "n1", k.xa, mean, rstd, 1e-5, NB)
                mix_out(nc, z, k, S, wqc, mean, rstd)
        attention(nc, z, k, S)
        with nc.sbuf_tensor("xa1", [P, NB * C], F32) as xa:
            k.xa = xa
            normalise_stats(nc, "n2", k.xb, mean, rstd, 1e-5, NB)
            normalise_rows(nc, k.xa, k.xb, mean, rstd, NB)
            normalise_stats(nc, "n3", k.xa, mean2, rstd2, 1e-5, NB)
        experts(nc, z, k, "f0_", (mean, rstd, mean2, rstd2), S["L0_ffn_W1"], S["L0_ffn_b1"], S["L0_ffn_W2"],
                    S["L0_ffn_b2"], S["L0_ffn_Wr"], S["L0_ffn_br"], S["L0_ffn_gamma"], S["L0_ffn_beta"],
                    False, False)
        with nc.sbuf_tensor("xa2", [P, NB * C], F32) as xa:
            k.xa = xa
            normalise_stats(nc, "n4", k.xb, mean, rstd, 1e-5, NB)
            normalise_rows(nc, k.xa, k.xb, mean, rstd, NB)
            with nc.sbuf_tensor("ctxw", [P, KC, C], F32) as ctxw, nc.sbuf_tensor("ksum", [P, C], F32) as ksum:
                relation_rows(nc, z, k, S, ctxw, ksum)
                linear_attention_out(nc, z, k, ctxw, ksum)
        relations(nc, z, k, S)
        normalise_stats(nc, "n5", k.xb, mean, rstd, 1e-5, NB)
        experts(nc, z, k, "f1_", (mean, rstd), S["L1_ffn_w1"], S["L1_ffn_b1"], S["L1_ffn_w2"],
                S["L1_ffn_b2"], S["L1_ffn_router_w_t"], None, None, None, True, True)
        with nc.semaphore("stored") as stored, nc.Block() as block:
            @block.sync
            def _(sp):
                full = (NB - 1) * P
                if full:
                    sp.dma_start(out[0:full, :].rearrange("(b p) f -> p b f", p=P),
                                 k.xb[:, 0:full // P * C].rearrange("p (b f) -> p b f", f=C)).then_inc(stored, 16)
                sp.dma_start(out[full:n, :], k.xb[0:z.TAIL, full // P * C:NB * C]).then_inc(stored, 16)
                sp.wait_ge(stored, 16 * (2 if full else 1))


COLUMNS = ("L0_gnn_attn_l", "L0_gnn_attn_r", "L0_mix_ln_g", "L0_mix_ln_b", "L0_mix_bg2", "L0_ffn_gamma",
           "L0_ffn_beta")


def _layouts(x, src, dst, edge_type_16, w):
    import numpy as np
    z = Sizes(x.shape[0], src.shape[0])
    E = src.shape[0]
    far = 1 << 20

    def table(a, fill):
        full = np.full(z.NGT * GE, fill, np.int32)
        full[:E] = a
        return full.reshape(z.NGT, P, G)
    lay = lambda a: np.ascontiguousarray(a.transpose(1, 0, 2).reshape(P, z.COLS))
    d = table(dst, far)
    before = np.full_like(d, -1)
    before[:, 1:] = d[:, :-1]
    behind = np.full_like(d, -1)
    behind[:, :-1] = d[:, 1:]
    xp = np.zeros((z.NB * P, C), np.float32)
    xp[:x.shape[0]] = x
    out = {"x": xp, "src": lay(table(src, 0)), "dst": lay(d), "dst_prev": lay(before),
           "dst_next": lay(behind), "etype": lay(table(edge_type_16, 0)),
           "bounds": np.ascontiguousarray(dst[GE - 1::GE][:z.NG - 1])}
    for name, a in w.items():
        a = np.asarray(a)
        if name == "L0_gnn_W":
            out["L0_gnn_W_t"] = a.T
        if name == "L0_mix_Wqkv":
            out["L0_mix_Wq_t"] = a[:, 0:C].T
        if name in COLUMNS:
            a = a.reshape(KC, P).T
        if name == "L1_mix_Wkv":
            out["L1_mix_Wk_t"], out["L1_mix_Wv_t"] = a[0:C].T, a[C:2 * C].T
        elif name in ("L1_mix_Wq", "L1_mix_Wproj", "L1_ffn_router_w"):
            out[name + "_t"] = a.T
        elif name in ("L0_ffn_b1", "L1_ffn_b1"):
            out[name] = a.reshape(NE, -1, P).transpose(0, 2, 1)
        else:
            out[name] = a
    return {name: np.ascontiguousarray(a) for name, a in out.items()}


def kernel(x, src, dst, edge_type_16, **weights):
    import numpy as _np
    import concourse.bacc as _bacc
    from concourse import mybir as _mybir
    from concourse.bass_utils import run_bass_kernel_spmd as _run

    x, src, dst, edge_type_16 = (_np.asarray(a) for a in (x, src, dst, edge_type_16))
    arrays = _layouts(x, src, dst, edge_type_16, weights)
    nc = _bacc.Bacc("TRN2", target_bir_lowering=False, num_devices=1)
    S = {"n_edges": src.shape[0]}
    for name, a in arrays.items():
        S[name] = nc.dram_tensor(name, a.shape, _mybir.dt.from_np(a.dtype), kind="ExternalInput").ap()
    out = nc.dram_tensor("out", x.shape, F32, kind="ExternalOutput").ap()
    graph_network(nc, S, out)
    r = _run(nc, [arrays], core_ids=[0])
    return r.results[0]["out"]
```

```python
from contextlib import ExitStack, contextmanager

import concourse.bass as bass
from concourse import mybir

P = 128
G = 8
R = 6
GE = G * P
C = 256
KC = C // P
HEADS = 8
D = C // HEADS
REL = 16
NE = 8
U = 4
AHEAD = 3
BASE = 4
HROW = C + HEADS
MROW = C + HEADS + REL
SLOPE = 0.2
BIG = 1e30

ALU = mybir.AluOpType
ACT = mybir.ActivationFunctionType
AX = mybir.AxisListType
F32 = mybir.dt.float32
I32 = mybir.dt.int32
BF16 = mybir.dt.bfloat16
ds = bass.ds


@contextmanager
def semaphores(nc, stage):
    used = []

    def one(name):
        used.append(nc.alloc_semaphore(stage + name))
        return used[-1]
    yield one
    nc.clear_and_free_semaphores(used)
    nc.all_engine_barrier()


def two_at_a_time(eng, n, body, peel=False):
    whole = (n - 1) // 2
    start = 0
    if peel and whole:
        body(0, 0, 0, False)
        body(1, 1, 0, False)
        start = 1
    if whole > start:
        with eng.Fori(start, whole) as k:
            body(k * 2, 0, k, False)
            body(k * 2 + 1, 1, k, False)
    for b in range(2 * whole, n):
        body(b, b % 2, b // 2, b == n - 1)


def in_turns(eng, n, body, per=7):
    if n >= per:
        with eng.Fori(0, n // per) as i:
            for q in range(per):
                body(i * per + q)
    for b in range(n - n % per, n):
        body(b)


class Sizes:
    def __init__(self, n, e):
        self.N = n
        self.NB = -(-n // P)
        self.TAIL = n - (self.NB - 1) * P
        self.NG = -(-e // GE)
        self.T = -(-(self.NG + self.NB - 1) // U) * U
        while True:
            groups = self.T + AHEAD - (self.NB - 1)
            self.NGT = R * -(-groups // R)
            if self.NGT - R - 1 + self.NB - 1 < self.T:
                break
            self.T += U
        self.NCH = -(-max(self.T + AHEAD, self.NGT) // P)
        self.COLS = self.NGT * G


def normalise_stats(nc, name, src, mean, rstd, eps, NB):
    with ExitStack() as c:
        six = c.enter_context(nc.sbuf_tensor(name + "_six", [P, NB, 6], F32))
        tmp = c.enter_context(nc.sbuf_tensor(name + "_tmp", [P, 3, NB], F32))
        var_ready = c.enter_context(nc.semaphore(name + "_var_ready"))
        root_ready = c.enter_context(nc.semaphore(name + "_root_ready"))
        flat = six[:].rearrange("p b s -> p (b s)")
        with nc.Block() as block:
            @block.vector
            def _(v):
                in_turns(v, NB, lambda b: v.bn_stats(flat[:, ds(b * 6, 6)], src[:, ds(b * C, C)]))
                v.drain()
                v.tensor_tensor(tmp[:, 0, :], six[:, :, 1], six[:, :, 4], ALU.add)
                v.tensor_tensor(tmp[:, 1, :], six[:, :, 1], six[:, :, 4], ALU.subtract)
                v.tensor_tensor(tmp[:, 2, :], six[:, :, 2], six[:, :, 5], ALU.add)
                v.drain()
                v.tensor_scalar(mean[:, :], tmp[:, 0, :], 0.5, None, ALU.mult)
                v.tensor_tensor(tmp[:, 1, :], tmp[:, 1, :], tmp[:, 1, :], ALU.mult)
                v.tensor_scalar(tmp[:, 2, :], tmp[:, 2, :], 1.0 / C, eps, ALU.mult, ALU.add)
                v.drain()
                v.scalar_tensor_tensor(tmp[:, 0, :], tmp[:, 1, :], 0.25, tmp[:, 2, :], ALU.mult,
                                       ALU.add).then_inc(var_ready, 1)
                v.wait_ge(root_ready, 1)
                v.reciprocal(rstd[:, :], tmp[:, 1, :])

            @block.scalar
            def _(act):
                act.wait_ge(var_ready, 1)
                act.activation(tmp[:, 1, :], tmp[:, 0, :], ACT.Sqrt).then_inc(root_ready, 1)


def normalise_rows(nc, dst, src, mean, rstd, NB):
    with nc.Block() as block:
        @block.vector
        def _(v):
            in_turns(v, NB, lambda b: v.tensor_scalar(
                dst[:, ds(b * C, C)], src[:, ds(b * C, C)], mean[:, ds(b, 1)], rstd[:, ds(b, 1)],
                ALU.subtract, ALU.mult))


def setup(nc, z, S, k):
    NB, NG = z.NB, z.NG
    with ExitStack() as c:
        sem = c.enter_context(semaphores(nc, "su_"))
        sb = lambda n, s, d=F32: c.enter_context(nc.sbuf_tensor("su_" + n, s, d))
        ints = sb("ints", [P, z.COLS], I32)
        others = sb("others", [P, 2, z.COLS], I32)
        othersf = sb("othersf", [P, 2, z.COLS])
        etypes = sb("etypes", [P, z.COLS], I32)
        bounds = sb("bounds", [NB + 1, NG - 1], I32)
        boundsf = sb("boundsf", [NB + 1, NG - 1])
        below = sb("below", [NB + 1, NG - 1])
        limit = sb("limit", [NB + 1, 1])
        counts = sb("counts", [NB + 1, 1])
        counti = sb("counti", [NB + 1, 1], I32)
        nch = z.NCH
        firsts = sb("firsts", [P, NB - 1], I32)
        firstsf = sb("firstsf", [P, NB - 1])
        gid = sb("gid", [P, nch])
        pairsf = sb("pairsf", [P, NB - 1])
        blockno = sb("blockno", [P, NB - 1])
        hit = sb("hit", [P, 2, nch, NB - 1])
        tables = sb("tables", [P, 2, nch])
        tablesi = sb("tablesi", [P, 2, nch], I32)
        blocks = sb("blocks", [P, nch * P], I32)
        srci = sb("srci", [P, z.COLS], I32)
        src_rel = sb("src_rel", [P, z.COLS], I32)
        iotas = sb("iotas", [P, P], I32)
        loaded, made, cvt, tab, tab2, tab3, ended = (sem(x) for x in
            ("loaded", "made", "cvt", "tab", "tab2", "tab3", "ended"))
        with nc.Block() as block:
            @block.sync
            def _(sp):
                sp.dma_start(ints[:], S["dst"]).then_inc(loaded, 16)
                sp.dma_start(others[:, 0, :], S["dst_prev"]).then_inc(loaded, 16)
                sp.dma_start(others[:, 1, :], S["dst_next"]).then_inc(loaded, 16)
                sp.dma_start(etypes[:], S["etype"]).then_inc(loaded, 16)
                sp.dma_start(bounds[:], S["bounds"].partition_broadcast(NB + 1)).then_inc(loaded, 16)
                sp.dma_start(k.xb[:].rearrange("p (b f) -> p b f", f=C),
                             S["x"].rearrange("(b p) f -> p b f", p=P)).then_inc(loaded, 16)
                sp.dma_start(srci[:], S["src"]).then_inc(loaded, 16)
                sp.wait_ge(loaded, 112)
                sp.wait_ge(cvt, 1)
                sp.dma_start(k.first_dram, counti[:]).then_inc(tab, 16)
                sp.wait_ge(tab, 16)
                row = k.first_dram.rearrange("n o -> o n")
                sp.dma_start(firsts[:], row[0, 1:NB].partition_broadcast(P)).then_inc(tab, 16)
                sp.wait_ge(tab, 32)
                sp.wait_ge(ended, 1)
                for i in range(nch):
                    for q in range(2):
                        sp.dma_start(k.table_dram[q, i * P:(i + 1) * P, :],
                                     tablesi[:, q, i:i + 1]).then_inc(tab2, 16)
                sp.dma_start(k.src_rel, src_rel[:]).then_inc(tab2, 16)
                sp.wait_ge(tab2, 16 * (2 * nch + 1))
                rows = k.table_dram.rearrange("q n o -> q (n o)")
                sp.dma_start(k.last_pair[:], rows[0:1, :]).then_inc(tab3, 16)
                sp.dma_start(k.pair_block[:], rows[1:2, :]).then_inc(tab3, 16)
                sp.dma_start(blocks[:], rows[1, :].partition_broadcast(P)).then_inc(tab3, 16)
                sp.wait_ge(tab3, 48)

            @block.gpsimd
            def _(p):
                p.memset(k.ident[:], 0.0).then_inc(made, 1)
                p.wait_ge(made, 1)
                p.affine_select(out=k.ident[:], in_=k.ident[:], compare_op=ALU.not_equal, fill=1.0,
                                base=0, pattern=[[-1, P]], channel_multiplier=1).then_inc(made, 1)
                p.memset(k.ones[:], 1.0)
                p.iota(iotas[:], [[1, P]], base=0, channel_multiplier=0).then_inc(made, 1)
                p.iota(k.pair_group[:], [[1, nch * P]], base=0, channel_multiplier=0)
                p.iota(limit[:], [[0, 1]], base=0, channel_multiplier=P,
                       allow_small_or_imprecise_dtypes=True)
                p.iota(gid[:], [[P, nch]], base=0, channel_multiplier=1,
                       allow_small_or_imprecise_dtypes=True)
                p.iota(blockno[:], [[1, NB - 1]], base=1, channel_multiplier=0,
                       allow_small_or_imprecise_dtypes=True)
                p.iota(k.mask[:], [[0, 1]], base=0, channel_multiplier=1,
                       allow_small_or_imprecise_dtypes=True).then_inc(made, 1)

            @block.vector
            def _(v):
                v.wait_ge(made, 4)
                v.wait_ge(loaded, 112)
                v.tensor_copy(k.iota[:], iotas[:])
                v.tensor_copy(boundsf[:], bounds[:])
                v.tensor_copy(k.dstf[:], ints[:])
                v.tensor_copy(k.etf[:], etypes[:])
                v.scalar_tensor_tensor(src_rel[:], srci[:], float(REL), etypes[:], ALU.mult, ALU.add)
                v.tensor_copy(othersf[:], others[:])
                v.tensor_scalar(k.mask[:], k.mask[:], float(z.TAIL), None, ALU.is_lt)
                v.drain()
                v.tensor_scalar(below[:], boundsf[:], limit[:, 0:1], None, ALU.is_lt)
                v.drain()
                v.tensor_reduce(counts[:], below[:], AX.X, ALU.add)
                v.drain()
                v.tensor_copy(counti[:], counts[:]).then_inc(cvt, 1)
                v.tensor_tensor(k.start[:], k.dstf[:], othersf[:, 0, :], ALU.not_equal)
                v.tensor_tensor(k.last[:], k.dstf[:], othersf[:, 1, :], ALU.not_equal)
                v.drain()
                v.tensor_scalar(k.start[:], k.start[:], -BIG, None, ALU.mult)
                v.wait_ge(tab, 32)
                v.tensor_copy(firstsf[:], firsts[:])
                v.drain()
                v.tensor_tensor(pairsf[:], firstsf[:], blockno[:], ALU.add)
                v.drain()
                for i in range(nch):
                    v.tensor_scalar(hit[:, 0, i, :], firstsf[:], gid[:, i:i + 1], None, ALU.is_le)
                    v.tensor_scalar(hit[:, 1, i, :], pairsf[:], gid[:, i:i + 1], None, ALU.is_le)
                v.drain()
                v.tensor_reduce(tables[:], hit[:], AX.X, ALU.add)
                v.drain()
                v.scalar_tensor_tensor(tables[:, 0, :], tables[:, 0, :], 1.0, gid[:], ALU.add, ALU.add)
                v.drain()
                v.tensor_copy(tablesi[:], tables[:]).then_inc(ended, 1)
                v.wait_ge(tab3, 48)
                v.tensor_scalar(k.pair_node[:], blocks[:], float(P), None, ALU.mult)
                v.tensor_tensor(k.pair_group[:], k.pair_group[:], k.pair_block[:], ALU.subtract)


def load_weights(nc, name, pairs):
    with ExitStack() as c:
        got = c.enter_context(nc.semaphore(name))
        with nc.Block() as block:
            @block.sync
            def _(sp):
                for dst, src in pairs:
                    sp.dma_start(dst, src).then_inc(got, 16)
                sp.wait_ge(got, 16 * len(pairs))


def rows_of(w):
    return w.rearrange("(k p) n -> p k n", p=P)


def attention_table(nc, z, k, S, kt):
    NB = z.NB
    A2 = 2 * HEADS
    with ExitStack() as c:
        sem = c.enter_context(semaphores(nc, "at_"))
        sb = lambda n, s, d=F32: c.enter_context(nc.sbuf_tensor("at_" + n, s, d))
        w = sb("w", [P, KC, C])
        wt = sb("wt", [P, KC, C])
        attn = sb("attn", [P, 2, KC])
        lr = sb("lr", [P, KC, A2])
        waug = sb("waug", [P, KC, C + A2])
        wk = sb("wk", [P, KC, C])
        st = sb("st", [P, 2, C])
        xt = sb("xt", [P, 2, C])
        row = sb("row", [P, 2, HROW])
        psT = c.enter_context(nc.psum_tensor("at_psT", [P, 2, 512], F32))
        psH = c.enter_context(nc.psum_tensor("at_psH", [P, 2, 512], F32))
        psK = c.enter_context(nc.psum_tensor("at_psK", [P, 2, 512], F32))
        load_weights(nc, "at_load", [
            (w[:], rows_of(S["L0_gnn_W"])), (wt[:], rows_of(S["L0_gnn_W_t"])),
            (attn[:, 0, :], S["L0_gnn_attn_l"]),
            (attn[:, 1, :], S["L0_gnn_attn_r"]),
            (wk[:], rows_of(S["L0_mix_Wqkv"])[:, :, C:2 * C])])
        spread, folded = sem("spread"), sem("folded")
        with nc.Block() as block:
            @block.vector
            def _(v):
                v.memset(lr[:], 0.0)
                v.drain()
                for kc in range(KC):
                    for q in range(P // D):
                        h = kc * (P // D) + q
                        for s in range(2):
                            v.tensor_copy(lr[q * D:(q + 1) * D, kc, s * HEADS + h:s * HEADS + h + 1],
                                          attn[q * D:(q + 1) * D, s, kc:kc + 1])
                v.drain()
                v.tensor_copy(waug[:, :, 0:C], w[:]).then_inc(spread, 1)
                v.wait_ge(folded, 1)
                v.tensor_copy(waug[:, :, C:C + A2], psH[:, :, 0:A2])

            @block.tensor
            def _(pe):
                pe.wait_ge(spread, 1)
                for m in range(KC):
                    for kc in range(KC):
                        mm = pe.matmul(psH[:, m, 0:A2], wt[:, kc, m * P:(m + 1) * P], lr[:, kc, :],
                                       start=kc == 0, stop=kc == KC - 1)
                mm.then_inc(folded, 1)
        staged, turned, back, made, taken, keys = (sem(x) for x in
            ("staged", "turned", "back", "made", "taken", "keys"))
        stored = [sem("stored0"), sem("stored1")]
        with nc.Block() as block:
            @block.scalar
            def _(act):
                act.sem_inc(staged, 2)
                act.sem_inc(keys, 2)

                def prep(b, u):
                    act.wait_ge(turned, b + 1)
                    act.nop()
                    act.copy(st[:, u, :], k.xa[:, ds(b * C, C)]).then_inc(staged, 1)

                def body(b, u, i, last):
                    if not last:
                        prep(b + 1, 1 - u)
                    act.wait_ge(made, b + 3)
                    act.nop()
                    for kc in range(KC):
                        o = act.copy(kt[:, ds(b * P + kc * NB * P, P)], psK[:, u, kc * P:(kc + 1) * P])
                    o.then_inc(keys, 1)
                prep(0, 0)
                two_at_a_time(act, NB, body)

            @block.tensor
            def _(pe):
                pe.sem_inc(turned, 2)
                pe.sem_inc(made, 2)

                def prep(b, u):
                    pe.wait_ge(staged, b + 3)
                    pe.wait_ge(back, b + 1)
                    for kc in range(KC):
                        t = pe.transpose(psT[:, u, kc * P:(kc + 1) * P], st[:, u, kc * P:(kc + 1) * P],
                                         k.ident[:])
                    t.then_inc(turned, 1)

                def body(b, u, i, last):
                    if not last:
                        prep(b + 1, 1 - u)
                    pe.wait_ge(back, b + 3)
                    pe.wait_ge(taken, b + 1)
                    pe.wait_ge(keys, b + 1)
                    for kc in range(KC):
                        pe.matmul(psH[:, u, 0:C + A2], xt[:, u, kc * P:(kc + 1) * P], waug[:, kc, :],
                                  start=kc == 0, stop=kc == KC - 1)
                    for m in range(KC):
                        for kc in range(KC):
                            t = pe.matmul(psK[:, u, m * P:(m + 1) * P], wk[:, kc, m * P:(m + 1) * P],
                                          xt[:, u, kc * P:(kc + 1) * P], start=kc == 0, stop=kc == KC - 1)
                    t.then_inc(made, 1)
                prep(0, 0)
                two_at_a_time(pe, NB, body)

            @block.vector
            def _(v):
                v.sem_inc(back, 2)
                v.sem_inc(taken, 2)

                def prep(b, u):
                    v.wait_ge(turned, b + 3)
                    v.wait_ge(made, b + 1)
                    v.tensor_copy(xt[:, u, :], psT[:, u, 0:C]).then_inc(back, 1)

                def body(b, u, i, last):
                    if not last:
                        prep(b + 1, 1 - u)
                    if not (isinstance(i, int) and i == 0):
                        v.wait_ge(stored[u], i * 16)
                    v.wait_ge(made, b + 3)
                    v.tensor_copy(k.a2[:, ds(b * HEADS, HEADS)], psH[:, u, C + HEADS:C + A2])
                    v.tensor_copy(row[:, u, :], psH[:, u, 0:HROW]).then_inc(taken, 1)
                prep(0, 0)
                two_at_a_time(v, NB, body, peel=True)

            @block.sync
            def _(sp):
                def body(b, u, i, last):
                    sp.wait_ge(taken, b + 3)
                    sp.dma_start(k.h_dram[ds(b * P, P), :], row[:, u, :]).then_inc(stored[u], 16)
                two_at_a_time(sp, NB, body)
                sp.wait_ge(stored[0], 16 * ((NB + 1) // 2))
                sp.wait_ge(stored[1], 16 * (NB // 2))


def keys_to_context(nc, z, k, S, kt, wqc):
    NB, N = z.NB, z.N
    NP = NB * P
    with ExitStack() as c:
        sem = c.enter_context(semaphores(nc, "kc_"))
        sb = lambda n, s, d=F32: c.enter_context(nc.sbuf_tensor("kc_" + n, s, d))
        wqt = sb("wqt", [P, KC, C])
        wv = sb("wv", [P, KC, C])
        top = sb("top", [P, KC])
        total = sb("total", [P, KC])
        st = sb("st", [P, 2, C])
        ek = sb("ek", [P, 2, C])
        zero = sb("zero", [P, C])
        cs = sb("cs", [P, KC, C])
        ct = sb("ct", [P, KC, C])
        cbd = sb("cbd", [P, KC, C])
        psT = c.enter_context(nc.psum_tensor("kc_psT", [P, 2, 512], F32))
        psC = c.enter_context(nc.psum_tensor("kc_psC", [P, 2, 512], F32))
        load_weights(nc, "kc_load", [(wqt[:], rows_of(S["L0_mix_Wq_t"])),
                                     (wv[:], rows_of(S["L0_mix_Wqkv"])[:, :, 2 * C:3 * C])])
        topped, powered = sem("topped"), sem("powered")
        with nc.Block() as block:
            @block.vector
            def _(v):
                v.memset(zero[:], 0.0)
                v.memset(cbd[:], 0.0)
                for kc in range(KC):
                    v.tensor_reduce(top[:, kc:kc + 1], kt[:, kc * NP:kc * NP + N], AX.X, ALU.max)
                v.drain()
                v.tensor_scalar(top[:], top[:], -1.0, None, ALU.mult).then_inc(topped, 1)
                if NP > N:
                    for kc in range(KC):
                        v.memset(kt[:, kc * NP + N:(kc + 1) * NP], 0.0)
                v.wait_ge(powered, 1)
                v.reciprocal(total[:], total[:])

            @block.scalar
            def _(act):
                act.wait_ge(topped, 1)
                for kc in range(KC):
                    o = act.activation(kt[:, kc * NP:kc * NP + N], kt[:, kc * NP:kc * NP + N], ACT.Exp,
                                       bias=top[:, kc:kc + 1], accum_out=total[:, kc:kc + 1])
                o.then_inc(powered, 1)
        staged, turned, back, summed = (sem(x) for x in ("staged", "turned", "back", "summed"))
        with nc.Block() as block:
            @block.scalar
            def _(act):
                act.sem_inc(staged, 2)

                def body(b, u, i, last):
                    act.wait_ge(turned, b + 1)
                    act.nop()
                    for kc in range(KC):
                        o = act.copy(st[:, u, kc * P:(kc + 1) * P], kt[:, ds(b * P + kc * NP, P)])
                    o.then_inc(staged, 1)
                two_at_a_time(act, NB, body)

            @block.tensor
            def _(pe):
                pe.sem_inc(turned, 2)
                pe.sem_inc(summed, 2)
                for kc in range(KC):
                    pe.matmul(psC[:, kc, 0:C], zero[:, 0:P], zero[:], start=True, stop=False)

                def prep(b, u):
                    pe.wait_ge(staged, b + 3)
                    pe.wait_ge(back, b + 1)
                    for kc in range(KC):
                        t = pe.transpose(psT[:, u, kc * P:(kc + 1) * P], st[:, u, kc * P:(kc + 1) * P],
                                         k.ident[:])
                    t.then_inc(turned, 1)

                def body(b, u, i, last):
                    if not last:
                        prep(b + 1, 1 - u)
                    pe.wait_ge(back, b + 3)
                    for kc in range(KC):
                        t = pe.matmul(psC[:, kc, 0:C], ek[:, u, kc * P:(kc + 1) * P],
                                      k.xa[:, ds(b * C, C)], start=False, stop=last)
                    t.then_inc(summed, 1)
                prep(0, 0)
                two_at_a_time(pe, NB, body)

            @block.vector
            def _(v):
                v.sem_inc(back, 2)

                def body(b, u, i, last):
                    v.wait_ge(turned, b + 3)
                    v.wait_ge(summed, b + 1)
                    v.tensor_copy(ek[:, u, :], psT[:, u, 0:C]).then_inc(back, 1)
                two_at_a_time(v, NB, body)
        step, worked = sem("step"), sem("worked")
        with nc.Block() as block:
            @block.vector
            def _(v):
                for kc in range(KC):
                    o = v.tensor_scalar(cs[:, kc, :], psC[:, kc, 0:C], total[:, kc:kc + 1], None, ALU.mult)
                o.then_inc(step, 1)
                v.wait_ge(worked, 1)
                v.tensor_copy(ct[:], psT[:, :, 0:C]).then_inc(step, 1)
                v.wait_ge(worked, 2)
                for kc in range(KC):
                    for q in range(P // D):
                        a = kc * P + q * D
                        o = v.tensor_copy(cbd[q * D:(q + 1) * D, kc, a:a + D],
                                          psC[q * D:(q + 1) * D, kc, a:a + D])
                o.then_inc(step, 1)
                v.wait_ge(worked, 3)
                v.tensor_copy(wqc[:], psT[:, :, 0:C])

            @block.tensor
            def _(pe):
                pe.wait_ge(step, 1)
                for m in range(KC):
                    for kc in range(KC):
                        t = pe.transpose(psT[:, m, kc * P:(kc + 1) * P], cs[:, kc, m * P:(m + 1) * P],
                                         k.ident[:])
                t.then_inc(worked, 1)
                pe.wait_ge(step, 2)
                for m in range(KC):
                    for kc in range(KC):
                        t = pe.matmul(psC[:, m, 0:C], ct[:, kc, m * P:(m + 1) * P], wv[:, kc, :],
                                      start=kc == 0, stop=kc == KC - 1)
                t.then_inc(worked, 1)
                pe.wait_ge(step, 3)
                for m in range(KC):
                    for kc in range(KC):
                        t = pe.matmul(psT[:, m, 0:C], wqt[:, kc, m * P:(m + 1) * P], cbd[:, kc, :],
                                      start=kc == 0, stop=kc == KC - 1)
                t.then_inc(worked, 1)


def mix_out(nc, z, k, S, wqc, mean, rstd):
    NB = z.NB
    GH = S["L0_mix_Wg1"].shape[1]
    with ExitStack() as c:
        sem = c.enter_context(semaphores(nc, "mo_"))
        sb = lambda n, s, d=F32: c.enter_context(nc.sbuf_tensor("mo_" + n, s, d))
        g1 = sb("g1", [P, KC, GH])
        g2 = sb("g2", [GH, C])
        wp = sb("wp", [P, KC, C])
        cols = sb("cols", [P, 3, KC])
        bg1 = sb("bg1", [GH, 1])
        bias = sb("bias", [1, 2, C])
        st = sb("st", [P, 2, 2 * C])
        xt = sb("xt", [P, 2, 2 * C])
        hid = sb("hid", [GH, 2, P])
        gate = sb("gate", [P, 2, C])
        prod = sb("prod", [P, 2, C])
        psT = c.enter_context(nc.psum_tensor("mo_psT", [P, 2, 512], F32))
        psG = c.enter_context(nc.psum_tensor("mo_psG", [GH, 2, 512], F32))
        psU = c.enter_context(nc.psum_tensor("mo_psU", [P, 2, 512], F32))
        psM = c.enter_context(nc.psum_tensor("mo_psM", [P, 2, 512], F32))
        load_weights(nc, "mo_load", [
            (g1[:], rows_of(S["L0_mix_Wg1"])), (g2[:], S["L0_mix_Wg2"]), (wp[:], rows_of(S["L0_mix_Wproj"])),
            (cols[:, 0, :], S["L0_mix_ln_g"]), (cols[:, 1, :], S["L0_mix_ln_b"]),
            (cols[:, 2, :], S["L0_mix_bg2"]),
            (bg1[:], S["L0_mix_bg1"].rearrange("(p o) -> p o", o=1)),
            (bias[:, 0, :], S["L0_mix_bproj"].rearrange("(o n) -> o n", o=1)),
            (bias[:, 1, :], S["L0_gnn_bias"].rearrange("(o n) -> o n", o=1))])
        staged, normed, turned, back, hidden, gelu, gated, sig, timed, projected, added = (
            sem(x) for x in ("staged", "normed", "turned", "back", "hidden", "gelu", "gated", "sig",
                             "timed", "projected", "added"))
        with nc.Block() as block:
            @block.scalar
            def _(act):
                for s in (staged, back, gelu, sig):
                    act.sem_inc(s, 2)

                def prep(b, u):
                    act.wait_ge(turned, b + 1)
                    act.nop()
                    act.copy(st[:, u, 0:C], k.xa[:, ds(b * C, C)]).then_inc(staged, 1)
                    act.wait_ge(turned, b + 3)
                    act.wait_ge(gated, b + 1)
                    act.nop()
                    act.copy(xt[:, u, 0:C], psT[:, u, 0:C])
                    for kc in range(KC):
                        o = act.activation(xt[:, u, C + kc * P:C + (kc + 1) * P],
                                           psT[:, u, C + kc * P:C + (kc + 1) * P], ACT.Identity,
                                           bias=cols[:, 1, kc:kc + 1], scale=cols[:, 0, kc:kc + 1])
                    o.then_inc(back, 1)

                def body(b, u, i, last):
                    if not last:
                        prep(b + 1, 1 - u)
                    act.wait_ge(hidden, b + 3)
                    act.nop()
                    act.activation(hid[:, u, :], psG[:, u, 0:P], ACT.Gelu, bias=bg1[:, 0:1]).then_inc(gelu, 1)
                    act.wait_ge(gated, b + 3)
                    act.wait_ge(timed, b + 1)
                    act.nop()
                    for kc in range(KC):
                        o = act.activation(gate[:, u, kc * P:(kc + 1) * P],
                                           psU[:, u, C + kc * P:C + (kc + 1) * P], ACT.Sigmoid,
                                           bias=cols[:, 2, kc:kc + 1])
                    o.then_inc(sig, 1)
                prep(0, 0)
                two_at_a_time(act, NB, body)

            @block.vector
            def _(v):
                for s in (normed, timed, added):
                    v.sem_inc(s, 2)

                def prep(b, u):
                    v.wait_ge(turned, b + 1)
                    v.tensor_scalar(st[:, u, C:2 * C], k.xa[:, ds(b * C, C)], mean[:, ds(b, 1)],
                                    rstd[:, ds(b, 1)], ALU.subtract, ALU.mult).then_inc(normed, 1)

                def add(b, u):
                    v.wait_ge(projected, b + 3)
                    v.tensor_tensor(k.xb[:, ds(b * C, C)], k.xb[:, ds(b * C, C)], psM[:, u, 0:C],
                                    ALU.add).then_inc(added, 1)

                def body(b, u, i, last):
                    if not last:
                        prep(b + 1, 1 - u)
                    if not (isinstance(b, int) and b == 0):
                        add(b - 1, 1 - u)
                    v.wait_ge(sig, b + 3)
                    v.wait_ge(projected, b + 1)
                    v.tensor_tensor(prod[:, u, :], psU[:, u, 0:C], gate[:, u, :], ALU.mult).then_inc(timed, 1)
                prep(0, 0)
                two_at_a_time(v, NB, body, peel=True)
                add(NB - 1, (NB - 1) % 2)

            @block.tensor
            def _(pe):
                for s in (turned, hidden, gated, projected):
                    pe.sem_inc(s, 2)

                def prep(b, u):
                    pe.wait_ge(staged, b + 3)
                    pe.wait_ge(normed, b + 3)
                    pe.wait_ge(back, b + 1)
                    for q in range(2 * KC):
                        t = pe.transpose(psT[:, u, q * P:(q + 1) * P], st[:, u, q * P:(q + 1) * P], k.ident[:])
                    t.then_inc(turned, 1)

                def project(b, u):
                    pe.wait_ge(timed, b + 3)
                    pe.wait_ge(added, b + 1)
                    for kc in range(KC):
                        pe.matmul(psM[:, u, 0:C], prod[:, u, kc * P:(kc + 1) * P], wp[:, kc, :],
                                  start=kc == 0, stop=False)
                    for r in range(2):
                        t = pe.matmul(psM[:, u, 0:C], k.ones[0:1, :], bias[:, r, :], start=False, stop=r == 1)
                    t.then_inc(projected, 1)

                def body(b, u, i, last):
                    pe.wait_ge(back, b + 3)
                    pe.wait_ge(gelu, b + 1)
                    for kc in range(KC):
                        t = pe.matmul(psG[:, u, 0:P], g1[:, kc, :], xt[:, u, C + kc * P:C + (kc + 1) * P],
                                      start=kc == 0, stop=kc == KC - 1)
                    t.then_inc(hidden, 1)
                    if not last:
                        prep(b + 1, 1 - u)
                    pe.wait_ge(timed, b + 1)
                    for m in range(KC):
                        for kc in range(KC):
                            pe.matmul(psU[:, u, m * P:(m + 1) * P], wqc[:, kc, m * P:(m + 1) * P],
                                      xt[:, u, kc * P:(kc + 1) * P], start=kc == 0, stop=kc == KC - 1)
                    if not (isinstance(b, int) and b == 0):
                        project(b - 1, 1 - u)
                    pe.wait_ge(gelu, b + 3)
                    for m in range(KC):
                        t = pe.matmul(psU[:, u, C + m * P:C + (m + 1) * P], g2[:, m * P:(m + 1) * P],
                                      hid[:, u, :], start=True, stop=True)
                    t.then_inc(gated, 1)
                prep(0, 0)
                two_at_a_time(pe, NB, body, peel=True)
                project(NB - 1, (NB - 1) % 2)


def gather_groups(nc, z, block, k, table, rows, ring, idx, landed, gathered, ready, go, freed):
    turns = z.NGT // R

    @block.sync
    def _(sp):
        def load(g, s):
            sp.dma_start(idx[:, s, :], rows[:, ds(g * G, G)]).then_inc(landed[s], 16)
        for s in range(R):
            load(s, s)
        with sp.Fori(1, turns) as i:
            for s in range(R):
                pair = sp.value_load(k.last_pair[0:1, ds((i - 1) * R + s, 1)], min_val=1,
                                     max_val=z.T)
                sp.wait_ge(freed, done(pair - 1))
                load(i * R + s, s)
        sp.wait_ge(ready, z.NGT)

    @block.gpsimd
    def _(p):
        def gather(i, s):
            p.wait_ge(landed[s], (i + 1) * 16)
            p.sem_inc(go, 1)
            for j in range(G):
                p.indirect_dma_start(ring[:, s * G + j, :], None, table,
                                     bass.IndirectOffsetOnAxis(ap=idx[:, s, j:j + 1], axis=0)
                                     ).then_inc(gathered[s], 16)

        def report(i, s):
            p.wait_ge(gathered[s], (i + 1) * 16 * G)
            p.sem_inc(ready, 1)
        gather(0, 0)
        for s in range(1, R):
            gather(0, s)
            report(0, s - 1)
        with p.Fori(1, turns) as i:
            for s in range(R):
                gather(i, s)
                if s:
                    report(i, s - 1)
                else:
                    report(i - 1, R - 1)
        report(turns - 1, R - 1)


def pair_turns(eng, z, step):
    for t in range(U):
        step(t, t)
    with eng.Fori(1, z.T // U) as i:
        for u in range(U):
            step(i * U + u, u)


def group_of(eng, z, k, t):
    return eng.value_load(k.pair_group[0:1, ds(t, 1)], min_val=0, max_val=z.NGT - 1)


def block_of(eng, z, k, t):
    return eng.value_load(k.pair_block[0:1, ds(t, 1)], min_val=0, max_val=z.NB - 1)


def done(t):
    return t + BASE + 1


def start_at(eng, value, *sems):
    for s in sems:
        eng.sem_inc(s, value)


def pair_one_hot(v, k, onehot, t, g):
    return v.scalar_tensor_tensor(onehot, k.dstf[:, ds(g * G, G)].unsqueeze(2).to_broadcast([P, G, P]),
                                  k.pair_node[:, ds(t, 1)],
                                  k.iota[:].unsqueeze(1).to_broadcast([P, G, P]), ALU.subtract, ALU.is_equal)


def attention(nc, z, k, S):
    NB = z.NB
    with ExitStack() as c:
        sem = c.enter_context(semaphores(nc, "ga_"))
        sb = lambda n, s, d=F32: c.enter_context(nc.sbuf_tensor("ga_" + n, s, d))
        acc = sb("acc", [P, NB, MROW - C])
        rden = sb("rden", [P, NB, HEADS])
        spill(nc, z, k, "ga_spill")
        with nc.Block() as block:
            @block.vector
            def _(v):
                v.memset(acc[:], 0.0)
                v.memset(k.xb[:], 0.0)
        attend(nc, z, k, S, acc)
        xs = sb("xs", [P, NB * C])
        with nc.Block() as block:
            restored = [sem(f"restored{q}") for q in range(2)]
            half = NB // 2 * C
            parts = [(0, half), (half, NB * C)] if half else [(0, NB * C)]
            xs_v = xs[:].rearrange("p (b f) -> p b f", f=C)
            xd = k.x_dram.rearrange("(b p) f -> p b f", p=P)

            @block.sync
            def _(sp):
                for q, (lo, hi) in enumerate(parts):
                    sp.dma_start(xs_v[:, lo // C:hi // C, :], xd[:, lo // C:hi // C, :]).then_inc(restored[q], 16)

            @block.vector
            def _(v):
                v.tensor_scalar(rden[:], acc[:, :, 0:HEADS], 1e-30, None, ALU.max)
                v.tensor_scalar(acc[:, :, HEADS:], acc[:, :, HEADS:], 1.0, None, ALU.max)
                v.drain()
                v.reciprocal(rden[:], rden[:])
                v.reciprocal(k.icnt[:].rearrange("p (b r) -> p b r", r=REL), acc[:, :, HEADS:])
                v.drain()
                for q, (lo, hi) in enumerate(parts):
                    heads = k.xb[:, lo:hi].rearrange("p (b h d) -> p b h d", h=HEADS, d=D)
                    scale = rden[:, lo // C:hi // C, :].unsqueeze(3).to_broadcast([P, (hi - lo) // C, HEADS, D])
                    v.tensor_tensor(heads, heads, scale, ALU.mult)
                    v.drain()
                    v.wait_ge(restored[q], 16)
                    v.tensor_tensor(k.xb[:, lo:hi], k.xb[:, lo:hi], xs[:, lo:hi], ALU.add)


def spill(nc, z, k, name):
    with nc.semaphore(name) as stored, nc.Block() as block:
        @block.sync
        def _(sp):
            sp.dma_start(k.x_dram.rearrange("(b p) f -> p b f", p=P),
                         k.xb[:].rearrange("p (b f) -> p b f", f=C)).then_inc(stored, 16)
            sp.wait_ge(stored, 16)


def attend(nc, z, k, S, acc):
    NB = z.NB
    with ExitStack() as c:
        sem = c.enter_context(semaphores(nc, "ga_"))
        sb = lambda n, s, d=F32: c.enter_context(nc.sbuf_tensor("ga_" + n, s, d))
        ring = sb("ring", [P, R * G, HROW])
        idx = sb("idx", [P, R, G], I32)
        onehot = sb("onehot", [P, U, G, P])
        onehot_t = sb("onehot_t", [P, G, P])
        sta = sb("sta", [P, G, HEADS])
        stb = sb("stb", [P, G, HEADS])
        starts = sb("starts", [G * HEADS, P])
        scan = sb("scan", [G * HEADS, P])
        runs = sb("runs", [P, 2, G, HEADS + 1])
        miss = sb("miss", [P, G])
        cand = sb("cand", [P, G, HEADS])
        red = sb("red", [P, HEADS])
        tot = sb("tot", [P, HEADS])
        log = sb("log", [P, HEADS])
        old = sb("old", [P, HEADS])
        look = sb("look", [P, NB, 2 * HEADS])
        esum = sb("esum", [P, G, HEADS])
        elog = sb("elog", [P, G, HEADS])
        arg = sb("arg", [P, G + 1, HEADS])
        w = sb("w", [P, U, G + 1, HEADS])
        msg = sb("msg", [P, 2, G, MROW])
        psI = c.enter_context(nc.psum_tensor("ga_psI", [P, 512], F32))
        psQ = c.enter_context(nc.psum_tensor("ga_psQ", [P, 512], F32))
        psT = c.enter_context(nc.psum_tensor("ga_psT", [P, G, P], F32))
        psX = c.enter_context(nc.psum_tensor("ga_psX", [P, 512], F32))
        psL = c.enter_context(nc.psum_tensor("ga_psL", [P, 512], F32))
        psS = c.enter_context(nc.psum_tensor("ga_psS", [P, 512], F32))
        landed = [sem(f"landed{s}") for s in range(R)]
        gathered = [sem(f"gathered{s}") for s in range(R)]
        ready, go, pe_go, hot, hot_t, turned = (
            sem(x) for x in ("ready", "go", "pe_go", "hot", "hot_t", "turned"))
        m_staged, m_turned, m_starts, m_scan, m_back, m_runs = (
            sem("m_" + x) for x in ("staged", "turned", "starts", "scan", "back", "runs"))
        maxed, shifts, looked, args, weights, messages, summed, added = (
            sem(x) for x in ("maxed", "shifts", "looked", "args", "weights", "messages", "summed", "added"))
        GH = G * HEADS
        psX_v = psX[:, 0:G * (HEADS + 1)].rearrange("p (j h) -> p j h", j=G)
        psL_v = psL[:, 0:G * 2 * HEADS].rearrange("p (j h) -> p j h", j=G)
        psQ_v = psQ[:, 0:GH].rearrange("p (j h) -> p j h", j=G)
        acc_f = acc[:].rearrange("p b r -> p (b r)")
        look_f = look[:].rearrange("p b h -> p (b h)")
        with nc.Block() as block:
            @block.vector
            def _(v):
                v.memset(look[:, :, HEADS:], -BIG)
                v.tensor_copy(look[:, :, 0:HEADS], k.a2[:].rearrange("p (b h) -> p b h", h=HEADS))
        with nc.Block() as block:
            gather_groups(nc, z, block, k, k.h_dram, S["src"], ring, idx, landed, gathered, ready, go, messages)

            def slot(g):
                return (g % R) * G

            @block.scalar
            def _(act):
                start_at(act, BASE, m_staged, m_starts, hot_t, weights)

                def stage(t):
                    g = group_of(act, z, k, t)
                    act.wait_ge(ready, g + 1)
                    act.wait_ge(m_turned, done(t - 1))
                    act.nop()
                    act.copy(sta[:], ring[:, ds(slot(g), G), C:HROW])
                    act.copy(stb[:], k.start[:, ds(g * G, G)].unsqueeze(2).to_broadcast([P, G, HEADS])
                             ).then_inc(m_staged, 1)

                def spread_starts(t, u):
                    g = group_of(act, z, k, t)
                    act.wait_ge(maxed, done(t - 2))
                    act.wait_ge(m_turned, done(t))
                    act.nop()
                    act.copy(starts[:], psI[0:GH, P:2 * P])
                    act.copy(runs[:, u % 2, :, HEADS:HEADS + 1],
                             k.last[:, ds(g * G, G)].unsqueeze(2)).then_inc(m_starts, 1)

                def turn_one_hot(t):
                    act.wait_ge(turned, done(t))
                    act.wait_ge(looked, done(t - 1))
                    act.nop()
                    for q in range(G // 4):
                        o = act.copy(onehot_t[:, 4 * q:4 * q + 4, :], psT[:, 4 * q:4 * q + 4, :])
                    o.then_inc(hot_t, 1)

                def power(t, u):
                    act.wait_ge(args, done(t))
                    act.wait_ge(added, done(t - U))
                    act.nop()
                    act.activation(w[:, u, :, :], arg[:], ACT.Exp).then_inc(weights, 1)

                def step(t, u):
                    stage(t + 3)
                    spread_starts(t + 3, (u + 3) % U)
                    turn_one_hot(t + 2)
                    power(t + 1, (u + 1) % U)
                stage(0)
                spread_starts(0, 0)
                stage(1)
                turn_one_hot(0)
                spread_starts(1, 1)
                stage(2)
                spread_starts(2, 2)
                turn_one_hot(1)
                power(0, 0)
                pair_turns(act, z, step)

            @block.tensor
            def _(pe):
                start_at(pe, BASE, m_turned, m_back, turned, maxed, looked, summed)

                def turn_runs(t):
                    pe.wait_ge(m_staged, done(t))
                    pe.wait_ge(m_scan, done(t - 1))
                    pe.sem_inc(pe_go, 1)
                    pe.transpose(psI[0:GH, 0:P], sta[:].rearrange("p j h -> p (j h)"), k.ident[:])
                    pe.transpose(psI[0:GH, P:2 * P], stb[:].rearrange("p j h -> p (j h)"), k.ident[:]
                                 ).then_inc(m_turned, 1)

                def turn_back(t):
                    pe.wait_ge(m_scan, done(t))
                    pe.wait_ge(m_runs, done(t - 1))
                    pe.sem_inc(pe_go, 1)
                    pe.transpose(psQ[:, 0:GH], scan[:], k.ident[0:GH, 0:GH]).then_inc(m_back, 1)

                def turn(t, u):
                    pe.wait_ge(hot, done(t))
                    pe.wait_ge(hot_t, done(t - 1))
                    for j in range(G):
                        o = pe.transpose(psT[:, j, :], onehot[:, u, j, :], k.ident[:])
                    o.then_inc(turned, 1)

                def maxima(t, u):
                    pe.wait_ge(m_runs, done(t))
                    pe.wait_ge(m_starts, done(t))
                    pe.wait_ge(hot, done(t))
                    pe.wait_ge(shifts, done(t - 1))
                    for j in range(G):
                        o = pe.matmul(psX_v[:, j, :], onehot[:, u, j, :], runs[:, u % 2, j, :],
                                      start=True, stop=True)
                    o.then_inc(maxed, 1)

                def look_up(t):
                    b = block_of(pe, z, k, t)
                    pe.wait_ge(shifts, done(t))
                    pe.wait_ge(hot_t, done(t))
                    pe.wait_ge(args, done(t - 1))
                    for j in range(G):
                        o = pe.matmul(psL_v[:, j, :], onehot_t[:, j, :], look_f[:, ds(b * 2 * HEADS, 2 * HEADS)],
                                      start=True, stop=True)
                    o.then_inc(looked, 1)

                def sum_up(t, u):
                    pe.wait_ge(messages, done(t))
                    pe.wait_ge(added, done(t - 1))
                    for j in range(G):
                        o = pe.matmul(psS[:, 0:MROW], onehot[:, u, j, :], msg[:, u % 2, j, :],
                                      start=j == 0, stop=j == G - 1)
                    o.then_inc(summed, 1)

                def step(t, u):
                    turn_back(t + 2)
                    look_up(t + 1)
                    turn_runs(t + 3)
                    turn(t + 2, (u + 2) % U)
                    maxima(t + 2, (u + 2) % U)
                    sum_up(t, u)
                turn_runs(0)
                turn_back(0)
                turn(0, 0)
                maxima(0, 0)
                turn_runs(1)
                turn_back(1)
                look_up(0)
                turn_runs(2)
                turn(1, 1)
                maxima(1, 1)
                pair_turns(pe, z, step)

            @block.vector
            def _(v):
                start_at(v, BASE, m_scan, m_runs, hot, shifts, args, messages, added)

                def scan_runs(t):
                    v.wait_ge(m_starts, done(t))
                    v.wait_ge(m_back, done(t - 1))
                    v.tensor_tensor_scan(scan[:], starts[:], psI[0:GH, 0:P], -BIG, ALU.add, ALU.max
                                         ).then_inc(m_scan, 1)

                def keep_ends(t, u, g):
                    v.wait_ge(m_back, done(t))
                    v.wait_ge(maxed, done(t - 2))
                    v.tensor_tensor(runs[:, u % 2, :, 0:HEADS], psQ_v,
                                    k.last[:, ds(g * G, G)].unsqueeze(2).to_broadcast([P, G, HEADS]),
                                    ALU.mult).then_inc(m_runs, 1)

                def mark(t, u, g):
                    v.wait_ge(summed, done(t - U))
                    pair_one_hot(v, k, onehot[:, u, :, :], t, g).then_inc(hot, 1)

                def shift(t, b):
                    shifts_b = look_f[:, ds(b * 2 * HEADS + HEADS, HEADS)]
                    v.tensor_copy(old[:], shifts_b)
                    v.wait_ge(maxed, done(t))
                    v.tensor_scalar(miss[:], psX_v[:, :, HEADS], -1.0, BIG, ALU.add, ALU.mult)
                    v.drain()
                    v.tensor_tensor(cand[:], psX_v[:, :, 0:HEADS],
                                    miss[:].unsqueeze(2).to_broadcast([P, G, HEADS]), ALU.add)
                    v.drain()
                    v.tensor_reduce(red[:], cand[:].rearrange("p j h -> p h j"), AX.X, ALU.max)
                    v.drain()
                    v.tensor_tensor(tot[:], red[:], look_f[:, ds(b * 2 * HEADS, HEADS)], ALU.add)
                    v.drain()
                    v.scalar_tensor_tensor(log[:], tot[:], SLOPE, tot[:], ALU.mult, ALU.max)
                    v.drain()
                    v.wait_ge(looked, done(t - 1))
                    v.tensor_tensor(shifts_b, log[:], old[:], ALU.max).then_inc(shifts, 1)
                    v.drain()
                    v.wait_ge(weights, done(t - 1))
                    v.tensor_tensor(arg[:, G, :], old[:], shifts_b, ALU.subtract)

                def arguments(t, g):
                    v.wait_ge(looked, done(t))
                    v.tensor_tensor(esum[:], ring[:, ds(slot(g), G), C:HROW], psL_v[:, :, 0:HEADS], ALU.add)
                    v.drain()
                    v.scalar_tensor_tensor(elog[:], esum[:], SLOPE, esum[:], ALU.mult, ALU.max)
                    v.drain()
                    v.tensor_tensor(arg[:, 0:G, :], elog[:], psL_v[:, :, HEADS:], ALU.subtract
                                    ).then_inc(args, 1)

                def weigh(t, u, g):
                    v.wait_ge(summed, done(t - 2))
                    v.tensor_tensor(msg[:, u % 2, :, C + HEADS:],
                                    k.iota[:, 0:REL].unsqueeze(1).to_broadcast([P, G, REL]),
                                    k.etf[:, ds(g * G, G)].unsqueeze(2).to_broadcast([P, G, REL]), ALU.is_equal)
                    v.wait_ge(weights, done(t))
                    v.tensor_scalar(msg[:, u % 2, :, C:C + HEADS], w[:, u, 0:G, :], 1.0, None, ALU.min)
                    v.scalar_tensor_tensor(
                        msg[:, u % 2, :, 0:C].rearrange("p j (h d) -> p j h d", d=D),
                        w[:, u, 0:G, :].unsqueeze(3).to_broadcast([P, G, HEADS, D]), 1.0,
                        ring[:, ds(slot(g), G), 0:C].rearrange("p j (h d) -> p j h d", d=D),
                        ALU.min, ALU.mult).then_inc(messages, 1)

                def add_up(t, u, b):
                    scale = w[:, u, G, :]
                    sums = k.xb[:, ds(b * C, C)]
                    heads = sums.rearrange("p (h d) -> p h d", d=D)
                    both = acc_f[:, ds(b * (MROW - C), MROW - C)]
                    den = acc_f[:, ds(b * (MROW - C), HEADS)]
                    v.tensor_tensor(heads, heads, scale.unsqueeze(2).to_broadcast([P, HEADS, D]), ALU.mult)
                    v.tensor_tensor(den, den, scale, ALU.mult)
                    v.drain()
                    v.wait_ge(summed, done(t))
                    v.tensor_tensor(sums, sums, psS[:, 0:C], ALU.add)
                    v.tensor_tensor(both, both, psS[:, C:MROW], ALU.add).then_inc(added, 1)

                def step(t, u):
                    weigh(t, u, group_of(v, z, k, t))
                    before = None if isinstance(t, int) and t == 0 else block_of(v, z, k, t - 1)
                    g1, g2, g3 = (group_of(v, z, k, t + i) for i in (1, 2, 3))
                    b2 = block_of(v, z, k, t + 2)
                    keep_ends(t + 2, u + 2, g2)
                    if before is not None:
                        add_up(t - 1, (u - 1) % U, before)
                    mark(t + 3, (u + 3) % U, g3)
                    scan_runs(t + 3)
                    arguments(t + 1, g1)
                    shift(t + 2, b2)
                scan_runs(0)
                keep_ends(0, 0, 0)
                mark(0, 0, 0)
                shift(0, 0)
                scan_runs(1)
                keep_ends(1, 1, group_of(v, z, k, 1))
                mark(1, 1, group_of(v, z, k, 1))
                arguments(0, 0)
                scan_runs(2)
                mark(2, 2, group_of(v, z, k, 2))
                shift(1, block_of(v, z, k, 1))
                pair_turns(v, z, step)
                add_up(z.T - 1, (z.T - 1) % U, block_of(v, z, k, z.T - 1))


def relations(nc, z, k, S):
    with ExitStack() as c:
        sem = c.enter_context(semaphores(nc, "rg_"))
        sb = lambda n, s, d=F32: c.enter_context(nc.sbuf_tensor("rg_" + n, s, d))
        ring = sb("ring", [P, R * G, C])
        idx = sb("idx", [P, R, G], I32)
        onehot = sb("onehot", [P, U, G, P])
        onehot_t = sb("onehot_t", [P, U, G, P])
        rel = sb("rel", [P, G, REL])
        picked = sb("picked", [P, G, REL])
        w = sb("w", [P, G])
        psT = c.enter_context(nc.psum_tensor("rg_psT", [P, G, P], F32))
        psL = c.enter_context(nc.psum_tensor("rg_psL", [P, 512], F32))
        psS = c.enter_context(nc.psum_tensor("rg_psS", [P, 512], F32))
        landed = [sem(f"landed{s}") for s in range(R)]
        gathered = [sem(f"gathered{s}") for s in range(R)]
        ready, go, hot, hot_t, turned, looked, weighted, summed, added = (
            sem(x) for x in ("ready", "go", "hot", "hot_t", "turned", "looked", "weighted", "summed", "added"))
        psL_v = psL[:, 0:G * REL].rearrange("p (j r) -> p j r", j=G)
        with nc.Block() as block:
            gather_groups(nc, z, block, k, k.y_dram, k.src_rel, ring, idx, landed, gathered, ready, go, summed)

            @block.scalar
            def _(act):
                start_at(act, BASE, hot_t)

                def turn_one_hot(t, u):
                    act.wait_ge(turned, done(t))
                    act.wait_ge(looked, done(t - U))
                    act.nop()
                    for q in range(G // 4):
                        o = act.copy(onehot_t[:, u, 4 * q:4 * q + 4, :], psT[:, 4 * q:4 * q + 4, :])
                    o.then_inc(hot_t, 1)
                turn_one_hot(0, 0)
                turn_one_hot(1, 1)
                pair_turns(act, z, lambda t, u: turn_one_hot(t + 2, (u + 2) % U))

            @block.tensor
            def _(pe):
                start_at(pe, BASE, turned, looked, summed)

                def turn(t, u):
                    pe.wait_ge(hot, done(t))
                    pe.wait_ge(hot_t, done(t - 1))
                    for j in range(G):
                        o = pe.transpose(psT[:, j, :], onehot[:, u, j, :], k.ident[:])
                    o.then_inc(turned, 1)

                def look_up(t, u):
                    b = block_of(pe, z, k, t)
                    pe.wait_ge(hot_t, done(t))
                    pe.wait_ge(weighted, done(t - 1))
                    for j in range(G):
                        o = pe.matmul(psL_v[:, j, :], onehot_t[:, u, j, :], k.icnt[:, ds(b * REL, REL)],
                                      start=True, stop=True)
                    o.then_inc(looked, 1)

                def sum_up(t, u):
                    g = group_of(pe, z, k, t)
                    pe.wait_ge(weighted, done(t))
                    pe.wait_ge(ready, g + 1)
                    pe.wait_ge(added, done(t - 1))
                    for j in range(G):
                        o = pe.matmul(psS[:, 0:C], onehot[:, u, j, :], ring[:, ds((g % R) * G + j, 1), :],
                                      start=j == 0, stop=j == G - 1)
                    o.then_inc(summed, 1)

                def step(t, u):
                    turn(t + 2, (u + 2) % U)
                    look_up(t + 1, (u + 1) % U)
                    sum_up(t, u)
                turn(0, 0)
                turn(1, 1)
                look_up(0, 0)
                pair_turns(pe, z, step)

            @block.vector
            def _(v):
                start_at(v, BASE, hot, weighted, added)

                def mark(t, u):
                    g = group_of(v, z, k, t)
                    v.wait_ge(summed, done(t - U))
                    pair_one_hot(v, k, onehot[:, u, :, :], t, g).then_inc(hot, 1)

                def weigh(t, u):
                    g = group_of(v, z, k, t)
                    v.tensor_tensor(rel[:], k.iota[:, 0:REL].unsqueeze(1).to_broadcast([P, G, REL]),
                                    k.etf[:, ds(g * G, G)].unsqueeze(2).to_broadcast([P, G, REL]), ALU.is_equal)
                    v.drain()
                    v.wait_ge(looked, done(t))
                    v.tensor_tensor(picked[:], rel[:], psL_v, ALU.mult)
                    v.drain()
                    v.tensor_reduce(w[:], picked[:], AX.X, ALU.add)
                    v.drain()
                    v.tensor_tensor(onehot[:, u, :, :], onehot[:, u, :, :],
                                    w[:].unsqueeze(2).to_broadcast([P, G, P]), ALU.mult).then_inc(weighted, 1)

                def add_up(t):
                    b = block_of(v, z, k, t)
                    v.wait_ge(summed, done(t))
                    v.tensor_tensor(k.xb[:, ds(b * C, C)], k.xb[:, ds(b * C, C)], psS[:, 0:C],
                                    ALU.add).then_inc(added, 1)
                    v.drain()

                def step(t, u):
                    mark(t + 2, (u + 2) % U)
                    if not (isinstance(t, int) and t == 0):
                        add_up(t - 1)
                    weigh(t + 1, (u + 1) % U)
                mark(0, 0)
                mark(1, 1)
                weigh(0, 0)
                pair_turns(v, z, step)
                add_up(z.T - 1)


def relation_rows(nc, z, k, S, ctxw, ksum):
    NB = z.NB
    with ExitStack() as c:
        work = c.enter_context(ExitStack())
        sem = c.enter_context(semaphores(nc, "rr_"))
        sb = lambda n, s, d=F32: work.enter_context(nc.sbuf_tensor("rr_" + n, s, d))
        wr = sb("wr", [P, KC, REL * C])
        rkq = sb("rkq", [P, KC, 3 * C])
        bias = sb("bias", [1, 2, C])
        comp = sb("comp", [P, REL * NE])
        with ExitStack() as c2:
            basis = c2.enter_context(nc.sbuf_tensor("rr_basis", [P, NE, KC, C], F32))
            nb = S["L1_gnn_basis"].shape[0]
            load_weights(nc, "rr_load", [
                (basis[:, b, :, :], rows_of(S["L1_gnn_basis"][b])) for b in range(nb)] + [
                (comp[:], S["L1_gnn_comp"].rearrange("r b -> (r b)").partition_broadcast(P)),
                (rkq[:, :, 0:C], rows_of(S["L1_gnn_root"])),
                (rkq[:, :, C:2 * C], rows_of(S["L1_mix_Wk_t"])),
                (rkq[:, :, 2 * C:], rows_of(S["L1_mix_Wq_t"])),
                (bias[:, 0, :], S["L1_gnn_bias"].rearrange("(o n) -> o n", o=1)),
                (bias[:, 1, :], S["L1_mix_bproj"].rearrange("(o n) -> o n", o=1))])
            with nc.Block() as block:
                @block.vector
                def _(v):
                    for b in range(nb):
                        for r in range(REL):
                            w = wr[:, :, r * C:(r + 1) * C]
                            s = comp[:, r * nb + b:r * nb + b + 1]
                            if b == 0:
                                v.tensor_scalar(w, basis[:, b, :, :], s, None, ALU.mult)
                            else:
                                v.scalar_tensor_tensor(w, basis[:, b, :, :], s, w, ALU.mult, ALU.add)
                        v.drain()
        st = sb("st", [P, 2, C + 2])
        xt = sb("xt", [P, 2, C])
        y = sb("y", [P, 2, REL * C // 2])
        low = sb("low", [P, 2, 2 * C])
        kk = sb("kk", [P, 2, C])
        zero = sb("zero", [P, C + 2])
        psT = c.enter_context(nc.psum_tensor("rr_psT", [P, 512], F32))
        psY = c.enter_context(nc.psum_tensor("rr_psY", [P, 2, 512], F32))
        psR = c.enter_context(nc.psum_tensor("rr_psR", [P, 512], F32))
        psQ = c.enter_context(nc.psum_tensor("rr_psQ", [P, 512], F32))
        psC = c.enter_context(nc.psum_tensor("rr_psC", [P, 2, 512], F32))
        YP = REL * C // 512
        staged, turned, back, rooted, root_in, kq, floored, powered, kq_in, summed, parts, parts_in = (
            sem(x) for x in ("staged", "turned", "back", "rooted", "root_in", "kq", "floored", "powered",
                             "kq_in", "summed", "parts", "parts_in"))
        stored = [sem("stored0"), sem("stored1")]
        with nc.Block() as block:
            @block.vector
            def _(v):
                v.memset(zero[:], 0.0)
                v.memset(st[:], 1.0)
        with nc.Block() as block:
            @block.scalar
            def _(act):
                for s in (staged, powered):
                    act.sem_inc(s, 2)
                act.sem_inc(parts_in, 2)

                def body(b, u, i, last):
                    act.wait_ge(summed, b + 1)
                    act.nop()
                    act.copy(st[:, u, 0:C], k.xa[:, ds(b * C, C)]).then_inc(staged, 1)
                    act.wait_ge(floored, b + 3)
                    act.nop()
                    act.activation(low[:, u, :], low[:, u, :], ACT.Exp).then_inc(powered, 1)
                    for q in range(YP):
                        half, at = divmod(q, YP // 2)
                        if at == 0 and not (isinstance(b, int) and b == 0):
                            act.wait_ge(stored[half], b * 16)
                        act.wait_ge(parts, b * YP + q + 1)
                        act.nop()
                        act.copy(y[:, half, at * 512:(at + 1) * 512], psY[:, q % 2, :]).then_inc(parts_in, 1)
                two_at_a_time(act, NB, body, peel=True)

            @block.tensor
            def _(pe):
                for s in (turned, rooted, kq, summed):
                    pe.sem_inc(s, 2)
                for kc in range(KC):
                    pe.matmul(psC[:, kc, 0:C + 2], zero[:, 0:P], zero[:], start=True, stop=False)

                def body(b, u, i, last):
                    pe.wait_ge(staged, b + 3)
                    pe.wait_ge(back, b + 2)
                    for kc in range(KC):
                        t = pe.transpose(psT[:, kc * P:(kc + 1) * P], st[:, u, kc * P:(kc + 1) * P], k.ident[:])
                    t.then_inc(turned, 1)
                    pe.wait_ge(back, b + 3)
                    pe.wait_ge(kq_in, b + 2)
                    for kc in range(KC):
                        t = pe.matmul(psQ[:, :], xt[:, u, kc * P:(kc + 1) * P], rkq[:, kc, C:],
                                      start=kc == 0, stop=kc == KC - 1)
                    t.then_inc(kq, 1)
                    pe.wait_ge(root_in, b + 2)
                    for kc in range(KC):
                        pe.matmul(psR[:, 0:C], xt[:, u, kc * P:(kc + 1) * P], rkq[:, kc, 0:C],
                                  start=kc == 0, stop=False)
                    for r in range(2):
                        t = pe.matmul(psR[:, 0:C], k.ones[0:1, :], bias[:, r, :], start=False, stop=r == 1)
                    t.then_inc(rooted, 1)
                    for q in range(YP):
                        pe.wait_ge(parts_in, b * YP + q + 1)
                        for kc in range(KC):
                            t = pe.matmul(psY[:, q % 2, :], xt[:, u, kc * P:(kc + 1) * P],
                                          wr[:, kc, q * 512:(q + 1) * 512], start=kc == 0, stop=kc == KC - 1)
                        t.then_inc(parts, 1)
                    pe.wait_ge(kq_in, b + 3)
                    for kc in range(KC):
                        t = pe.matmul(psC[:, kc, 0:C + 2], kk[:, u, kc * P:(kc + 1) * P], st[:, u, :],
                                      start=False, stop=last)
                    t.then_inc(summed, 1)
                two_at_a_time(pe, NB, body)

            @block.vector
            def _(v):
                for s in (back, root_in, floored, kq_in):
                    v.sem_inc(s, 2)

                def body(b, u, i, last):
                    v.wait_ge(turned, b + 3)
                    v.wait_ge(summed, b + 1)
                    v.tensor_copy(xt[:, u, :], psT[:, 0:C]).then_inc(back, 1)
                    v.wait_ge(kq, b + 3)
                    v.tensor_scalar(low[:, u, :], psQ[:, :], 0.0, None, ALU.min).then_inc(floored, 1)
                    v.wait_ge(rooted, b + 3)
                    v.tensor_tensor(k.xb[:, ds(b * C, C)], k.xb[:, ds(b * C, C)], psR[:, 0:C], ALU.add
                                    ).then_inc(root_in, 1)
                    v.wait_ge(powered, b + 3)
                    v.wait_ge(staged, b + 3)
                    if last:
                        v.scalar_tensor_tensor(kk[:, u, :], psQ[:, 0:C], 0.0, low[:, u, 0:C], ALU.max, ALU.add)
                        v.drain()
                        v.tensor_scalar(kk[:, u, :], kk[:, u, :], k.mask[:, 0:1], None, ALU.mult)
                    else:
                        v.scalar_tensor_tensor(kk[:, u, :], psQ[:, 0:C], 0.0, low[:, u, 0:C], ALU.max, ALU.add)
                    v.scalar_tensor_tensor(k.xa[:, ds(b * C, C)], psQ[:, C:2 * C], 0.0, low[:, u, C:], ALU.max,
                                           ALU.add).then_inc(kq_in, 1)
                two_at_a_time(v, NB, body)

            @block.sync
            def _(sp):
                rows = k.y_dram.rearrange("(n r) c -> n (r c)", r=REL)

                def body(b, u, i, last):
                    for half in range(2):
                        width = REL * C // 2
                        sp.wait_ge(parts_in, b * YP + YP // 2 * (half + 1) + 2)
                        sp.dma_start(rows[ds(b * P, P), half * width:(half + 1) * width], y[:, half, :]
                                     ).then_inc(stored[half], 16)
                two_at_a_time(sp, NB, body)
                for half in range(2):
                    sp.wait_ge(stored[half], 16 * NB)
        work.close()
        sb = lambda n, s, d=F32: c.enter_context(nc.sbuf_tensor("rr_" + n, s, d))
        wv = sb("wv", [P, KC, C])
        wp = sb("wp", [P, KC, C])
        cs = sb("cs", [P, KC, C + 2])
        ct = sb("ct", [P, KC, C])
        cbd = sb("cbd", [P, KC, C])
        kcol = sb("kcol", [P, KC, P])
        load_weights(nc, "rr_load2", [(wv[:], rows_of(S["L1_mix_Wv_t"])), (wp[:], rows_of(S["L1_mix_Wproj_t"]))])
        step, worked = sem("step"), sem("worked")
        with nc.Block() as block:
            @block.vector
            def _(v):
                v.memset(cbd[:], 0.0)
                v.tensor_copy(cs[:], psC[:, :, 0:C + 2])
                v.drain()
                for kc in range(KC):
                    o = v.tensor_scalar(kcol[:, kc, :], k.ones[:], cs[:, kc, C:C + 1], None, ALU.mult)
                o.then_inc(step, 1)
                v.wait_ge(worked, 1)
                v.tensor_copy(ct[:], psC[:, :, 0:C])
                v.tensor_copy(ksum[:], psT[:, 0:C]).then_inc(step, 1)
                v.wait_ge(worked, 2)
                for kc in range(KC):
                    for q in range(P // D):
                        a = kc * P + q * D
                        o = v.tensor_copy(cbd[q * D:(q + 1) * D, kc, a:a + D],
                                          psY[q * D:(q + 1) * D, kc, a:a + D])
                o.then_inc(step, 1)
                v.wait_ge(worked, 3)
                v.tensor_copy(ctxw[:], psC[:, :, 0:C])

            @block.tensor
            def _(pe):
                pe.wait_ge(step, 1)
                for m in range(KC):
                    for kc in range(KC):
                        pe.transpose(psC[:, m, kc * P:(kc + 1) * P], cs[:, kc, m * P:(m + 1) * P], k.ident[:])
                for kc in range(KC):
                    t = pe.matmul(psT[:, kc * P:(kc + 1) * P], kcol[:, kc, :], k.ident[:], start=True, stop=True)
                t.then_inc(worked, 1)
                pe.wait_ge(step, 2)
                for m in range(KC):
                    for kc in range(KC):
                        t = pe.matmul(psY[:, m, 0:C], wv[:, kc, m * P:(m + 1) * P], ct[:, kc, :],
                                      start=kc == 0, stop=kc == KC - 1)
                t.then_inc(worked, 1)
                pe.wait_ge(step, 3)
                for m in range(KC):
                    for kc in range(KC):
                        t = pe.matmul(psC[:, m, 0:C], cbd[:, kc, m * P:(m + 1) * P], wp[:, kc, :],
                                      start=kc == 0, stop=kc == KC - 1)
                t.then_inc(worked, 1)


def linear_attention_out(nc, z, k, ctxw, ksum):
    NB = z.NB
    with ExitStack() as c:
        sem = c.enter_context(semaphores(nc, "lo_"))
        sb = lambda n, s, d=F32: c.enter_context(nc.sbuf_tensor("lo_" + n, s, d))
        prod = sb("prod", [P, C])
        den = sb("den", [P, HEADS])
        st = sb("st", [P, 2, C])
        xt = sb("xt", [P, 2, C])
        psT = c.enter_context(nc.psum_tensor("lo_psT", [P, 2, 512], F32))
        psM = c.enter_context(nc.psum_tensor("lo_psM", [P, 2, 512], F32))
        scaled, turned, back, projected, added = (sem(x) for x in
            ("scaled", "turned", "back", "projected", "added"))
        with nc.Block() as block:
            @block.vector
            def _(v):
                v.sem_inc(scaled, 2)
                v.sem_inc(added, 2)

                def scale(b, u):
                    q = k.xa[:, ds(b * C, C)]
                    v.tensor_tensor(prod[:], q, ksum[:], ALU.mult)
                    v.drain()
                    v.tensor_reduce(den[:], prod[:].rearrange("p (h d) -> p h d", d=D), AX.X, ALU.add)
                    v.drain()
                    v.tensor_scalar(den[:], den[:], 1e-6, None, ALU.max)
                    v.drain()
                    v.reciprocal(den[:], den[:])
                    v.drain()
                    v.wait_ge(turned, b + 1)
                    v.tensor_tensor(st[:, u, :].rearrange("p (h d) -> p h d", d=D),
                                    q.rearrange("p (h d) -> p h d", d=D),
                                    den[:].unsqueeze(2).to_broadcast([P, HEADS, D]), ALU.mult
                                    ).then_inc(scaled, 1)

                def add(b, u):
                    v.wait_ge(projected, b + 3)
                    v.tensor_tensor(k.xb[:, ds(b * C, C)], k.xb[:, ds(b * C, C)], psM[:, u, 0:C], ALU.add
                                    ).then_inc(added, 1)

                def body(b, u, i, last):
                    if not last:
                        scale(b + 1, 1 - u)
                    if not (isinstance(b, int) and b == 0):
                        add(b - 1, 1 - u)
                scale(0, 0)
                two_at_a_time(v, NB, body, peel=True)
                add(NB - 1, (NB - 1) % 2)

            @block.tensor
            def _(pe):
                pe.sem_inc(turned, 2)
                pe.sem_inc(projected, 2)

                def prep(b, u):
                    pe.wait_ge(scaled, b + 3)
                    pe.wait_ge(back, b + 1)
                    for kc in range(KC):
                        t = pe.transpose(psT[:, u, kc * P:(kc + 1) * P], st[:, u, kc * P:(kc + 1) * P], k.ident[:])
                    t.then_inc(turned, 1)

                def body(b, u, i, last):
                    if not last:
                        prep(b + 1, 1 - u)
                    pe.wait_ge(back, b + 3)
                    pe.wait_ge(added, b + 1)
                    for kc in range(KC):
                        t = pe.matmul(psM[:, u, 0:C], xt[:, u, kc * P:(kc + 1) * P], ctxw[:, kc, :],
                                      start=kc == 0, stop=kc == KC - 1)
                    t.then_inc(projected, 1)
                prep(0, 0)
                two_at_a_time(pe, NB, body)

            @block.scalar
            def _(act):
                act.sem_inc(back, 2)

                def body(b, u, i, last):
                    act.wait_ge(turned, b + 3)
                    act.wait_ge(projected, b + 1)
                    act.nop()
                    act.copy(xt[:, u, :], psT[:, u, 0:C]).then_inc(back, 1)
                two_at_a_time(act, NB, body)


def experts(nc, z, k, name, norms, w1d, b1d, w2d, b2d, routed, br, gamma, beta, tokens, probs):
    NB = z.NB
    HID = w1d.shape[2]
    HC = HID // P
    with ExitStack() as c:
        sem = lambda n: c.enter_context(nc.semaphore(name + n))
        sb = lambda n, s, d=F32: c.enter_context(nc.sbuf_tensor(name + n, s, d))
        w1 = sb("w1", [P, NE, KC, HID])
        w2 = sb("w2", [P, NE, HC, C])
        b1 = sb("b1", [P, NE, HC])
        b2 = sb("b2", [NE, C])
        wr = sb("wr", [P, KC, NE])
        brow = sb("brow", [1, NE])
        cols = sb("cols", [P, 2, KC])
        lower = sb("lower", [P, NE, NE])
        st = sb("st", [P, 2, C])
        xt = sb("xt", [P, 2, C])
        lg = sb("lg", [P, NE])
        mx = sb("mx", [P, 2])
        ex = sb("ex", [P, NE])
        gt = sb("gt", [P, NE, NE])
        eq = sb("eq", [P, NE, NE])
        rank = sb("rank", [P, NE])
        gates = sb("gates", [P, 2, NE])
        gates_t = sb("gates_t", [NE, 2, P])
        hid = sb("hid", [P, 2, HC * P])
        psT = c.enter_context(nc.psum_tensor(name + "psT", [P, 512], F32))
        psG = c.enter_context(nc.psum_tensor(name + "psG", [P, 512], F32))
        psW = c.enter_context(nc.psum_tensor(name + "psW", [P, 512], F32))
        psB = c.enter_context(nc.psum_tensor(name + "psB", [P, 512], F32))
        psH = c.enter_context(nc.psum_tensor(name + "psH", [P, 2, 512], F32))
        psO = c.enter_context(nc.psum_tensor(name + "psO", [P, 2, 512], F32))
        loads = [(w1[:, e, :, :], rows_of(w1d[e])) for e in range(NE)]
        loads += [(w2[:, e, :, :], rows_of(w2d[e])) for e in range(NE)]
        loads += [(b1[:, e, :], b1d[e]) for e in range(NE)]
        loads += [(b2[:], b2d), (wr[:], rows_of(routed))]
        if br is not None:
            loads.append((brow[:], br.rearrange("(o n) -> o n", o=1)))
        if gamma is not None:
            loads += [(cols[:, 0, :], gamma), (cols[:, 1, :], beta)]
        load_weights(nc, name + "load", loads)
        zeroed = sem("zeroed")
        with nc.Block() as block:
            @block.gpsimd
            def _(p):
                p.memset(lower[:], 0.0).then_inc(zeroed, 1)
                p.wait_ge(zeroed, 1)
                p.affine_select(out=lower[:], in_=lower[:], compare_op=ALU.is_ge, fill=1.0, base=0,
                                pattern=[[-1, NE], [1, NE]], channel_multiplier=0)
            if br is None:
                @block.vector
                def _(v):
                    v.memset(brow[:], 0.0)
        staged, turned, back, logits, e_arg, e_done, gated, gates_turned, gates_back, biased, bias_in = (
            sem(x) for x in ("staged", "turned", "back", "logits", "e_arg", "e_done", "gated",
                             "gates_turned", "gates_back", "biased", "bias_in"))
        hidden, act_out, outs, taken = (sem(x) for x in ("hidden", "act_out", "outs", "taken"))
        with nc.Block() as block:
            @block.scalar
            def _(act):
                for s in (back, e_done, act_out):
                    act.sem_inc(s, 2)

                def prep(b, u):
                    act.wait_ge(turned, b + 3)
                    act.nop()
                    for kc in range(KC):
                        x = (xt[:, u, kc * P:(kc + 1) * P], psT[:, kc * P:(kc + 1) * P])
                        if gamma is None:
                            o = act.copy(*x)
                        else:
                            o = act.activation(*x, ACT.Identity, bias=cols[:, 1, kc:kc + 1], scale=cols[:, 0, kc:kc + 1])
                    o.then_inc(back, 1)

                def power(b):
                    act.wait_ge(e_arg, b + 3)
                    act.nop()
                    act.activation(ex[:], ex[:], ACT.Exp).then_inc(e_done, 1)

                def body(b, u, i, last):
                    for e in range(NE):
                        n = b * NE + e
                        act.wait_ge(hidden, n + 3)
                        act.wait_ge(outs, n + 1)
                        act.nop()
                        for q in range(HC):
                            o = act.activation(hid[:, e % 2, q * P:(q + 1) * P],
                                               psH[:, e % 2, q * P:(q + 1) * P], ACT.Gelu,
                                               bias=b1[:, e, q:q + 1])
                        o.then_inc(act_out, 1)
                        if e == 1 and not last:
                            prep(b + 1, 1 - u)
                        if e == 3 and not last:
                            power(b + 1)
                prep(0, 0)
                power(0)
                two_at_a_time(act, NB, body)

            @block.tensor
            def _(pe):
                for s in (turned, logits, gates_turned, biased, hidden, outs):
                    pe.sem_inc(s, 2)

                def prep(b, u):
                    pe.wait_ge(staged, b + 3)
                    pe.wait_ge(back, b + 2)
                    for kc in range(KC):
                        t = pe.transpose(psT[:, kc * P:(kc + 1) * P], st[:, u, kc * P:(kc + 1) * P], k.ident[:])
                    t.then_inc(turned, 1)

                def route(b, u):
                    pe.wait_ge(back, b + 3)
                    pe.wait_ge(gated, b + 2)
                    for kc in range(KC):
                        pe.matmul(psG[:, 0:NE], xt[:, u, kc * P:(kc + 1) * P], wr[:, kc, :],
                                  start=kc == 0, stop=False)
                    pe.matmul(psG[:, 0:NE], k.ones[0:1, :], brow[:], start=False, stop=True).then_inc(logits, 1)

                def bias(b, u):
                    pe.wait_ge(gated, b + 3)
                    pe.wait_ge(gates_back, b + 2)
                    pe.transpose(psW[0:NE, 0:P], gates[:, u, :], k.ident[:]).then_inc(gates_turned, 1)
                    pe.wait_ge(gates_back, b + 3)
                    pe.wait_ge(bias_in, b + 2)
                    pe.matmul(psB[:, 0:C], gates_t[:, u, :], b2[:], start=True, stop=True).then_inc(biased, 1)

                def hide(b, u, e):
                    pe.wait_ge(act_out, b * NE + e + 1)
                    for q in range(HC):
                        for kc in range(KC):
                            t = pe.matmul(psH[:, e % 2, q * P:(q + 1) * P], w1[:, e, kc, q * P:(q + 1) * P],
                                          xt[:, u, kc * P:(kc + 1) * P], start=kc == 0, stop=kc == KC - 1)
                    t.then_inc(hidden, 1)

                def body(b, u, i, last):
                    hide(b, u, 0)
                    for e in range(NE):
                        if e + 1 < NE:
                            hide(b, u, e + 1)
                        if not last:
                            if e == 1:
                                prep(b + 1, 1 - u)
                            if e == 3:
                                route(b + 1, 1 - u)
                            if e == 6:
                                bias(b + 1, 1 - u)
                        n = b * NE + e
                        pe.wait_ge(act_out, n + 3)
                        pe.wait_ge(taken, n + 1)
                        for q in range(HC):
                            t = pe.matmul(psO[:, e % 2, 0:C], hid[:, e % 2, q * P:(q + 1) * P],
                                          w2[:, e, q, :], start=q == 0, stop=q == HC - 1)
                        t.then_inc(outs, 1)
                prep(0, 0)
                route(0, 0)
                bias(0, 0)
                two_at_a_time(pe, NB, body)

            @block.vector
            def _(v):
                for s in (staged, e_arg, gated, gates_back, bias_in, taken):
                    v.sem_inc(s, 2)

                def prep(b, u):
                    v.wait_ge(turned, b + 1)
                    o = v.tensor_scalar(st[:, u, :], k.xb[:, ds(b * C, C)], norms[0][:, ds(b, 1)],
                                        norms[1][:, ds(b, 1)], ALU.subtract, ALU.mult)
                    if len(norms) == 4:
                        v.drain()
                        o = v.tensor_scalar(st[:, u, :], st[:, u, :], norms[2][:, ds(b, 1)],
                                            norms[3][:, ds(b, 1)], ALU.subtract, ALU.mult)
                    o.then_inc(staged, 1)
                    if tokens:
                        v.drain()
                        v.tensor_tensor(k.xb[:, ds(b * C, C)], k.xb[:, ds(b * C, C)], st[:, u, :], ALU.add)

                def choose(b, u):
                    v.wait_ge(logits, b + 3)
                    v.tensor_copy(lg[:], psG[:, 0:NE])
                    v.tensor_reduce(mx[:, 0:1], psG[:, 0:NE], AX.X, ALU.max)
                    v.drain()
                    v.tensor_scalar(ex[:], lg[:], mx[:, 0:1], None, ALU.subtract).then_inc(e_arg, 1)
                    if probs:
                        v.wait_ge(e_done, b + 3)
                        v.tensor_reduce(mx[:, 1:2], ex[:], AX.X, ALU.add)
                        v.drain()
                        v.reciprocal(mx[:, 1:2], mx[:, 1:2])
                        v.drain()
                        v.tensor_scalar(ex[:], ex[:], mx[:, 1:2], None, ALU.mult)
                        v.drain()
                        v.tensor_copy(lg[:], ex[:])
                        v.drain()
                    other = lg[:].unsqueeze(1).to_broadcast([P, NE, NE])
                    own = lg[:].unsqueeze(2).to_broadcast([P, NE, NE])
                    v.tensor_tensor(gt[:], other, own, ALU.is_gt)
                    v.tensor_tensor(eq[:], other, own, ALU.is_equal)
                    v.drain()
                    v.tensor_tensor(eq[:], eq[:], lower[:], ALU.mult)
                    v.drain()
                    v.tensor_tensor(gt[:], gt[:], eq[:], ALU.add)
                    v.drain()
                    v.tensor_reduce(rank[:], gt[:], AX.X, ALU.add)
                    v.drain()
                    v.tensor_scalar(rank[:], rank[:], 2.0, None, ALU.is_lt)
                    v.drain()
                    v.wait_ge(e_done, b + 3)
                    v.tensor_tensor(ex[:], ex[:], rank[:], ALU.mult)
                    v.drain()
                    v.tensor_reduce(mx[:, 1:2], ex[:], AX.X, ALU.add)
                    v.drain()
                    v.tensor_scalar(mx[:, 1:2], mx[:, 1:2], 1e-12, None, ALU.max)
                    v.drain()
                    v.reciprocal(mx[:, 1:2], mx[:, 1:2])
                    v.drain()
                    v.tensor_scalar(gates[:, u, :], ex[:], mx[:, 1:2], None, ALU.mult).then_inc(gated, 1)

                def biases(b, u):
                    v.wait_ge(gates_turned, b + 3)
                    v.tensor_copy(gates_t[:, u, :], psW[0:NE, 0:P]).then_inc(gates_back, 1)
                    v.drain()
                    v.wait_ge(biased, b + 3)
                    v.tensor_tensor(k.xb[:, ds(b * C, C)], k.xb[:, ds(b * C, C)], psB[:, 0:C], ALU.add
                                    ).then_inc(bias_in, 1)

                def body(b, u, i, last):
                    for e in range(NE):
                        if not last:
                            if e == 0:
                                prep(b + 1, 1 - u)
                            if e == 3:
                                choose(b + 1, 1 - u)
                            if e == 6:
                                biases(b + 1, 1 - u)
                        v.drain()
                        v.wait_ge(outs, b * NE + e + 3)
                        x = k.xb[:, ds(b * C, C)]
                        v.scalar_tensor_tensor(x, psO[:, e % 2, 0:C], gates[:, u, e:e + 1], x, ALU.mult,
                                               ALU.add).then_inc(taken, 1)
                prep(0, 0)
                choose(0, 0)
                biases(0, 0)
                two_at_a_time(v, NB, body)


class Kept:
    pass


def graph_network(nc, S, out):
    n, _ = out.shape
    z = Sizes(n, S["n_edges"])
    NB = z.NB
    k = Kept()
    with ExitStack() as c:
        sb = lambda n, s, d=F32: c.enter_context(nc.sbuf_tensor(n, s, d))
        k.xb = sb("xb", [P, NB * C])
        k.ident = sb("ident", [P, P])
        k.iota = sb("iota", [P, P])
        k.ones = sb("ones", [P, P])
        k.mask = sb("mask", [P, 1])
        k.a2 = sb("a2", [P, NB * HEADS])
        k.icnt = sb("icnt", [P, NB * REL])
        k.dstf = sb("dstf", [P, z.COLS])
        k.etf = sb("etf", [P, z.COLS], BF16)
        k.start = sb("start", [P, z.COLS], BF16)
        k.last = sb("last", [P, z.COLS], BF16)
        k.last_pair = sb("last_pair", [1, z.NCH * P], I32)
        k.pair_block = sb("pair_block", [1, z.NCH * P], I32)
        k.pair_group = sb("pair_group", [1, z.NCH * P], I32)
        k.pair_node = sb("pair_node", [P, z.NCH * P])
        k.src_rel = nc.dram_tensor("src_rel", (P, z.COLS), I32).ap()
        k.table_dram = nc.dram_tensor("table_dram", (2, z.NCH * P, 1), I32).ap()
        mean = sb("mean", [P, NB])
        rstd = sb("rstd", [P, NB])
        mean2 = sb("mean2", [P, NB])
        rstd2 = sb("rstd2", [P, NB])
        k.first_dram = nc.dram_tensor("first_dram", (NB + 1, 1), I32).ap()
        k.x_dram = nc.dram_tensor("x_dram", (NB * P, C), F32).ap()
        k.h_dram = nc.dram_tensor("h_dram", (NB * P, HROW), F32).ap()
        k.y_dram = nc.dram_tensor("y_dram", (NB * P * REL, C), F32).ap()
        setup(nc, z, S, k)

        with nc.sbuf_tensor("xa0", [P, NB * C], F32) as xa:
            k.xa = xa
            normalise_stats(nc, "n0", k.xb, mean, rstd, 1e-5, NB)
            normalise_rows(nc, k.xa, k.xb, mean, rstd, NB)
            with nc.sbuf_tensor("wqc", [P, KC, C], F32) as wqc:
                with nc.sbuf_tensor("kt", [P, KC * NB * P], F32) as kt:
                    attention_table(nc, z, k, S, kt)
                    keys_to_context(nc, z, k, S, kt, wqc)
                normalise_stats(nc, "n1", k.xa, mean, rstd, 1e-5, NB)
                mix_out(nc, z, k, S, wqc, mean, rstd)
        attention(nc, z, k, S)
        with nc.sbuf_tensor("xa1", [P, NB * C], F32) as xa:
            k.xa = xa
            normalise_stats(nc, "n2", k.xb, mean, rstd, 1e-5, NB)
            normalise_rows(nc, k.xa, k.xb, mean, rstd, NB)
            normalise_stats(nc, "n3", k.xa, mean2, rstd2, 1e-5, NB)
        experts(nc, z, k, "f0_", (mean, rstd, mean2, rstd2), S["L0_ffn_W1"], S["L0_ffn_b1"], S["L0_ffn_W2"],
                    S["L0_ffn_b2"], S["L0_ffn_Wr"], S["L0_ffn_br"], S["L0_ffn_gamma"], S["L0_ffn_beta"],
                    False, False)
        with nc.sbuf_tensor("xa2", [P, NB * C], F32) as xa:
            k.xa = xa
            normalise_stats(nc, "n4", k.xb, mean, rstd, 1e-5, NB)
            normalise_rows(nc, k.xa, k.xb, mean, rstd, NB)
            with nc.sbuf_tensor("ctxw", [P, KC, C], F32) as ctxw, nc.sbuf_tensor("ksum", [P, C], F32) as ksum:
                relation_rows(nc, z, k, S, ctxw, ksum)
                linear_attention_out(nc, z, k, ctxw, ksum)
        relations(nc, z, k, S)
        normalise_stats(nc, "n5", k.xb, mean, rstd, 1e-5, NB)
        experts(nc, z, k, "f1_", (mean, rstd), S["L1_ffn_w1"], S["L1_ffn_b1"], S["L1_ffn_w2"],
                S["L1_ffn_b2"], S["L1_ffn_router_w_t"], None, None, None, True, True)
        with nc.semaphore("stored") as stored, nc.Block() as block:
            @block.sync
            def _(sp):
                full = (NB - 1) * P
                if full:
                    sp.dma_start(out[0:full, :].rearrange("(b p) f -> p b f", p=P),
                                 k.xb[:, 0:full // P * C].rearrange("p (b f) -> p b f", f=C)).then_inc(stored, 16)
                sp.dma_start(out[full:n, :], k.xb[0:z.TAIL, full // P * C:NB * C]).then_inc(stored, 16)
                sp.wait_ge(stored, 16 * (2 if full else 1))


COLUMNS = ("L0_gnn_attn_l", "L0_gnn_attn_r", "L0_mix_ln_g", "L0_mix_ln_b", "L0_mix_bg2", "L0_ffn_gamma",
           "L0_ffn_beta")


def _layouts(x, src, dst, edge_type_16, w):
    import numpy as np
    z = Sizes(x.shape[0], src.shape[0])
    E = src.shape[0]
    far = 1 << 20

    def table(a, fill):
        full = np.full(z.NGT * GE, fill, np.int32)
        full[:E] = a
        return full.reshape(z.NGT, P, G)
    lay = lambda a: np.ascontiguousarray(a.transpose(1, 0, 2).reshape(P, z.COLS))
    d = table(dst, far)
    before = np.full_like(d, -1)
    before[:, 1:] = d[:, :-1]
    behind = np.full_like(d, -1)
    behind[:, :-1] = d[:, 1:]
    xp = np.zeros((z.NB * P, C), np.float32)
    xp[:x.shape[0]] = x
    out = {"x": xp, "src": lay(table(src, 0)), "dst": lay(d), "dst_prev": lay(before),
           "dst_next": lay(behind), "etype": lay(table(edge_type_16, 0)),
           "bounds": np.ascontiguousarray(dst[GE - 1::GE][:z.NG - 1])}
    for name, a in w.items():
        a = np.asarray(a)
        if name == "L0_gnn_W":
            out["L0_gnn_W_t"] = a.T
        if name == "L0_mix_Wqkv":
            out["L0_mix_Wq_t"] = a[:, 0:C].T
        if name in COLUMNS:
            a = a.reshape(KC, P).T
        if name == "L1_mix_Wkv":
            out["L1_mix_Wk_t"], out["L1_mix_Wv_t"] = a[0:C].T, a[C:2 * C].T
        elif name in ("L1_mix_Wq", "L1_mix_Wproj", "L1_ffn_router_w"):
            out[name + "_t"] = a.T
        elif name in ("L0_ffn_b1", "L1_ffn_b1"):
            out[name] = a.reshape(NE, -1, P).transpose(0, 2, 1)
        else:
            out[name] = a
    return {name: np.ascontiguousarray(a) for name, a in out.items()}


def kernel(x, src, dst, edge_type_16, **weights):
    import numpy as _np
    import concourse.bacc as _bacc
    from concourse import mybir as _mybir
    from concourse.bass_utils import run_bass_kernel_spmd as _run

    x, src, dst, edge_type_16 = (_np.asarray(a) for a in (x, src, dst, edge_type_16))
    arrays = _layouts(x, src, dst, edge_type_16, weights)
    nc = _bacc.Bacc("TRN2", target_bir_lowering=False, num_devices=1)
    S = {"n_edges": src.shape[0]}
    for name, a in arrays.items():
        S[name] = nc.dram_tensor(name, a.shape, _mybir.dt.from_np(a.dtype), kind="ExternalInput").ap()
    out = nc.dram_tensor("out", x.shape, F32, kind="ExternalOutput").ap()
    graph_network(nc, S, out)
    r = _run(nc, [arrays], core_ids=[0])
    return r.results[0]["out"]
```
